# Optimizing a Trainium2 kernel written in Bass

```python
import numpy as np
import jax
import jax.numpy as jnp

def _softmax(x, axis=-1):
    return jax.nn.softmax(x, axis=axis)

def _gelu(x):
    return jax.nn.gelu(x, approximate=True)

def _silu(x):
    return jax.nn.silu(x)

def _sigmoid(x):
    return jax.nn.sigmoid(x)

def _layernorm(x, axis=-1, eps=1e-05):
    m = jnp.mean(x, axis=axis, keepdims=True)
    v = jnp.var(x, axis=axis, keepdims=True)
    return (x - m) / jnp.sqrt(v + eps)

def _scatter_add(tgt, idx, src, axis=0):
    return tgt.at[idx].add(src)

def _segment_sum(src, seg, n):
    return jax.ops.segment_sum(src, seg, n)
kernel_name = 'mk_gnn_preln_d4_gnn_r32_0f8f19'

def setup_inputs(seed: int=0):
    np.random.seed(seed)
    _w = jnp.asarray

    def _rec_inputs():
        import jax
        import jax.numpy as jnp
        _gk = jax.random.key(seed)
        x = -0.000202 + 1 * jax.random.normal(jax.random.fold_in(_gk, 1), (50000, 128), jnp.float32)
        src = jax.random.randint(jax.random.fold_in(_gk, 2), (25000,), 0, 50000, jnp.int32)
        dst = jax.random.randint(jax.random.fold_in(_gk, 3), (25000,), 0, 50000, jnp.int32)
        _o = jnp.argsort(dst, stable=True)
        src = src[_o]
        dst = dst[_o]
        edge_type_8 = jax.random.randint(jax.random.fold_in(_gk, 13), (25000,), 0, 8, jnp.int32)
        return (x, src, dst, edge_type_8)
    x, src, dst, edge_type_8 = _rec_inputs()

    def _L0_gnn_setup():
        import jax, jax.numpy as jnp
        import numpy as np
        IN_DIM = 128
        OUT_DIM = 128
        NUM_RELS = 8
        N_NODES = 50000
        N_EDGES = 15625
        key = jax.random.key(seed)
        k_x, k_ei_s, k_ei_d, k_et, k_w, k_sw = jax.random.split(key, 6)
        x = jax.random.normal(k_x, (N_NODES, IN_DIM), dtype=jnp.float32)
        src = jax.random.randint(k_ei_s, (N_EDGES,), 0, N_NODES)
        dst = jax.random.randint(k_ei_d, (N_EDGES,), 0, N_NODES)
        edge_index = jnp.stack([src, dst], axis=0).astype(jnp.int64)
        edge_type = jax.random.randint(k_et, (N_EDGES,), 0, NUM_RELS).astype(jnp.int64)
        bw = float(np.sqrt(6.0 / (IN_DIM + OUT_DIM)))
        weight = jax.random.uniform(k_w, (NUM_RELS, IN_DIM, OUT_DIM), dtype=jnp.float32, minval=-bw, maxval=bw)
        self_loop_weight = jax.random.uniform(k_sw, (IN_DIM, OUT_DIM), dtype=jnp.float32, minval=-bw, maxval=bw)
        bias = jnp.zeros((OUT_DIM,), dtype=jnp.float32)
        return {'x': x, 'weight': weight, 'self_loop_weight': self_loop_weight, 'bias': bias, 'edge_index': edge_index, 'edge_type': edge_type, 'num_entities': N_NODES}
    _L0_gnn_all = _L0_gnn_setup()
    _L0_gnn_in = {k: v for k, v in _L0_gnn_all.items() if k in ('weight', 'self_loop_weight', 'bias')}
    del _L0_gnn_all

    def _L1_gnn_setup():
        import jax, jax.numpy as jnp
        import numpy as np
        HEAD_NUM = 4
        EMB = 128
        N_NODES = 50000
        N_EDGES = 18750
        key = jax.random.key(seed)
        k1, k2, k3, k4, k5, k6 = jax.random.split(key, 6)
        embeds = jax.random.normal(k1, (N_NODES, EMB), dtype=jnp.float32)
        qW = jax.random.normal(k2, (EMB, EMB), dtype=jnp.float32) * (1.0 / np.sqrt(EMB))
        kW = jax.random.normal(k3, (EMB, EMB), dtype=jnp.float32) * (1.0 / np.sqrt(EMB))
        vW = jax.random.normal(k4, (EMB, EMB), dtype=jnp.float32) * (1.0 / np.sqrt(EMB))
        rows = jax.random.randint(k5, (N_EDGES,), 0, N_NODES, dtype=jnp.int32)
        cols = jax.random.randint(k6, (N_EDGES,), 0, N_NODES, dtype=jnp.int32)
        return {'embeds': embeds, 'qW': qW, 'kW': kW, 'vW': vW, 'rows': rows, 'cols': cols, 'n_nodes': N_NODES}
    _L1_gnn_all = _L1_gnn_setup()
    _L1_gnn_in = {k: v for k, v in _L1_gnn_all.items() if k in ('qW', 'kW', 'vW')}
    del _L1_gnn_all

    def _L2_gnn_setup():
        import jax, jax.numpy as jnp
        import numpy as np
        N, E, D, H = (50000, 50000, 128, 128)
        LN_EPS = 1e-05

        def _layernorm(h, g, b):
            mu = jnp.mean(h, axis=-1, keepdims=True)
            var = jnp.mean((h - mu) ** 2, axis=-1, keepdims=True)
            return (h - mu) * jax.lax.rsqrt(var + LN_EPS) * g + b

        def _sage_mean(x, src, dst, W_self, W_neigh, bias, num_nodes):
            msg = x[src]
            s = jax.ops.segment_sum(msg, dst, num_segments=num_nodes)
            cnt = jax.ops.segment_sum(jnp.ones((src.shape[0],), x.dtype), dst, num_segments=num_nodes)
            mean = s / jnp.maximum(cnt, 1.0)[:, None]
            return x @ W_self.T + mean @ W_neigh.T + bias
        key = jax.random.key(seed)
        ks = jax.random.split(key, 8)
        sc = 0.05
        return {'x': jax.random.normal(ks[0], (N, D), jnp.float32), 'src': jax.random.randint(ks[1], (E,), 0, N, jnp.int32), 'dst': jax.random.randint(ks[2], (E,), 0, N, jnp.int32), 'W_self0': jax.random.normal(ks[3], (H, D), jnp.float32) * sc, 'W_neigh0': jax.random.normal(ks[4], (H, D), jnp.float32) * sc, 'b0': jnp.zeros((H,), jnp.float32), 'W_self1': jax.random.normal(ks[5], (H, H), jnp.float32) * sc, 'W_neigh1': jax.random.normal(ks[6], (H, H), jnp.float32) * sc, 'b1': jnp.zeros((H,), jnp.float32), 'ln_g': jnp.ones((H,), jnp.float32), 'ln_b': jnp.zeros((H,), jnp.float32)}
    _L2_gnn_all = _L2_gnn_setup()
    _L2_gnn_in = {k: v for k, v in _L2_gnn_all.items() if k in ('W_self0', 'W_neigh0', 'b0', 'W_self1', 'W_neigh1', 'b1', 'ln_g', 'ln_b')}
    del _L2_gnn_all

    def _L3_gnn_setup():
        import jax, jax.numpy as jnp
        import numpy as np
        N_NODES = 3125
        N_EDGES = 50000
        DIM_IN = 128
        DIM_OUT = 128
        key = jax.random.key(seed)
        k_x, k_e, k_w = jax.random.split(key, 3)
        x = jax.random.normal(k_x, (N_NODES, DIM_IN), dtype=jnp.float32)
        edge_index = jax.random.randint(k_e, (2, N_EDGES), 0, N_NODES, dtype=jnp.int64)
        limit = np.sqrt(6.0 / (DIM_IN + DIM_OUT)).astype(np.float32)
        W = jax.random.uniform(k_w, (DIM_IN, DIM_OUT), dtype=jnp.float32, minval=-limit, maxval=limit)
        return {'x': x, 'edge_index': edge_index, 'W': W}
    _L3_gnn_all = _L3_gnn_setup()
    _L3_gnn_in = {k: v for k, v in _L3_gnn_all.items() if k in ('W',)}
    del _L3_gnn_all
    return {'x': x, 'src': src, 'dst': dst, 'edge_type_8': edge_type_8, 'L0_gnn_weight': _L0_gnn_in['weight'], 'L0_gnn_self_loop_weight': _L0_gnn_in['self_loop_weight'], 'L0_gnn_bias': _L0_gnn_in['bias'], 'L1_gnn_qW': _L1_gnn_in['qW'], 'L1_gnn_kW': _L1_gnn_in['kW'], 'L1_gnn_vW': _L1_gnn_in['vW'], 'L2_gnn_W_self0': _L2_gnn_in['W_self0'], 'L2_gnn_W_neigh0': _L2_gnn_in['W_neigh0'], 'L2_gnn_b0': _L2_gnn_in['b0'], 'L2_gnn_W_self1': _L2_gnn_in['W_self1'], 'L2_gnn_W_neigh1': _L2_gnn_in['W_neigh1'], 'L2_gnn_b1': _L2_gnn_in['b1'], 'L2_gnn_ln_g': _L2_gnn_in['ln_g'], 'L2_gnn_ln_b': _L2_gnn_in['ln_b'], 'L3_gnn_W': _L3_gnn_in['W']}

def reference(x, src, dst, edge_type_8, L0_gnn_weight, L0_gnn_self_loop_weight, L0_gnn_bias, L1_gnn_qW, L1_gnn_kW, L1_gnn_vW, L2_gnn_W_self0, L2_gnn_W_neigh0, L2_gnn_b0, L2_gnn_W_self1, L2_gnn_W_neigh1, L2_gnn_b1, L2_gnn_ln_g, L2_gnn_ln_b, L3_gnn_W):
    import jax
    import jax.numpy as jnp

    def _L0_gnn_ref(x, weight, self_loop_weight, bias, edge_index, edge_type, num_entities):
        import jax, jax.numpy as jnp
        import numpy as np
        IN_DIM = 128
        OUT_DIM = 128
        NUM_RELS = 8
        N_NODES = 50000
        N_EDGES = 15625
        hr = jnp.einsum('nd,rdo->rno', x, weight)
        src, dst = (edge_index[0], edge_index[1])
        msg = hr[edge_type, src]
        agg = jax.ops.segment_sum(msg, dst, num_segments=num_entities)
        out = agg + x @ self_loop_weight + bias
        return jax.nn.relu(out)

    def _L1_gnn_ref(embeds, qW, kW, vW, rows, cols, n_nodes):
        import jax, jax.numpy as jnp
        import numpy as np
        HEAD_NUM = 4
        EMB = 128
        N_NODES = 50000
        N_EDGES = 18750
        H = HEAD_NUM
        D = embeds.shape[1]
        Dh = D // H
        rowEmb = embeds[rows]
        colEmb = embeds[cols]
        q = (rowEmb @ qW).reshape(-1, H, Dh)
        k = (colEmb @ kW).reshape(-1, H, Dh)
        v = (colEmb @ vW).reshape(-1, H, Dh)
        att = jnp.einsum('ehd,ehd->eh', q, k)
        att = jnp.clip(att, -10.0, 10.0)
        expAtt = jnp.exp(att)
        attNorm = jax.ops.segment_sum(expAtt, rows, num_segments=n_nodes)
        att = expAtt / (attNorm[rows] + 1e-08)
        res = (att[..., None] * v).reshape(-1, D)
        out = jax.ops.segment_sum(res, rows, num_segments=n_nodes)
        return out

    def _L2_gnn_ref(x, src, dst, W_self0, W_neigh0, b0, W_self1, W_neigh1, b1, ln_g, ln_b):
        import jax, jax.numpy as jnp
        import numpy as np
        N, E, D, H = (50000, 50000, 128, 128)
        LN_EPS = 1e-05

        def _layernorm(h, g, b):
            mu = jnp.mean(h, axis=-1, keepdims=True)
            var = jnp.mean((h - mu) ** 2, axis=-1, keepdims=True)
            return (h - mu) * jax.lax.rsqrt(var + LN_EPS) * g + b

        def _sage_mean(x, src, dst, W_self, W_neigh, bias, num_nodes):
            msg = x[src]
            s = jax.ops.segment_sum(msg, dst, num_segments=num_nodes)
            cnt = jax.ops.segment_sum(jnp.ones((src.shape[0],), x.dtype), dst, num_segments=num_nodes)
            mean = s / jnp.maximum(cnt, 1.0)[:, None]
            return x @ W_self.T + mean @ W_neigh.T + bias
        n = x.shape[0]
        h = _sage_mean(x, src, dst, W_self0, W_neigh0, b0, n)
        h = jax.nn.relu(_layernorm(h, ln_g, ln_b))
        h = _sage_mean(h, src, dst, W_self1, W_neigh1, b1, n)
        h = _layernorm(h, ln_g, ln_b)
        return h

    def _L3_gnn_ref(x, edge_index, W):
        import jax, jax.numpy as jnp
        import numpy as np
        N_NODES = 3125
        N_EDGES = 50000
        DIM_IN = 128
        DIM_OUT = 128
        N = x.shape[0]
        x_proj = x @ W
        loop = jnp.arange(N, dtype=edge_index.dtype)
        src = jnp.concatenate([edge_index[0], loop])
        dst = jnp.concatenate([edge_index[1], loop])
        deg = jax.ops.segment_sum(jnp.ones(src.shape, dtype=x.dtype), dst, num_segments=N)
        dis = jnp.where(deg > 0, jax.lax.rsqrt(deg), 0.0)
        norm = dis[src] * dis[dst]
        msgs = x_proj[src] * norm[:, None]
        return jax.ops.segment_sum(msgs, dst, num_segments=N)
    edge_index = jnp.stack([src, dst])
    h = jnp.maximum(_layernorm(x, axis=-1), 0.0)
    x = x + _L0_gnn_ref(h, L0_gnn_weight, L0_gnn_self_loop_weight, L0_gnn_bias, edge_index, edge_type_8, 50000)
    h = jnp.maximum(_layernorm(x, axis=-1), 0.0)
    x = x + _L1_gnn_ref(h, L1_gnn_qW, L1_gnn_kW, L1_gnn_vW, src, dst, 50000)
    h = jnp.maximum(_layernorm(x, axis=-1), 0.0)
    x = x + _L2_gnn_ref(h, src, dst, L2_gnn_W_self0, L2_gnn_W_neigh0, L2_gnn_b0, L2_gnn_W_self1, L2_gnn_W_neigh1, L2_gnn_b1, L2_gnn_ln_g, L2_gnn_ln_b)
    h = jnp.maximum(_layernorm(x, axis=-1), 0.0)
    x = x + _L3_gnn_ref(h, edge_index, L3_gnn_W)
    return x

_drawn_inputs = setup_inputs


def setup_inputs(seed=0):
    import zlib

    import numpy as np

    out = dict(_drawn_inputs(seed))
    spreads = {'L0_gnn_bias': (0.0, 0.1),
     'L2_gnn_b0': (0.0, 0.1),
     'L2_gnn_b1': (0.0, 0.1),
     'L2_gnn_ln_g': (1.0, 0.2),
     'L2_gnn_ln_b': (0.0, 0.1)}
    factors = {}
    for name, (base, spread) in spreads.items():
        noise = np.random.default_rng([zlib.crc32(name.encode()), seed]).standard_normal(out[name].shape)
        drawn = base * np.exp(spread * noise) if base else spread * noise
        out[name] = jnp.asarray(drawn.astype(out[name].dtype))
    for name, factor in factors.items():
        out[name] = (out[name] * factor).astype(out[name].dtype)
    return out
```

```python
import concourse.bass as bass
from concourse import mybir
from contextlib import ExitStack


class Step:

    def __init__(self, i, times, offset):
        self.i, self.times, self.offset = i, times, offset

    def scaled(self, m, plus=0):
        if self.i is None:
            return self.offset * m + plus
        return self.i * (self.times * m) + (self.offset * m + plus)

    def mod(self, m):
        return self.offset % m

    def div(self, m):
        if self.i is None:
            return Step(None, 1, self.offset // m)
        return Step(self.i, self.times // m, self.offset // m)


class Signal:

    def __init__(self, sem, per, credit=0):
        self.sem, self.per, self.credit = sem, per, credit

    def after(self, step, first=0, n=None):
        n = self.per if n is None else n
        return step.scaled(self.per, self.credit + first * self.per + n)

    def before(self, step, back, first=0):
        return step.scaled(self.per, self.credit + (first - back + 1) * self.per)


def wait_landed(eng, signal, value):
    if not isinstance(value, int) or value > 0:
        eng.wait_ge(signal.sem, value)


class Chain:

    def __init__(self, eng, sem):
        self.eng, self.sem, self.base, self.per = eng, sem, 0, 0

    def open(self, per):
        self.per = per

    def close(self, steps):
        self.base += self.per * steps

    def begin(self, step):
        self.step, self.k = step, 0

    def mark(self, ins):
        self.k += 1
        ins.then_inc(self.sem, 1)

    def wait(self):
        self.eng.wait_ge(self.sem, self.step.scaled(self.per, self.base + self.k))

    def end(self):
        assert self.k == self.per, (self.k, self.per)


def run_steps(eng, stages, total, unroll, ahead=0, behind=0):
    deepest = max(lag for _, lag in stages)
    low = -(-(deepest + behind) // unroll) * unroll
    high = (total - 1 - ahead) // unroll * unroll

    def turn(it, i=None):
        for stage, lag in stages:
            if i is not None:
                stage(Step(i, unroll, it - lag))
            elif 0 <= it - lag < total:
                stage(Step(None, 1, it - lag))

    for it in range(low):
        turn(it)
    with eng.Fori(low // unroll, high // unroll) as i:
        for u in range(unroll):
            turn(u, i)
    for it in range(high, total + deepest):
        turn(it)


def gnn_stack_kernel(nc, x, src, dst, edge_type, w_rel, w_loop, b_loop, w_q, w_k, w_v,
                     w_self0, w_neigh0, b0, w_self1, w_neigh1, b1, ln_g, ln_b, w_gcn, out):
    fp32 = mybir.dt.float32
    i32 = mybir.dt.int32
    ALU = mybir.AluOpType
    ACT = mybir.ActivationFunctionType
    AX = mybir.AxisListType

    P = 128
    N, D = x.shape
    E = src.shape[0]
    NREL = w_rel.shape[0]
    HEADS = 4
    DH = D // HEADS
    EPS = 1e-5

    COL_A, COL_C, COL_DIS = D, D + 1, D + 2
    COL_CNT = D
    W = D + HEADS

    TPR = 4
    TILES = -(-E // P)
    ROUNDS = TILES // TPR
    assert TILES == ROUNDS * TPR and ROUNDS % 2 == 1
    FULL = E // P
    REST = E - FULL * P
    SPARE = 2 * P
    PAD = N + SPARE

    K = 4
    GROUP = K * P
    GROUPS = -(-N // GROUP)
    SLOTS = 6

    REL, ATT, SAGE0, SAGE1, GCN = range(5)
    SEG_PHASES = [REL, SAGE0, SAGE1, GCN]

    rows1 = nc.dram_tensor("rows1", (N, W), fp32, kind="Internal").ap()
    rows2 = nc.dram_tensor("rows2", (N, W), fp32, kind="Internal").ap()
    rowsg = nc.dram_tensor("rowsg", (N, W), fp32, kind="Internal").ap()
    rows3 = nc.dram_tensor("rows3", (N, W), fp32, kind="Internal").ap()
    sums = nc.dram_tensor("sums", (PAD + 1, W), fp32, kind="Internal").ap()
    attsums = nc.dram_tensor("attsums", (PAD + 1, W), fp32, kind="Internal").ap()

    ctx = ExitStack()
    with ctx:
        def sb(name, shape, dt=fp32):
            return ctx.enter_context(nc.sbuf_tensor(name, shape, dt))

        def sem(name):
            return ctx.enter_context(nc.semaphore(name))

        ident = sb("ident", [P, P])
        ones_row = sb("ones_row", [1, P])
        zeros = sb("zeros", [P, 5148])
        eps_col = sb("eps_col", [P, 1])
        ones_col = sb("ones_col", [P, 1])
        w_rel_sb = sb("w_rel_sb", [P, NREL, D])
        w_in = sb("w_in", [P, 4, D])
        w_t = sb("w_t", [P, 4, D])
        w_loop_sb = sb("w_loop_sb", [P, D])
        w_q_sb = sb("w_q_sb", [P, D])
        w_kv_sb = sb("w_kv_sb", [P, 2, D])
        w_gcn_sb = sb("w_gcn_sb", [P, D])
        bias_rows = sb("bias_rows", [1, 3, D])
        ln_g_bc = sb("ln_g_bc", [P, D])
        ln_b_bc = sb("ln_b_bc", [P, D])
        key_rows = sb("key_rows", [P, 4, 2, P], i32)
        key_rows_f = sb("key_rows_f", [P, 4, 2, P])
        src_f = sb("src_f", [P, TILES])
        dst_f = sb("dst_f", [P, TILES])
        next_f = sb("next_f", [P, TILES])
        type_f = sb("type_f", [P, TILES])
        carry_key = sb("carry_key", [P, TILES])
        src_i = sb("src_i", [P, TILES], i32)
        dst_i = sb("dst_i", [P, TILES], i32)
        last_i = sb("last_i", [P, TILES], i32)
        spare_f = sb("spare_f", [P, TPR])
        earlier = sb("earlier", [P, 2, 2 * P])
        gidx = sb("gidx", [P, 2, TPR], i32)
        didx = sb("didx", [P, 2, TPR], i32)
        sidx = sb("sidx", [P, 2, TPR], i32)
        slot_keys = sb("slot_keys", [P, 2, 2, TPR])
        got = sb("got", [P, 2, TPR, W])
        got_d = sb("got_d", [P, 2, TPR, W])
        e_stats = sb("e_stats", [P, TPR, 6])
        e_mv = sb("e_mv", [P, TPR, 2])
        e_sd = sb("e_sd", [P, TPR])
        e_h = sb("e_h", [P, 2, TPR, D])
        e_ht = sb("e_ht", [P, 2, TPR * P])
        e_htm = sb("e_htm", [P, 2, NREL, P])
        eq = sb("eq", [P, 2, TPR, 2, P])
        msg = sb("msg", [P, 2, TPR, W])
        res = sb("res", [P, 2, TPR, W])
        psum_out = sb("psum_out", [P, 2, TPR, W])
        q_sb = sb("q_sb", [P, 2, 2, D])
        qk = sb("qk", [P, 2, D])
        att_raw = sb("att_raw", [P, 2, 2 * HEADS])
        dup_out = sb("dup_out", [P, TPR, 2 * P])
        att_sum = sb("att_sum", [P, 2 * HEADS])
        dup = sb("dup", [P, TPR])
        sp_a = sb("sp_a", [P, TPR])
        sp_b = sb("sp_b", [P, TPR])
        xr = sb("xr", [P, SLOTS, K, W])
        sr = sb("sr", [P, SLOTS, K, W])
        x2r = sb("x2r", [P, SLOTS, K, W])
        in_stats = sb("in_stats", [P, K, 6])
        in_mv = sb("in_mv", [P, K, 2])
        in_sd = sb("in_sd", [P, K])
        mid_stats = sb("mid_stats", [P, K, 6])
        mid_mv = sb("mid_mv", [P, K, 2])
        mid_sd = sb("mid_sd", [P, K])
        mid_ac = sb("mid_ac", [P, 2, 2, K])
        root_deg = sb("root_deg", [P, K])
        out_stats = sb("out_stats", [P, K, 6])
        out_mv = sb("out_mv", [P, K, 2])
        out_sd = sb("out_sd", [P, K])
        per_edge = sb("per_edge", [P, K])
        rstd = sb("rstd", [P, K])
        den = sb("den", [P, K, HEADS])
        n_h = sb("n_h", [P, 2, K, D])
        n_ht = sb("n_ht", [P, 2, K * P])
        n_t = sb("n_t", [P, 2, K, D])
        n_u = sb("n_u", [P, 2, K, D])

        bank = [ctx.enter_context(nc.psum_tensor(f"bank{i}", [P, 512], fp32)) for i in range(8)]
        kv_bank = [bank[3], bank[6]]

        s_const = sem("s_const")
        s_pads = sem("s_pads")
        s_weights = sem("s_weights")
        s_keys = sem("s_keys")
        s_keysf = sem("s_keysf")
        s_keyst = sem("s_keyst")
        s_keysc = sem("s_keysc")
        s_prep = sem("s_prep")
        s_setup = sem("s_setup")
        s_wt = sem("s_wt")
        s_zero_sums = sem("s_zero_sums")
        s_zero_att = sem("s_zero_att")
        s_gate = sem("s_gate")

        gidx_ready = Signal(sem("gidx_ready"), 1)
        slots_ready = Signal(sem("slots_ready"), 1)
        sidx_ready = Signal(sem("sidx_ready"), 1)
        gathered = [Signal(sem(f"gathered{b}"), 16 * TPR) for b in range(2)]
        gathered_d = [Signal(sem(f"gathered_d{b}"), 16 * TPR) for b in range(2)]
        e_var_ready = Signal(sem("e_var_ready"), 1)
        e_sd_ready = Signal(sem("e_sd_ready"), 1)
        e_scale_ready = Signal(sem("e_scale_ready"), 1)
        h_ready = Signal(sem("h_ready"), 1, 2)
        turned = Signal(sem("turned"), 1, 2)
        ht_ready = Signal(sem("ht_ready"), 1, 2)
        htm_ready = Signal(sem("htm_ready"), TPR)
        y_ready = Signal(sem("y_ready"), TPR, 2 * TPR)
        keys_spread = Signal(sem("keys_spread"), 1)
        eq_ready = Signal(sem("eq_ready"), 1, 2)
        msg_ready = Signal(sem("msg_ready"), 1, 2)
        seg_done = Signal(sem("seg_done"), TPR, 2 * TPR)
        seg_out = Signal(sem("seg_out"), TPR, 2 * TPR)
        scattered = [Signal(sem(f"scattered{b}"), 16 * TPR) for b in range(2)]
        a_h = Signal(sem("a_h"), 2, 4)
        a_turned = Signal(sem("a_turned"), 2, 4)
        a_ht = Signal(sem("a_ht"), 2, 4)
        a_qkv = Signal(sem("a_qkv"), 2, 4)
        a_q = Signal(sem("a_q"), 2, 4)
        a_logit = Signal(sem("a_logit"), 2, 4)
        a_exp = Signal(sem("a_exp"), 2, 4)
        a_res = Signal(sem("a_res"), 2, 4)
        a_sum = Signal(sem("a_sum"), 4, 8)
        a_out = Signal(sem("a_out"), 4, 8)
        a_eq = Signal(sem("a_eq"), 1, 2)
        a_spread = Signal(sem("a_spread"), 1)
        a_acc = Signal(sem("a_acc"), 64)
        credited = [h_ready, turned, ht_ready, y_ready, eq_ready, msg_ready, seg_done, seg_out,
                    a_h, a_turned, a_ht, a_qkv, a_q, a_logit, a_exp, a_res, a_sum, a_out, a_eq]
        loaded = [Signal(sem(f"loaded{s}"), 32) for s in range(SLOTS)]
        loaded2 = [Signal(sem(f"loaded2_{s}"), 16) for s in range(SLOTS)]
        stored = [Signal(sem(f"stored{s}"), 16) for s in range(SLOTS)]
        in_var = Signal(sem("in_var"), 1)
        in_sd_ready = Signal(sem("in_sd_ready"), 1)
        in_scale = Signal(sem("in_scale"), 1)
        out_var = Signal(sem("out_var"), 1)
        out_sd_ready = Signal(sem("out_sd_ready"), 1)
        n_h_ready = Signal(sem("n_h_ready"), 1, 2)
        n_turned = Signal(sem("n_turned"), 1, 2)
        n_ht_ready = Signal(sem("n_ht_ready"), 1, 2)
        n_y_ready = Signal(sem("n_y_ready"), 1, 2)
        n_y_used = Signal(sem("n_y_used"), 1, 2)
        mid_var = Signal(sem("mid_var"), 1)
        mid_sd_ready = Signal(sem("mid_sd_ready"), 1)
        mid_scale = Signal(sem("mid_scale"), 1, 2)
        mid_ready = Signal(sem("mid_ready"), 1)
        row_ready = Signal(sem("row_ready"), 1, 2)
        credited += [n_h_ready, n_turned, n_ht_ready, n_y_ready, n_y_used, mid_scale, row_ready]
        dve_edge = sem("dve_edge")
        dve_in = sem("dve_in")
        dve_in_scales = sem("dve_in_scales")
        dve_combine = sem("dve_combine")
        dve_mid_scales = sem("dve_mid_scales")
        dve_finish = sem("dve_finish")
        dve_out_scales = sem("dve_out_scales")
        dve_setup = sem("dve_setup")

        block = ctx.enter_context(nc.Block())

        def gate(eng):
            eng.sem_inc(s_gate, 1)

        def parity_first(phase, b):
            return phase * (ROUNDS // 2 + 1 - b)

        def seg_index(phase):
            return SEG_PHASES.index(phase)

        def stores_before(phase, s):
            return phase * (GROUPS // SLOTS + (1 if s < GROUPS % SLOTS else 0))

        MATMUL = [REL, SAGE0, SAGE1, GCN]
        MID_NORM = [SAGE0, SAGE1]
        ROW_STATS = [REL, ATT, SAGE1]

        def first(phases, phase):
            return phases.index(phase) * GROUPS

        node_in = {REL: x, ATT: rows1, SAGE0: rows2, SAGE1: rowsg, GCN: rows3}
        node_sum = {REL: sums, ATT: attsums, SAGE0: sums, SAGE1: sums, GCN: sums}
        node_out = {REL: rows1, ATT: rows2, SAGE0: rowsg, SAGE1: rows3, GCN: out}
        node_w = {REL: w_loop_sb[:, :], SAGE0: w_t[:, 0, :], SAGE1: w_t[:, 2, :], GCN: w_gcn_sb[:, :]}
        edge_w = {SAGE0: w_t[:, 1, :], SAGE1: w_t[:, 3, :], GCN: w_gcn_sb[:, :]}
        edge_in = {REL: x, ATT: rows1, SAGE0: rows2, SAGE1: rowsg, GCN: rows3}

        ZROWS = zeros.shape[1] // W
        ZPARTS = N // P // ZROWS
        assert ZPARTS * ZROWS * P <= N
        ZERO_DMAS = ZPARTS + 1
        ZLEFT = PAD + 1 - ZPARTS * ZROWS * P
        ZLEFT_A = ZLEFT // P * P
        ZERO_COUNT = ZPARTS + (1 if ZLEFT_A else 0) + (1 if ZLEFT - ZLEFT_A else 0)

        @block.sync
        def _(sp):
            for sig in credited:
                sp.sem_inc(sig.sem, sig.credit)
            sp.wait_ge(s_pads, 1)
            for n, (keys, shift) in enumerate([(src, 0), (dst, 0), (dst, 1), (edge_type, 0)]):
                sp.dma_start(key_rows[:, n, 0, :], keys[shift:shift + P * P].rearrange("(t p) -> t p", p=P))\
                    .then_inc(s_keys, 16)
                full = (E - shift) // P
                sp.dma_start(key_rows[0:full - P, n, 1, :],
                             keys[shift + P * P:shift + full * P].rearrange("(t p) -> t p", p=P)).then_inc(s_keys, 16)
                left = E - shift - full * P
                sp.dma_start(key_rows[full - P:full - P + 1, n, 1, 0:left],
                             keys[shift + full * P:E].rearrange("(t p) -> t p", t=1)).then_inc(s_keys, 16)
            sp.wait_ge(s_const, 1)
            for table, s_zero in ((sums, s_zero_sums), (attsums, s_zero_att)):
                at = 0
                for _z in range(ZPARTS):
                    sp.dma_start(table[at:at + ZROWS * P, :].rearrange("(p r) c -> p (r c)", p=P), zeros[:, :])\
                        .then_inc(s_zero, 16)
                    at += ZROWS * P
                if ZLEFT_A:
                    sp.dma_start(table[at:at + ZLEFT_A, :].rearrange("(p r) c -> p (r c)", p=P),
                                 zeros[:, 0:ZLEFT_A // P * W]).then_inc(s_zero, 16)
                    at += ZLEFT_A
                if ZLEFT - ZLEFT_A:
                    sp.dma_start(table[at:PAD + 1, :], zeros[0:ZLEFT - ZLEFT_A, 0:W]).then_inc(s_zero, 16)

            for phase in range(5):
                if phase == ATT:
                    sp.wait_ge(a_acc.sem, ROUNDS * 64)
                else:
                    for b in range(2):
                        sp.wait_ge(scattered[b].sem, parity_first(seg_index(phase) + 1, b) * 16 * TPR)
                if phase > 0:
                    for s in range(SLOTS):
                        sp.wait_ge(stored[s].sem, 16 * stores_before(phase, s))

                def span(g):
                    if g.i is None and g.offset == GROUPS - 1:
                        return slice(N - GROUP, N)
                    return bass.ds(g.scaled(GROUP), GROUP)

                def load(g):
                    s = g.mod(SLOTS)
                    v = g.div(SLOTS)
                    wait_landed(sp, stored[s], stored[s].before(v, 1, stores_before(phase, s)))
                    table = node_in[phase]
                    width = table.shape[1]
                    sp.dma_start(xr[:, s, :, 0:width], table[span(g), :].rearrange("(p k) c -> p k c", k=K))\
                        .then_inc(loaded[s].sem, 16)
                    sp.dma_start(sr[:, s, :, :], node_sum[phase][span(g), :].rearrange("(p k) c -> p k c", k=K))\
                        .then_inc(loaded[s].sem, 16)
                    if phase == SAGE1:
                        sp.dma_start(x2r[:, s, :, :], rows2[span(g), :].rearrange("(p k) c -> p k c", k=K))\
                            .then_inc(loaded2[s].sem, 16)

                def store(g):
                    s = g.mod(SLOTS)
                    sp.wait_ge(row_ready.sem, row_ready.after(g, phase * GROUPS))
                    if g.i is None and g.offset == GROUPS - 1:
                        o = (GROUPS - 2) % SLOTS
                        sp.wait_ge(stored[o].sem, 16 * (stores_before(phase, o) + (GROUPS - 2) // SLOTS + 1))
                    table = node_out[phase]
                    ring = x2r if phase == SAGE1 else xr
                    sp.dma_start(table[span(g), :].rearrange("(p k) c -> p k c", k=K),
                                 ring[:, s, :, 0:table.shape[1]]).then_inc(stored[s].sem, 16)

                run_steps(sp, [(load, 0), (store, 4)], GROUPS, SLOTS, behind=SLOTS)
            for s in range(SLOTS):
                sp.wait_ge(stored[s].sem, 16 * stores_before(5, s))

        @block.gpsimd
        def _(pool):
            nc.gpsimd.memset(key_rows[:, :, :, :], PAD).then_inc(s_pads, 1)
            nc.gpsimd.memset(zeros[:, :], 0.0).then_inc(s_const, 1)
            nc.gpsimd.memset(ident[:, :], 0.0).then_inc(s_const, 1)
            nc.gpsimd.memset(ones_row[:, :], 1.0).then_inc(s_const, 1)
            nc.gpsimd.memset(ones_col[:, :], 1.0).then_inc(s_const, 1)
            nc.gpsimd.memset(eps_col[:, :], EPS).then_inc(s_const, 1)
            nc.gpsimd.memset(msg[:, :, :, :], 0.0).then_inc(s_const, 1)
            nc.gpsimd.memset(psum_out[:, :, :, :], 0.0).then_inc(s_const, 1)
            nc.gpsimd.memset(earlier[:, :, :], 1.0).then_inc(s_const, 1)
            nc.gpsimd.memset(carry_key[:, :], -1.0).then_inc(s_const, 1)
            nc.gpsimd.memset(res[:, :, :, :], 0.0).then_inc(s_const, 1)
            nc.gpsimd.memset(got[:, :, :, :], 0.0).then_inc(s_const, 1)
            nc.gpsimd.memset(got_d[:, :, :, :], 0.0).then_inc(s_const, 1)
            nc.gpsimd.memset(xr[:, :, :, :], 0.0).then_inc(s_const, 1)
            nc.gpsimd.memset(x2r[:, :, :, :], 0.0).then_inc(s_const, 1)
            nc.gpsimd.iota(spare_f[:, :].rearrange("p (q a) -> p q a", a=2), pattern=[[0, 2], [P, 2]], base=N,
                           channel_multiplier=1, allow_small_or_imprecise_dtypes=True).then_inc(s_const, 1)
            pool.wait_ge(s_const, 15)
            nc.gpsimd.affine_select(out=ident[:, :], in_=ident[:, :], compare_op=ALU.not_equal, fill=1.0,
                                    base=0, pattern=[[-1, P]], channel_multiplier=1).then_inc(s_const, 1)
            nc.gpsimd.affine_select(out=earlier[:, :, :], in_=earlier[:, :, :], compare_op=ALU.is_gt, fill=0.0,
                                    base=0, pattern=[[P, 2], [-1, 2 * P]], channel_multiplier=1).then_inc(s_const, 1)
            nc.gpsimd.memset(msg[:, :, :, COL_CNT:COL_CNT + 1], 1.0).then_inc(s_const, 1)
            pool.wait_ge(s_keysc, 1)
            nc.gpsimd.affine_select(out=carry_key[:, 1:TILES], in_=dst_f[:, 0:TILES - 1], compare_op=ALU.is_ge,
                                    fill=-1.0, base=-(P - 1), pattern=[[0, TILES - 1]], channel_multiplier=1)\
                .then_inc(s_setup, 1)
            bound = pool.to_reg(N - 1)
            top = pool.to_reg(PAD)

            for phase in range(5):
                if phase > 0:
                    for s in range(SLOTS):
                        pool.wait_ge(stored[s].sem, 16 * stores_before(phase, s))
                table = edge_in[phase]
                width = table.shape[1]

                def gather(r, tiles=range(TPR)):
                    b = r.mod(2)
                    if tiles[0] == 0:
                        pool.wait_ge(gidx_ready.sem, gidx_ready.after(r, phase * ROUNDS))
                        if phase == ATT:
                            pool.wait_ge(a_h.sem, a_h.before(r, 2))
                        else:
                            pool.wait_ge(h_ready.sem, h_ready.before(r, 2, seg_index(phase) * ROUNDS))
                        gate(pool)
                    for j in tiles:
                        pool.indirect_dma_start(
                            out=got[:, b, j, 0:width], out_offset=None, in_=table[:, :],
                            in_offset=bass.IndirectOffsetOnAxis(ap=gidx[:, b, j:j + 1], axis=0),
                            bounds_check=bound, oob_is_err=False).then_inc(gathered[b].sem, 16)
                        if phase == ATT:
                            pool.indirect_dma_start(
                                out=got_d[:, b, j, :], out_offset=None, in_=table[:, :],
                                in_offset=bass.IndirectOffsetOnAxis(ap=didx[:, b, j:j + 1], axis=0),
                                bounds_check=bound, oob_is_err=False).then_inc(gathered_d[b].sem, 16)

                    if phase == REL and r.i is None and r.offset == 1:
                        pool.wait_ge(s_zero_sums, 16 * ZERO_COUNT)

                def scatter(r):
                    b = r.mod(2)
                    seg = seg_index(phase)
                    pool.wait_ge(sidx_ready.sem, sidx_ready.after(r, phase * ROUNDS))
                    for j in range(TPR):
                        pool.wait_ge(seg_out.sem, seg_out.after(r, seg * ROUNDS, j + 1))
                        gate(pool)
                        pool.indirect_dma_start(
                            out=sums[:, :], out_offset=bass.IndirectOffsetOnAxis(ap=sidx[:, b, j:j + 1], axis=0),
                            in_=psum_out[:, b, j, :], in_offset=None,
                            bounds_check=bound, oob_is_err=False).then_inc(scattered[b].sem, 16)

                def add_pair(r, q):
                    b = r.mod(2)
                    if q == 0:
                        pool.wait_ge(sidx_ready.sem, sidx_ready.after(r, phase * ROUNDS))
                    pool.wait_ge(a_out.sem, a_out.after(r, 0, 2 * q + 2))
                    wait_landed(pool, a_acc, a_acc.after(r, 0, 32 * q))
                    gate(pool)
                    for j in (2 * q, 2 * q + 1):
                        pool.indirect_dma_start(
                            out=attsums[:, :], out_offset=bass.IndirectOffsetOnAxis(ap=sidx[:, b, j:j + 1], axis=0),
                            in_=psum_out[:, b, j, :], in_offset=None, bounds_check=top, oob_is_err=True,
                            compute_op=ALU.add).then_inc(a_acc.sem, 16)

                if phase == ATT:
                    pool.wait_ge(s_zero_att, 16 * ZERO_COUNT)
                    run_steps(pool, [(lambda r: gather(r, range(0, 2)), 0), (lambda r: add_pair(r, 0), 2),
                                     (lambda r: gather(r, range(2, 4)), 0), (lambda r: add_pair(r, 1), 2)],
                              ROUNDS, 2, behind=2)
                else:
                    run_steps(pool, [(gather, 0), (scatter, 2)], ROUNDS, 2)

        @block.scalar
        def _(act):
            act.dma_start(w_rel_sb[:, :, :], w_rel.rearrange("r d o -> d r o")).then_inc(s_weights, 16)
            act.dma_start(w_loop_sb[:, :], w_loop).then_inc(s_weights, 16)
            for n, w in enumerate((w_self0, w_neigh0, w_self1, w_neigh1)):
                act.dma_start(w_in[:, n, :], w).then_inc(s_weights, 16)
            act.dma_start(w_q_sb[:, :], w_q).then_inc(s_weights, 16)
            act.dma_start(w_kv_sb[:, 0, :], w_k).then_inc(s_weights, 16)
            act.dma_start(w_kv_sb[:, 1, :], w_v).then_inc(s_weights, 16)
            act.dma_start(w_gcn_sb[:, :], w_gcn).then_inc(s_weights, 16)
            for n, v in enumerate((b_loop, b0, b1)):
                act.dma_start(bias_rows[:, n, :], v.rearrange("(a n) -> a n", a=1)).then_inc(s_weights, 16)
            act.dma_start(ln_g_bc[:, :], ln_g.rearrange("(a n) -> a n", a=1).to_broadcast([P, D])).then_inc(s_weights, 16)
            act.dma_start(ln_b_bc[:, :], ln_b.rearrange("(a n) -> a n", a=1).to_broadcast([P, D])).then_inc(s_weights, 16)
            act.wait_ge(s_const, 18)

            def seg_phase(phase):
                first_r = seg_index(phase) * ROUNDS

                def normalise(r):
                    b = r.mod(2)
                    if phase == REL:
                        act.wait_ge(e_var_ready.sem, e_var_ready.after(r))
                        nc.scalar.activation(e_sd[:, :], e_mv[:, :, 1], ACT.Sqrt, bias=eps_col[:, 0:1])\
                            .then_inc(e_sd_ready.sem, 1)
                        act.wait_ge(e_scale_ready.sem, e_scale_ready.after(r))
                    v = r.div(2)
                    act.wait_ge(gathered[b].sem, gathered[b].after(v, parity_first(phase, b)))
                    act.wait_ge(turned.sem, turned.before(r, 2, first_r))
                    for j in range(TPR):
                        last = nc.scalar.activation(e_h[:, b, j, :], got[:, b, j, 0:D], ACT.Relu,
                                                    bias=got[:, b, j, COL_C:COL_C + 1],
                                                    scale=got[:, b, j, COL_A:COL_A + 1])
                    last.then_inc(h_ready.sem, 1)

                def take_turned(r):
                    b = r.mod(2)
                    act.wait_ge(turned.sem, turned.after(r, first_r))
                    act.wait_ge(y_ready.sem, y_ready.before(r, 2, first_r))
                    nc.scalar.activation(e_ht[:, b, :], bank[0][:, :], ACT.Copy).then_inc(ht_ready.sem, 1)

                def take_sums(r):
                    b = r.mod(2)
                    wait_landed(act, scattered[b], scattered[b].before(r.div(2), 1, parity_first(seg_index(phase), b)))
                    for j in range(TPR):
                        act.wait_ge(seg_done.sem, seg_done.after(r, first_r, j + 1))
                        nc.scalar.activation(psum_out[:, b, j, :], bank[4 + j % 2][:, 0:W], ACT.Copy)\
                            .then_inc(seg_out.sem, 1)

                run_steps(act, [(take_sums, 1), (normalise, 0), (take_turned, 0)], ROUNDS, 2, behind=2)

            def att_phase():
                def normalise(r, q):
                    b = r.mod(2)
                    if q == 0:
                        act.wait_ge(gathered[b].sem, gathered[b].after(r.div(2), parity_first(ATT, b)))
                        act.wait_ge(gathered_d[b].sem, gathered_d[b].after(r.div(2)))
                    act.wait_ge(a_turned.sem, a_turned.after(r, 0, 2 * 0 + q + 1 - 2))
                    for a in range(2):
                        for n, rows in enumerate((got, got_d)):
                            last = nc.scalar.activation(e_h[:, q, 2 * n + a, :], rows[:, b, 2 * q + a, 0:D], ACT.Relu,
                                                        bias=rows[:, b, 2 * q + a, COL_C:COL_C + 1],
                                                        scale=rows[:, b, 2 * q + a, COL_A:COL_A + 1])
                    last.then_inc(a_h.sem, 1)

                def take_turned(r, q):
                    act.wait_ge(a_turned.sem, a_turned.after(r, 0, q + 1))
                    act.wait_ge(a_qkv.sem, a_qkv.after(r, 0, q + 1 - 2))
                    nc.scalar.activation(e_ht[:, q, :], bank[q][:, :], ACT.Copy).then_inc(a_ht.sem, 1)

                def take_q(r, q):
                    act.wait_ge(a_qkv.sem, a_qkv.after(r, 0, q + 1))
                    act.wait_ge(a_logit.sem, a_logit.after(r, 0, q + 1 - 2))
                    nc.scalar.activation(q_sb[:, q, :, :], bank[2][:, 256 * q:256 * q + 256], ACT.Copy)\
                        .then_inc(a_q.sem, 1)

                def exponentials(r, q):
                    act.wait_ge(a_logit.sem, a_logit.after(r, 0, q + 1))
                    b = r.mod(2)
                    act.wait_ge(a_sum.sem, a_sum.before(r, 2))
                    nc.scalar.activation(res[:, b, 2 * q:2 * q + 2, D:W],
                                         att_raw[:, q, :].rearrange("p (a h) -> p a h", a=2), ACT.Exp)\
                        .then_inc(a_exp.sem, 1)

                def take_sums(r, q):
                    b = r.mod(2)
                    wait_landed(act, a_acc, a_acc.before(r, 2))
                    for a in range(2):
                        j = 2 * q + a
                        act.wait_ge(a_sum.sem, a_sum.after(r, 0, j + 1))
                        nc.scalar.activation(psum_out[:, b, j, :], bank[4 + a][:, 0:W], ACT.Copy)\
                            .then_inc(a_out.sem, 1)

                def last_sums(r):
                    take_sums(r, 0)
                    take_sums(r, 1)

                def pairs(r):
                    normalise(r, 0)
                    take_turned(r, 0)
                    normalise(r, 1)
                    take_q(r, 0)
                    take_turned(r, 1)
                    exponentials(r, 0)
                    take_q(r, 1)
                    exponentials(r, 1)

                run_steps(act, [(last_sums, 1), (pairs, 0)], ROUNDS, 2, behind=2)

            def node_phase(phase):
                def in_root(g):
                    act.wait_ge(in_var.sem, in_var.after(g))
                    nc.scalar.activation(in_sd[:, :], in_mv[:, :, 1], ACT.Sqrt, bias=eps_col[:, 0:1])\
                        .then_inc(in_sd_ready.sem, 1)

                def normalise(g):
                    s, b = g.mod(SLOTS), g.mod(2)
                    mm = first(MATMUL, phase)
                    act.wait_ge(loaded[s].sem, loaded[s].after(g.div(SLOTS), stores_before(phase, s)))
                    if phase == REL:
                        act.wait_ge(in_scale.sem, in_scale.after(g))
                    act.wait_ge(n_turned.sem, n_turned.before(g, 2, mm))
                    for k in range(K):
                        last = nc.scalar.activation(n_h[:, b, k, :], xr[:, s, k, 0:D], ACT.Relu,
                                                    bias=xr[:, s, k, COL_C:COL_C + 1],
                                                    scale=xr[:, s, k, COL_A:COL_A + 1])
                    last.then_inc(n_h_ready.sem, 1)

                def take_turned(g):
                    b = g.mod(2)
                    mm = first(MATMUL, phase)
                    act.wait_ge(n_turned.sem, n_turned.after(g, mm))
                    act.wait_ge(n_y_ready.sem, n_y_ready.before(g, 2, mm))
                    nc.scalar.activation(n_ht[:, b, :], bank[b][:, :], ACT.Copy).then_inc(n_ht_ready.sem, 1)

                def mid_root(g):
                    act.wait_ge(mid_var.sem, mid_var.after(g, first(MID_NORM, phase)))
                    if phase == SAGE1:
                        nc.scalar.activation(root_deg[:, :], sr[:, g.mod(SLOTS), :, COL_CNT], ACT.Sqrt,
                                             bias=ones_col[:, 0:1])
                    nc.scalar.activation(mid_sd[:, :], mid_mv[:, :, 1], ACT.Sqrt, bias=eps_col[:, 0:1])\
                        .then_inc(mid_sd_ready.sem, 1)

                def mid_normalise(g):
                    b = g.mod(2)
                    act.wait_ge(mid_scale.sem, mid_scale.after(g, first(MID_NORM, phase)))
                    act.wait_ge(row_ready.sem, row_ready.before(g, 2, phase * GROUPS))
                    for k in range(K):
                        last = nc.scalar.activation(n_u[:, b, k, :], n_t[:, b, k, :], ACT.Identity,
                                                    bias=mid_ac[:, b, 1, k:k + 1], scale=mid_ac[:, b, 0, k:k + 1])
                    last.then_inc(mid_ready.sem, 1)

                def out_root(g):
                    act.wait_ge(out_var.sem, out_var.after(g, first(ROW_STATS, phase)))
                    nc.scalar.activation(out_sd[:, :], out_mv[:, :, 1], ACT.Sqrt, bias=eps_col[:, 0:1])\
                        .then_inc(out_sd_ready.sem, 1)

                stages = {
                    REL: [(in_root, 0), (out_root, 1), (normalise, 0), (take_turned, 0)],
                    ATT: [(out_root, 0)],
                    SAGE0: [(normalise, 0), (mid_root, 1), (take_turned, 0), (mid_normalise, 1)],
                    SAGE1: [(normalise, 0), (mid_root, 1), (out_root, 2), (take_turned, 0), (mid_normalise, 1)],
                    GCN: [(normalise, 0), (take_turned, 0)],
                }[phase]
                run_steps(act, stages, GROUPS, SLOTS)

            for phase in range(5):
                if phase == ATT:
                    att_phase()
                else:
                    seg_phase(phase)
                node_phase(phase)

        @block.tensor
        def _(pe):
            pe.wait_ge(s_const, 18)
            pe.wait_ge(s_keysf, 1)
            for n in range(4):
                for half in range(2):
                    at = (2 * n + half) * P
                    last = nc.tensor.transpose(bank[at // 512][:, at % 512:at % 512 + P],
                                               key_rows_f[:, n, half, :], ident[:, :])
            last.then_inc(s_keyst, 1)
            pe.wait_ge(s_weights, 16 * 15)
            for n in range(4):
                last = nc.tensor.transpose(bank[2][:, n * P:(n + 1) * P], w_in[:, n, :], ident[:, :])
            last.then_inc(s_wt, 1)
            pe.wait_ge(s_prep, 1)

            def spread(n, r, j, out_ps):
                return nc.tensor.matmul(out_ps, lhsT=slot_keys[:, r.mod(2), n, j:j + 1].to_broadcast([P, P]),
                                        rhs=ident[:, :], start=True, stop=True)

            def seg_phase(phase):
                f = seg_index(phase) * ROUNDS

                def spread_keys(r):
                    pe.wait_ge(slots_ready.sem, slots_ready.after(r, phase * ROUNDS))
                    pe.wait_ge(eq_ready.sem, eq_ready.before(r, 1, f))
                    if phase == REL:
                        pe.wait_ge(y_ready.sem, y_ready.before(r, 1, f))
                    for j in range(TPR):
                        last = spread(0, r, j, bank[2][:, j * P:(j + 1) * P])
                    if phase == REL:
                        for j in range(TPR):
                            last = spread(1, r, j, bank[3][:, j * P:(j + 1) * P])
                    last.then_inc(keys_spread.sem, 1)

                def turn_rows(r):
                    pe.wait_ge(h_ready.sem, h_ready.after(r, f))
                    pe.wait_ge(ht_ready.sem, ht_ready.before(r, 1, f))
                    for j in range(TPR):
                        last = nc.tensor.transpose(bank[0][:, j * P:(j + 1) * P], e_h[:, r.mod(2), j, :], ident[:, :])
                    last.then_inc(turned.sem, 1)

                def products(r):
                    b = r.mod(2)
                    pe.wait_ge(ht_ready.sem, ht_ready.after(r, f))
                    pe.wait_ge(msg_ready.sem, msg_ready.before(r, 1, f))
                    for j in range(TPR):
                        o = bank[1][:, j * P:(j + 1) * P]
                        if phase == REL:
                            pe.wait_ge(htm_ready.sem, htm_ready.after(r, 0, j + 1))
                            for rel in range(NREL):
                                last = nc.tensor.matmul(o, lhsT=e_htm[:, j % 2, rel, :], rhs=w_rel_sb[:, rel, :],
                                                        start=(rel == 0), stop=(rel == NREL - 1))
                        else:
                            last = nc.tensor.matmul(o, lhsT=e_ht[:, b, j * P:(j + 1) * P], rhs=edge_w[phase],
                                                    start=True, stop=True)
                        last.then_inc(y_ready.sem, 1)

                def segment_sums(r):
                    b = r.mod(2)
                    pe.wait_ge(eq_ready.sem, eq_ready.after(r, f))
                    pe.wait_ge(msg_ready.sem, msg_ready.after(r, f))
                    for j in range(TPR):
                        o = bank[4 + j % 2][:, 0:W]
                        pe.wait_ge(seg_out.sem, seg_out.after(r, f, j + 1 - 2))
                        nc.tensor.matmul(o, lhsT=eq[:, b, j, 0, :], rhs=msg[:, b, j, :], start=True, stop=False)
                        pe.wait_ge(seg_out.sem, seg_out.after(r, f, j))
                        carried = psum_out[:, b, j - 1, :] if j else psum_out[:, 1 - b, TPR - 1, :]
                        nc.tensor.matmul(o, lhsT=eq[:, b, j, 1, :], rhs=carried, start=False, stop=True)\
                            .then_inc(seg_done.sem, 1)

                run_steps(pe, [(segment_sums, 1), (spread_keys, 0), (turn_rows, 0), (products, 0)], ROUNDS, 2)

            def att_phase():
                def pair_sums(r, q):
                    b = r.mod(2)
                    if q == 0:
                        pe.wait_ge(a_eq.sem, a_eq.after(r))
                    pe.wait_ge(a_res.sem, a_res.after(r, 0, q + 1))
                    for a in range(2):
                        pe.wait_ge(a_out.sem, a_out.after(r, 0, 2 * q + a + 1 - 2))
                        for a2 in range(2):
                            last = nc.tensor.matmul(bank[4 + a][:, 0:W], lhsT=eq[:, b, 2 * q + a2, a, :],
                                                    rhs=res[:, b, 2 * q + a2, :], start=(a2 == 0), stop=(a2 == 1))
                        last.then_inc(a_sum.sem, 1)

                def last_sums(r):
                    pair_sums(r, 0)
                    pair_sums(r, 1)

                def spread_keys(r):
                    pe.wait_ge(slots_ready.sem, slots_ready.after(r, ATT * ROUNDS))
                    pe.wait_ge(a_eq.sem, a_eq.before(r, 1))
                    for j in range(TPR):
                        last = spread(0, r, j, bank[7][:, j * P:(j + 1) * P])
                    last.then_inc(a_spread.sem, 1)

                def pairs(r):
                    for q in range(2):
                        pe.wait_ge(a_h.sem, a_h.after(r, 0, q + 1))
                        pe.wait_ge(a_ht.sem, a_ht.after(r, 0, q + 1 - 2))
                        for n in range(4):
                            last = nc.tensor.transpose(bank[q][:, n * P:(n + 1) * P], e_h[:, q, n, :], ident[:, :])
                        last.then_inc(a_turned.sem, 1)
                        pe.wait_ge(a_ht.sem, a_ht.after(r, 0, q + 1))
                        pe.wait_ge(a_q.sem, a_q.after(r, 0, q + 1 - 2))
                        pe.wait_ge(a_res.sem, a_res.after(r, 0, q + 1 - 2))
                        for a in range(2):
                            nc.tensor.matmul(bank[2][:, 256 * q + a * P:256 * q + (a + 1) * P],
                                             lhsT=e_ht[:, q, a * P:(a + 1) * P], rhs=w_q_sb[:, :],
                                             start=True, stop=True)
                            last = nc.tensor.matmul(kv_bank[q][:, 256 * a:256 * a + 256],
                                                    lhsT=e_ht[:, q, (2 + a) * P:(3 + a) * P],
                                                    rhs=w_kv_sb[:, :, :].rearrange("p n d -> p (n d)"),
                                                    start=True, stop=True)
                        last.then_inc(a_qkv.sem, 1)

                run_steps(pe, [(last_sums, 1), (spread_keys, 0), (pairs, 0)], ROUNDS, 2)

            def node_phase(phase):
                mm = first(MATMUL, phase)

                def turn_rows(g):
                    b = g.mod(2)
                    pe.wait_ge(n_h_ready.sem, n_h_ready.after(g, mm))
                    pe.wait_ge(n_ht_ready.sem, n_ht_ready.before(g, 2, mm))
                    for k in range(K):
                        last = nc.tensor.transpose(bank[b][:, k * P:(k + 1) * P], n_h[:, b, k, :], ident[:, :])
                    last.then_inc(n_turned.sem, 1)

                def products(g):
                    b = g.mod(2)
                    pe.wait_ge(n_ht_ready.sem, n_ht_ready.after(g, mm))
                    pe.wait_ge(n_y_used.sem, n_y_used.before(g, 2, mm))
                    bias = {REL: 0, SAGE0: 1, SAGE1: 2}.get(phase)
                    for k in range(K):
                        o = bank[2 + b][:, k * P:(k + 1) * P]
                        if bias is not None:
                            nc.tensor.matmul(o, lhsT=ones_row[:, :], rhs=bias_rows[:, bias, :], start=True, stop=False)
                        last = nc.tensor.matmul(o, lhsT=n_ht[:, b, k * P:(k + 1) * P], rhs=node_w[phase],
                                                start=(bias is None), stop=True)
                    last.then_inc(n_y_ready.sem, 1)

                run_steps(pe, [(turn_rows, 0), (products, 0)], GROUPS, SLOTS)

            for phase in range(5):
                if phase == ATT:
                    att_phase()
                else:
                    seg_phase(phase)
                    node_phase(phase)

        @block.vector
        def _(dve):
            own = Chain(dve, dve_setup)
            own.begin(Step(None, 1, 0))
            dve.wait_ge(s_const, 18)
            dve.wait_ge(s_keys, 16 * 12)
            nc.vector.tensor_copy(key_rows_f[:, :, :, :], key_rows[:, :, :, :]).then_inc(s_keysf, 1)
            dve.wait_ge(s_keyst, 1)
            for n, cols in enumerate((src_f, dst_f, next_f, type_f)):
                at = 2 * n * P
                last = nc.vector.tensor_copy(cols[:, :], bank[at // 512][:, at % 512:at % 512 + TILES])
            last.then_inc(s_keysc, 1)
            dve.wait_ge(s_keysc, 1)
            own.mark(nc.vector.tensor_copy(src_i[:, :], src_f[:, :]))
            own.mark(nc.vector.tensor_copy(dst_i[:, :], dst_f[:, :]))
            own.mark(nc.vector.tensor_tensor(next_f[:, :], dst_f[:, :], next_f[:, :], ALU.is_equal))
            own.wait()
            own.mark(nc.vector.scalar_tensor_tensor(out=last_i[:, :], in0=next_f[:, :], scalar=float(PAD),
                                                    in1=dst_f[:, :], op0=ALU.mult, op1=ALU.max))
            dve.wait_ge(s_wt, 1)
            own.mark(nc.vector.tensor_copy(w_t[:, :, :].rearrange("p n d -> p (n d)"), bank[2][:, :]))
            own.wait()
            dve.wait_ge(s_setup, 1)
            dve.sem_inc(s_prep, 1)

            edge_chain = Chain(dve, dve_edge)
            in_chain = Chain(dve, dve_in)
            in_scales_chain = Chain(dve, dve_in_scales)
            combine_chain = Chain(dve, dve_combine)
            mid_scales_chain = Chain(dve, dve_mid_scales)
            finish_chain = Chain(dve, dve_finish)
            out_scales_chain = Chain(dve, dve_out_scales)

            def first_indices(phase):
                for b in range(2):
                    fill_slots(phase, b, slice(b * TPR, (b + 1) * TPR))
                    if phase == ATT:
                        nc.vector.tensor_copy(didx[:, b, :], dst_i[:, b * TPR:(b + 1) * TPR])
                    nc.vector.tensor_copy(gidx[:, b, :], src_i[:, b * TPR:(b + 1) * TPR])\
                        .then_inc(gidx_ready.sem, 1)

            def fill_slots(phase, b, columns):
                if phase == REL:
                    nc.vector.tensor_copy(slot_keys[:, b, 1, :], type_f[:, columns])
                nc.vector.tensor_copy(slot_keys[:, b, 0, :], (src_f if phase == ATT else dst_f)[:, columns])\
                    .then_inc(slots_ready.sem, 1)

            def next_slots(phase, r):
                if r.i is None and r.offset + 2 >= ROUNDS:
                    return
                fill_slots(phase, r.mod(2), bass.ds(r.scaled(TPR, 2 * TPR), TPR))

            def next_indices(phase, r):
                b = r.mod(2)
                dve.wait_ge(gathered[b].sem, gathered[b].after(r.div(2), parity_first(phase, b)))
                if phase == ATT:
                    dve.wait_ge(gathered_d[b].sem, gathered_d[b].after(r.div(2)))
                if r.i is None and r.offset + 2 >= ROUNDS:
                    return
                at = r.scaled(TPR, 2 * TPR)
                if phase == ATT:
                    nc.vector.tensor_copy(didx[:, b, :], dst_i[:, bass.ds(at, TPR)])
                nc.vector.tensor_copy(gidx[:, b, :], src_i[:, bass.ds(at, TPR)]).then_inc(gidx_ready.sem, 1)

            def seg_phase(phase):
                f = seg_index(phase) * ROUNDS
                own = edge_chain
                own.open(2 if phase == REL else 0)

                def statistics(r):
                    b = r.mod(2)
                    for j in range(TPR):
                        last = nc.vector.bn_stats(e_stats[:, j, :], got[:, b, j, 0:D])
                    own.mark(last)
                    own.wait()
                    gate(dve)
                    for j in range(TPR):
                        last = nc.vector.bn_aggr(e_mv[:, j, :], e_stats[:, j, :])
                    last.then_inc(e_var_ready.sem, 1)

                def scales(r):
                    b = r.mod(2)
                    dve.wait_ge(e_sd_ready.sem, e_sd_ready.after(r))
                    own.mark(nc.vector.reciprocal(got[:, b, :, COL_A], e_sd[:, :]))
                    own.wait()
                    nc.vector.scalar_tensor_tensor(out=got[:, b, :, COL_C], in0=e_mv[:, :, 0], scalar=-1.0,
                                                   in1=got[:, b, :, COL_A], op0=ALU.mult, op1=ALU.mult)\
                        .then_inc(e_scale_ready.sem, 1)

                def same_keys(r):
                    b = r.mod(2)
                    dve.wait_ge(keys_spread.sem, keys_spread.after(r, f))
                    dve.wait_ge(seg_done.sem, seg_done.before(r, 2, f))
                    for j in range(TPR):
                        for n, keys in enumerate((dst_f, carry_key)):
                            last = nc.vector.tensor_scalar(eq[:, b, j, n, :], bank[2][:, j * P:(j + 1) * P],
                                                           keys[:, bass.ds(r.scaled(TPR, j), 1)], None, ALU.is_equal)
                    last.then_inc(eq_ready.sem, 1)

                def by_relation(r):
                    b = r.mod(2)
                    dve.wait_ge(ht_ready.sem, ht_ready.after(r, f))
                    for j in range(TPR):
                        dve.wait_ge(y_ready.sem, y_ready.after(r, f, j + 1 - 2))
                        for rel in range(NREL):
                            last = nc.vector.scalar_tensor_tensor(
                                out=e_htm[:, j % 2, rel, :], in0=bank[3][:, j * P:(j + 1) * P], scalar=float(rel),
                                in1=e_ht[:, b, j * P:(j + 1) * P], op0=ALU.is_equal, op1=ALU.mult)
                        last.then_inc(htm_ready.sem, 1)

                def take_messages(r):
                    b = r.mod(2)
                    dve.wait_ge(y_ready.sem, y_ready.after(r, f))
                    nc.vector.tensor_copy(msg[:, b, :, 0:D], bank[1][:, :].rearrange("p (j d) -> p j d", j=TPR))\
                        .then_inc(msg_ready.sem, 1)

                def round_(r):
                    b = r.mod(2)
                    own.begin(r)
                    next_indices(phase, r)
                    if phase == REL:
                        statistics(r)
                    wait_landed(dve, scattered[b], scattered[b].before(r.div(2), 1, parity_first(seg_index(phase), b)))
                    nc.vector.tensor_copy(sidx[:, b, :], last_i[:, bass.ds(r.scaled(TPR), TPR)])\
                        .then_inc(sidx_ready.sem, 1)
                    same_keys(r)
                    next_slots(phase, r)
                    if phase == REL:
                        scales(r)
                        by_relation(r)
                    take_messages(r)
                    own.end()

                first_indices(phase)
                run_steps(dve, [(round_, 0)], ROUNDS, 2, ahead=2, behind=2)
                own.close(ROUNDS)

            def att_phase():
                own = edge_chain
                own.open(7)

                def same_keys(r):
                    b = r.mod(2)
                    dve.wait_ge(a_spread.sem, a_spread.after(r))
                    dve.wait_ge(a_sum.sem, a_sum.before(r, 2))
                    for j in range(TPR):
                        q = j // 2
                        last = nc.vector.tensor_scalar(eq[:, b, j, :, :].rearrange("p a e -> p (a e)"),
                                                       bank[7][:, 256 * q:256 * q + 256],
                                                       src_f[:, bass.ds(r.scaled(TPR, j), 1)], None, ALU.is_equal)
                    last.then_inc(a_eq.sem, 1)

                def sum_rows(r):
                    b = r.mod(2)
                    dve.wait_ge(a_eq.sem, a_eq.after(r))
                    own.mark(nc.vector.tensor_tensor(sp_a[:, :], spare_f[:, :], src_f[:, bass.ds(r.scaled(TPR), TPR)],
                                                     ALU.subtract))
                    for j in range(TPR):
                        last = nc.vector.tensor_tensor_reduce(
                            out=dup_out[:, j, :], in0=eq[:, b, j, :, :].rearrange("p a e -> p (a e)"),
                            in1=earlier[:, j % 2, :], scale=1.0, scalar=0.0, op0=ALU.mult, op1=ALU.add,
                            accum_out=dup[:, j:j + 1])
                    own.mark(last)
                    own.wait()
                    own.mark(nc.vector.scalar_tensor_tensor(out=sp_b[:, :], in0=dup[:, :], scalar=0.5, in1=sp_a[:, :],
                                                            op0=ALU.is_gt, op1=ALU.mult))
                    own.wait()
                    wait_landed(dve, a_acc, a_acc.before(r, 2))
                    nc.vector.tensor_tensor(sidx[:, b, :], sp_b[:, :], src_f[:, bass.ds(r.scaled(TPR), TPR)], ALU.add)\
                        .then_inc(sidx_ready.sem, 1)

                def logits(r, q):
                    kv = kv_bank[q][:, :].rearrange("p (a n d) -> p a n d", a=2, n=2)
                    dve.wait_ge(a_q.sem, a_q.after(r, 0, q + 1))
                    own.mark(nc.vector.tensor_tensor(qk[:, :, :], q_sb[:, q, :, :], kv[:, :, 0, :], ALU.mult))
                    own.wait()
                    own.mark(nc.vector.tensor_reduce(att_sum[:, :], qk[:, :, :].rearrange("p a (h d) -> p (a h) d", d=DH),
                                                     AX.X, ALU.add))
                    own.wait()
                    dve.wait_ge(a_exp.sem, a_exp.after(r, 0, q + 1 - 2))
                    nc.vector.tensor_scalar(att_raw[:, q, :], att_sum[:, :], 10.0, -10.0, ALU.min, ALU.max)\
                        .then_inc(a_logit.sem, 1)

                def weighted(r, q):
                    b = r.mod(2)
                    kv = kv_bank[q][:, :].rearrange("p (a n d) -> p a n d", a=2, n=2)
                    dve.wait_ge(a_exp.sem, a_exp.after(r, 0, q + 1))
                    for a in range(2):
                        e = res[:, b, 2 * q + a, D:W].unsqueeze(2).to_broadcast([P, HEADS, DH])
                        last = nc.vector.tensor_tensor(
                            res[:, b, 2 * q + a, 0:D].rearrange("p (h d) -> p h d", d=DH),
                            kv[:, a, 1, :].rearrange("p (h d) -> p h d", d=DH), e, ALU.mult)
                    last.then_inc(a_res.sem, 1)

                def round_(r):
                    own.begin(r)
                    next_indices(ATT, r)
                    same_keys(r)
                    next_slots(ATT, r)
                    sum_rows(r)
                    logits(r, 0)
                    logits(r, 1)
                    weighted(r, 0)
                    weighted(r, 1)
                    own.end()

                first_indices(ATT)
                run_steps(dve, [(round_, 0)], ROUNDS, 2, ahead=2, behind=2)
                own.close(ROUNDS)

            def node_phase(phase):
                rows = x2r if phase == SAGE1 else xr

                def arrived(g):
                    s = g.mod(SLOTS)
                    dve.wait_ge(loaded[s].sem, loaded[s].after(g.div(SLOTS), stores_before(phase, s)))
                    if phase == SAGE1:
                        dve.wait_ge(loaded2[s].sem, loaded2[s].after(g.div(SLOTS)))

                def moments(own, source, stats, mv):
                    for k in range(K):
                        last = nc.vector.bn_stats(stats[:, k, :], source(k))
                    own.mark(last)
                    own.wait()
                    gate(dve)
                    for k in range(K):
                        last = nc.vector.bn_aggr(mv[:, k, :], stats[:, k, :])
                    return last

                def scales(own, sd, mv, a, c):
                    own.mark(nc.vector.reciprocal(a, sd))
                    own.wait()
                    return nc.vector.scalar_tensor_tensor(out=c, in0=mv[:, :, 0], scalar=-1.0, in1=a,
                                                          op0=ALU.mult, op1=ALU.mult)

                def in_moments(g, own):
                    s = g.mod(SLOTS)
                    arrived(g)
                    moments(own, lambda k: xr[:, s, k, 0:D], in_stats, in_mv).then_inc(in_var.sem, 1)

                def in_scales(g, own):
                    s = g.mod(SLOTS)
                    dve.wait_ge(in_sd_ready.sem, in_sd_ready.after(g))
                    scales(own, in_sd[:, :], in_mv, xr[:, s, :, COL_A], xr[:, s, :, COL_C]).then_inc(in_scale.sem, 1)

                def product(g):
                    dve.wait_ge(n_y_ready.sem, n_y_ready.after(g, first(MATMUL, phase)))
                    return bank[2 + g.mod(2)][:, :].rearrange("p (k d) -> p k d", k=K)

                def out_moments(g, own):
                    moments(own, lambda k: rows[:, g.mod(SLOTS), k, 0:D], out_stats, out_mv).then_inc(out_var.sem, 1)

                def out_scales(g, own):
                    s = g.mod(SLOTS)
                    dve.wait_ge(out_sd_ready.sem, out_sd_ready.after(g, first(ROW_STATS, phase)))
                    if phase != SAGE1:
                        scales(own, out_sd[:, :], out_mv, rows[:, s, :, COL_A], rows[:, s, :, COL_C])\
                            .then_inc(row_ready.sem, 1)
                        return
                    own.mark(nc.vector.reciprocal(rstd[:, :], out_sd[:, :]))
                    own.wait()
                    own.mark(nc.vector.tensor_tensor(rows[:, s, :, COL_A], rstd[:, :], rows[:, s, :, COL_DIS], ALU.mult))
                    own.wait()
                    nc.vector.scalar_tensor_tensor(out=rows[:, s, :, COL_C], in0=out_mv[:, :, 0], scalar=-1.0,
                                                   in1=rows[:, s, :, COL_A], op0=ALU.mult, op1=ALU.mult)\
                        .then_inc(row_ready.sem, 1)

                def combine_rel(g, own):
                    s, b = g.mod(SLOTS), g.mod(2)
                    y = product(g)
                    own.mark(nc.vector.tensor_tensor(n_t[:, b, :, :], y, sr[:, s, :, 0:D], ALU.add))
                    own.wait()
                    own.mark(nc.vector.scalar_tensor_tensor(out=xr[:, s, :, 0:D], in0=n_t[:, b, :, :], scalar=0.0,
                                                            in1=xr[:, s, :, 0:D], op0=ALU.max, op1=ALU.add))
                    own.wait()
                    dve.sem_inc(n_y_used.sem, 1)
                    out_moments(g, own)

                def combine_att(g, own):
                    s, b = g.mod(SLOTS), g.mod(2)
                    arrived(g)
                    own.mark(nc.vector.tensor_scalar(den[:, :, :], sr[:, s, :, D:W], 1e-8, None, ALU.add))
                    own.wait()
                    own.mark(nc.vector.reciprocal(den[:, :, :], den[:, :, :]))
                    own.wait()
                    for k in range(K):
                        last = nc.vector.tensor_tensor(
                            n_t[:, b, k, :].rearrange("p (h d) -> p h d", d=DH),
                            sr[:, s, k, 0:D].rearrange("p (h d) -> p h d", d=DH),
                            den[:, k, :].unsqueeze(2).to_broadcast([P, HEADS, DH]), ALU.mult)
                    own.mark(last)
                    own.wait()
                    own.mark(nc.vector.tensor_tensor(xr[:, s, :, 0:D], n_t[:, b, :, :], xr[:, s, :, 0:D], ALU.add))
                    own.wait()
                    out_moments(g, own)

                def combine_mid(g, own):
                    s, b = g.mod(SLOTS), g.mod(2)
                    arrived(g)
                    y = product(g)
                    own.mark(nc.vector.tensor_scalar(per_edge[:, :], sr[:, s, :, COL_CNT], 1.0, None, ALU.max))
                    own.wait()
                    own.mark(nc.vector.reciprocal(per_edge[:, :], per_edge[:, :]))
                    own.wait()
                    for k in range(K):
                        last = nc.vector.scalar_tensor_tensor(out=n_t[:, b, k, :], in0=sr[:, s, k, 0:D],
                                                              scalar=per_edge[:, k:k + 1], in1=y[:, k, :],
                                                              op0=ALU.mult, op1=ALU.add)
                    own.mark(last)
                    own.wait()
                    dve.sem_inc(n_y_used.sem, 1)
                    moments(own, lambda k: n_t[:, b, k, :], mid_stats, mid_mv).then_inc(mid_var.sem, 1)

                def mid_scales(g, own):
                    b = g.mod(2)
                    dve.wait_ge(mid_sd_ready.sem, mid_sd_ready.after(g, first(MID_NORM, phase)))
                    if phase == SAGE1:
                        nc.vector.reciprocal(rows[:, g.mod(SLOTS), :, COL_DIS], root_deg[:, :])
                    scales(own, mid_sd[:, :], mid_mv, mid_ac[:, b, 0, :], mid_ac[:, b, 1, :]).then_inc(mid_scale.sem, 1)

                def finish_mid(g, own):
                    s, b = g.mod(SLOTS), g.mod(2)
                    dve.wait_ge(mid_ready.sem, mid_ready.after(g, first(MID_NORM, phase)))
                    gains = ln_g_bc[:, :].unsqueeze(1).to_broadcast([P, K, D])
                    shifts = ln_b_bc[:, :].unsqueeze(1).to_broadcast([P, K, D])
                    if phase == SAGE0:
                        nc.vector.memset(xr[:, s, :, COL_A], 1.0)
                        nc.vector.memset(xr[:, s, :, COL_C], 0.0)
                    own.mark(nc.vector.tensor_tensor(n_u[:, b, :, :], n_u[:, b, :, :], gains, ALU.mult))
                    own.wait()
                    if phase == SAGE0:
                        nc.vector.tensor_tensor(xr[:, s, :, 0:D], n_u[:, b, :, :], shifts, ALU.add)\
                            .then_inc(row_ready.sem, 1)
                        return
                    own.mark(nc.vector.tensor_tensor(n_u[:, b, :, :], n_u[:, b, :, :], shifts, ALU.add))
                    own.wait()
                    own.mark(nc.vector.tensor_tensor(x2r[:, s, :, 0:D], n_u[:, b, :, :], x2r[:, s, :, 0:D], ALU.add))
                    own.wait()
                    out_moments(g, own)

                def combine_gcn(g, own):
                    s, b = g.mod(SLOTS), g.mod(2)
                    y = product(g)
                    own.mark(nc.vector.tensor_tensor(n_t[:, b, :, :], y, sr[:, s, :, 0:D], ALU.add))
                    own.wait()
                    dve.sem_inc(n_y_used.sem, 1)
                    for k in range(K):
                        last = nc.vector.scalar_tensor_tensor(out=xr[:, s, k, 0:D], in0=n_t[:, b, k, :],
                                                              scalar=xr[:, s, k, COL_DIS:COL_DIS + 1],
                                                              in1=xr[:, s, k, 0:D], op0=ALU.mult, op1=ALU.add)
                    last.then_inc(row_ready.sem, 1)

                stages = {
                    REL: [(in_moments, 0, in_chain, 1), (combine_rel, 1, combine_chain, 3),
                          (in_scales, 0, in_scales_chain, 1), (out_scales, 1, out_scales_chain, 1)],
                    ATT: [(combine_att, 0, combine_chain, 5), (out_scales, 0, out_scales_chain, 1)],
                    SAGE0: [(combine_mid, 1, combine_chain, 4), (finish_mid, 2, finish_chain, 1),
                            (mid_scales, 1, mid_scales_chain, 1)],
                    SAGE1: [(combine_mid, 1, combine_chain, 4), (finish_mid, 2, finish_chain, 4),
                            (mid_scales, 1, mid_scales_chain, 1), (out_scales, 2, out_scales_chain, 2)],
                    GCN: [(combine_gcn, 1, combine_chain, 1)],
                }[phase]

                def counted(stage, chain, per):
                    chain.open(per)

                    def run(g):
                        chain.begin(g)
                        stage(g, chain)
                        chain.end()
                    return run

                run_steps(dve, [(counted(stage, chain, per), lag) for stage, lag, chain, per in stages], GROUPS, SLOTS)
                for _, _, chain, _ in stages:
                    chain.close(GROUPS)

            for phase in range(5):
                if phase == ATT:
                    att_phase()
                else:
                    seg_phase(phase)
                node_phase(phase)


_INS = ['x', 'src', 'dst', 'edge_type_8', 'L0_gnn_weight', 'L0_gnn_self_loop_weight', 'L0_gnn_bias',
        'L1_gnn_qW', 'L1_gnn_kW', 'L1_gnn_vW', 'L2_gnn_W_self0', 'L2_gnn_W_neigh0', 'L2_gnn_b0',
        'L2_gnn_W_self1', 'L2_gnn_W_neigh1', 'L2_gnn_b1', 'L2_gnn_ln_g', 'L2_gnn_ln_b', 'L3_gnn_W']


def kernel(**inputs):
    import numpy as _np
    import concourse.bacc as _bacc
    from concourse import mybir as _mybir
    from concourse.bass_utils import run_bass_kernel_spmd as _run

    nc = _bacc.Bacc("TRN2", target_bir_lowering=False, num_devices=1)
    arrays, args = {}, []
    for name in _INS:
        a = _np.ascontiguousarray(inputs[name])
        arrays[f"in_{name}_dram"] = a
        args.append(nc.dram_tensor(f"in_{name}_dram", a.shape, _mybir.dt.from_np(a.dtype), kind="ExternalInput").ap())
    args.append(nc.dram_tensor("out_0_dram", inputs['x'].shape, _mybir.dt.float32, kind="ExternalOutput").ap())
    gnn_stack_kernel(nc, *args)
    r = _run(nc, [arrays], core_ids=[0])
    return r.results[0]["out_0_dram"]
```

```python
import concourse.bass as bass
from concourse import mybir
from contextlib import ExitStack


class Step:

    def __init__(self, i, times, offset):
        self.i, self.times, self.offset = i, times, offset

    def scaled(self, m, plus=0):
        if self.i is None:
            return self.offset * m + plus
        return self.i * (self.times * m) + (self.offset * m + plus)

    def mod(self, m):
        return self.offset % m

    def div(self, m):
        if self.i is None:
            return Step(None, 1, self.offset // m)
        return Step(self.i, self.times // m, self.offset // m)


class Signal:

    def __init__(self, sem, per, credit=0):
        self.sem, self.per, self.credit = sem, per, credit

    def after(self, step, first=0, n=None):
        n = self.per if n is None else n
        return step.scaled(self.per, self.credit + first * self.per + n)

    def before(self, step, back, first=0):
        return step.scaled(self.per, self.credit + (first - back + 1) * self.per)


def wait_landed(eng, signal, value):
    if not isinstance(value, int) or value > 0:
        eng.wait_ge(signal.sem, value)


class Chain:

    def __init__(self, eng, sem):
        self.eng, self.sem, self.base, self.per = eng, sem, 0, 0

    def open(self, per):
        self.per = per

    def close(self, steps):
        self.base += self.per * steps

    def begin(self, step):
        self.step, self.k = step, 0

    def mark(self, ins):
        self.k += 1
        ins.then_inc(self.sem, 1)

    def wait(self):
        self.eng.wait_ge(self.sem, self.step.scaled(self.per, self.base + self.k))

    def end(self):
        assert self.k == self.per, (self.k, self.per)


def run_steps(eng, stages, total, unroll, ahead=0, behind=0):
    deepest = max(lag for _, lag in stages)
    low = -(-(deepest + behind) // unroll) * unroll
    high = (total - 1 - ahead) // unroll * unroll

    def turn(it, i=None):
        for stage, lag in stages:
            if i is not None:
                stage(Step(i, unroll, it - lag))
            elif 0 <= it - lag < total:
                stage(Step(None, 1, it - lag))

    for it in range(low):
        turn(it)
    with eng.Fori(low // unroll, high // unroll) as i:
        for u in range(unroll):
            turn(u, i)
    for it in range(high, total + deepest):
        turn(it)


def gnn_stack_kernel(nc, x, src, dst, edge_type, w_rel, w_loop, b_loop, w_q, w_k, w_v,
                     w_self0, w_neigh0, b0, w_self1, w_neigh1, b1, ln_g, ln_b, w_gcn, out):
    fp32 = mybir.dt.float32
    i32 = mybir.dt.int32
    bf16 = mybir.dt.bfloat16
    ALU = mybir.AluOpType
    ACT = mybir.ActivationFunctionType
    AX = mybir.AxisListType

    P = 128
    N, D = x.shape
    E = src.shape[0]
    NREL = w_rel.shape[0]
    HEADS = 4
    DH = D // HEADS
    EPS = 1e-5

    COL_A, COL_C, COL_DIS = D, D + 1, D + 2
    COL_CNT = D
    W = D + HEADS

    TPR = 4
    TILES = -(-E // P)
    ROUNDS = TILES // TPR
    assert TILES == ROUNDS * TPR and ROUNDS % 2 == 1
    FULL = E // P
    REST = E - FULL * P
    SPARE = 2 * P
    PAD = N + SPARE

    K = 4
    GROUP = K * P
    GROUPS = -(-N // GROUP)
    SLOTS = 6

    REL, ATT, SAGE0, SAGE1, GCN = range(5)
    SEG_PHASES = [REL, SAGE0, SAGE1, GCN]

    rows1 = nc.dram_tensor("rows1", (N, W), fp32, kind="Internal").ap()
    rows2 = nc.dram_tensor("rows2", (N, W), fp32, kind="Internal").ap()
    rowsg = nc.dram_tensor("rowsg", (N, W), fp32, kind="Internal").ap()
    rows3 = nc.dram_tensor("rows3", (N, W), fp32, kind="Internal").ap()
    sums = nc.dram_tensor("sums", (PAD + 1, W), fp32, kind="Internal").ap()
    attsums = nc.dram_tensor("attsums", (PAD + 1, W), fp32, kind="Internal").ap()

    ctx = ExitStack()
    with ctx:
        def sb(name, shape, dt=fp32):
            return ctx.enter_context(nc.sbuf_tensor(name, shape, dt))

        def sem(name):
            return ctx.enter_context(nc.semaphore(name))

        ident = sb("ident", [P, P])
        ident_bf = sb("ident_bf", [P, P], bf16)
        zeros = sb("zeros", [P, 5148])
        eps_col = sb("eps_col", [P, 1])
        ones_col = sb("ones_col", [P, 1])
        w_rel_sb = sb("w_rel_sb", [P, NREL, D])
        w_in = sb("w_in", [P, 4, D])
        w_t = sb("w_t", [P, 4, D])
        w_loop_sb = sb("w_loop_sb", [P, D])
        w_q_sb = sb("w_q_sb", [P, D])
        w_kv_sb = sb("w_kv_sb", [P, 2, D])
        w_gcn_sb = sb("w_gcn_sb", [P, D])
        BP = 3
        bias_f = sb("bias_f", [BP, 3, D])
        bias_part = sb("bias_part", [BP, 3, 3, D], bf16)
        bias_left = sb("bias_left", [BP, 2, 3, D])
        bias_sum = sb("bias_sum", [BP, 3, D])
        part_mask = sb("part_mask", [BP, BP])
        bias_bf = sb("bias_bf", [BP, 3, K, D], bf16)
        ones_bf = sb("ones_bf", [BP, P], bf16)
        ln_g_bc = sb("ln_g_bc", [P, D])
        ln_b_bc = sb("ln_b_bc", [P, D])
        key_rows = sb("key_rows", [P, 4, 2, P], i32)
        key_rows_f = sb("key_rows_f", [P, 4, 2, P])
        src_f = sb("src_f", [P, TILES])
        dst_f = sb("dst_f", [P, TILES])
        next_f = sb("next_f", [P, TILES])
        type_f = sb("type_f", [P, TILES])
        low_i = sb("low_i", [P, 2, TILES], i32)
        src_parts = sb("src_parts", [P, 2, TILES], bf16)
        dst_parts = sb("dst_parts", [P, 3, TILES], bf16)
        seg_keys = sb("seg_keys", [P, TILES, 2])
        src_i = sb("src_i", [P, TILES], i32)
        dst_i = sb("dst_i", [P, TILES], i32)
        last_i = sb("last_i", [P, TILES], i32)
        spare_f = sb("spare_f", [P, TPR])
        earlier = sb("earlier", [P, 2, 2 * P])
        gidx = sb("gidx", [P, 2, TPR], i32)
        didx = sb("didx", [P, 2, TPR], i32)
        sidx = sb("sidx", [P, 2, TPR], i32)
        slot_keys = sb("slot_keys", [P, 2, 3, TPR], bf16)
        got = sb("got", [P, 2, TPR, W])
        got_d = sb("got_d", [P, 2, TPR, W])
        e_stats = sb("e_stats", [P, TPR, 6])
        e_mv = sb("e_mv", [P, TPR, 2])
        e_sd = sb("e_sd", [P, TPR])
        e_h = sb("e_h", [P, 2, TPR, D])
        e_ht = sb("e_ht", [P, 2, TPR * P])
        e_htm = sb("e_htm", [P, 2, NREL, P])
        eq = sb("eq", [P, 2, TPR, 2, P])
        msg = sb("msg", [P, 2, TPR, W])
        res = sb("res", [P, 2, TPR, W])
        psum_out = sb("psum_out", [P, 2, TPR, W])
        q_sb = sb("q_sb", [P, 2, 2, D])
        qk = sb("qk", [P, 2, D])
        att_raw = sb("att_raw", [P, 2, 2 * HEADS])
        dup_out = sb("dup_out", [P, TPR, 2 * P])
        att_sum = sb("att_sum", [P, 2 * HEADS])
        dup = sb("dup", [P, TPR])
        sp_a = sb("sp_a", [P, TPR])
        sp_b = sb("sp_b", [P, TPR])
        xr = sb("xr", [P, SLOTS, K, W])
        sr = sb("sr", [P, SLOTS, K, W])
        x2r = sb("x2r", [P, SLOTS, K, W])
        in_stats = sb("in_stats", [P, 2, K, 6])
        in_mv = sb("in_mv", [P, 2, K, 2])
        in_sd = sb("in_sd", [P, 2, K])
        mid_stats = sb("mid_stats", [P, 2, K, 6])
        mid_mv = sb("mid_mv", [P, 2, K, 2])
        mid_sd = sb("mid_sd", [P, 2, K])
        mid_ac = sb("mid_ac", [P, 2, 2, K])
        root_deg = sb("root_deg", [P, 2, K])
        out_stats = sb("out_stats", [P, 2, K, 6])
        out_mv = sb("out_mv", [P, 2, K, 2])
        out_sd = sb("out_sd", [P, 2, K])
        per_edge = sb("per_edge", [P, K])
        rstd = sb("rstd", [P, K])
        den = sb("den", [P, K, HEADS])
        n_h = sb("n_h", [P, 2, K, D])
        n_ht = sb("n_ht", [P, 2, K * P])
        n_t = sb("n_t", [P, 2, K, D])
        n_u = sb("n_u", [P, 2, K, D])

        bank = [ctx.enter_context(nc.psum_tensor(f"bank{i}", [P, 512], fp32)) for i in range(8)]
        kv_bank = [bank[3], bank[6]]

        s_const = sem("s_const")
        s_pads = sem("s_pads")
        s_weights = sem("s_weights")
        s_keys = sem("s_keys")
        s_keysf = sem("s_keysf")
        s_keyst = sem("s_keyst")
        s_keysc = sem("s_keysc")
        s_prep = sem("s_prep")
        s_setup = sem("s_setup")
        s_wt = sem("s_wt")
        s_zero_sums = sem("s_zero_sums")
        s_zero_att = sem("s_zero_att")
        s_gate = sem("s_gate")

        gidx_ready = Signal(sem("gidx_ready"), 1)
        slots_ready = Signal(sem("slots_ready"), 1)
        sidx_ready = Signal(sem("sidx_ready"), 1)
        gathered = [Signal(sem(f"gathered{b}"), 16 * TPR) for b in range(2)]
        gathered_d = [Signal(sem(f"gathered_d{b}"), 16 * TPR) for b in range(2)]
        e_var_ready = Signal(sem("e_var_ready"), 1)
        e_sd_ready = Signal(sem("e_sd_ready"), 1)
        e_scale_ready = Signal(sem("e_scale_ready"), 1)
        h_ready = Signal(sem("h_ready"), 1, 2)
        turned = Signal(sem("turned"), 1, 2)
        ht_ready = Signal(sem("ht_ready"), 1, 2)
        htm_ready = Signal(sem("htm_ready"), TPR, 2 * TPR)
        y_ready = Signal(sem("y_ready"), TPR, 2 * TPR)
        keys_spread = Signal(sem("keys_spread"), 1)
        eq_ready = Signal(sem("eq_ready"), 1, 2)
        msg_ready = Signal(sem("msg_ready"), 1, 2)
        seg_done = Signal(sem("seg_done"), TPR, 2 * TPR)
        seg_out = Signal(sem("seg_out"), TPR, 2 * TPR)
        scattered = [Signal(sem(f"scattered{b}"), 16 * TPR) for b in range(2)]
        a_h = Signal(sem("a_h"), 2, 4)
        a_turned = Signal(sem("a_turned"), 2, 4)
        a_ht = Signal(sem("a_ht"), 2, 4)
        a_qkv = Signal(sem("a_qkv"), 2, 4)
        a_q = Signal(sem("a_q"), 2, 4)
        a_logit = Signal(sem("a_logit"), 2, 4)
        a_exp = Signal(sem("a_exp"), 2, 4)
        a_res = Signal(sem("a_res"), 2, 4)
        a_sum = Signal(sem("a_sum"), 4, 8)
        a_out = Signal(sem("a_out"), 4, 8)
        a_eq = Signal(sem("a_eq"), 1, 2)
        a_spread = Signal(sem("a_spread"), 1)
        a_acc = Signal(sem("a_acc"), 64)
        credited = [h_ready, turned, ht_ready, htm_ready, y_ready, eq_ready, msg_ready, seg_done, seg_out,
                    a_h, a_turned, a_ht, a_qkv, a_q, a_logit, a_exp, a_res, a_sum, a_out, a_eq]
        loaded = [Signal(sem(f"loaded{s}"), 32) for s in range(SLOTS)]
        loaded2 = [Signal(sem(f"loaded2_{s}"), 16) for s in range(SLOTS)]
        stored = [Signal(sem(f"stored{s}"), 16) for s in range(SLOTS)]
        in_var = Signal(sem("in_var"), 1)
        in_sd_ready = Signal(sem("in_sd_ready"), 1)
        in_scale = Signal(sem("in_scale"), 1)
        out_var = Signal(sem("out_var"), 1)
        out_sd_ready = Signal(sem("out_sd_ready"), 1)
        n_h_ready = Signal(sem("n_h_ready"), 1, 2)
        n_turned = Signal(sem("n_turned"), 1, 2)
        n_ht_ready = Signal(sem("n_ht_ready"), 1, 2)
        n_y_ready = Signal(sem("n_y_ready"), 1, 2)
        n_y_used = Signal(sem("n_y_used"), 1, 2)
        mid_var = Signal(sem("mid_var"), 1)
        mid_sd_ready = Signal(sem("mid_sd_ready"), 1)
        mid_scale = Signal(sem("mid_scale"), 1, 2)
        mid_ready = Signal(sem("mid_ready"), 1)
        scaled_ready = Signal(sem("scaled_ready"), 1)
        affine_ready = Signal(sem("affine_ready"), 1)
        n_u_used = Signal(sem("n_u_used"), 1, 2)
        row_ready = Signal(sem("row_ready"), 1, 2)
        credited += [n_h_ready, n_turned, n_ht_ready, n_y_ready, n_y_used, mid_scale, n_u_used, row_ready]
        dve_edge = sem("dve_edge")
        dve_scales = sem("dve_scales")
        dve_in = sem("dve_in")
        dve_in_scales = sem("dve_in_scales")
        dve_combine = sem("dve_combine")
        dve_mid_scales = sem("dve_mid_scales")
        dve_finish = sem("dve_finish")
        dve_out_scales = sem("dve_out_scales")
        dve_setup = sem("dve_setup")

        block = ctx.enter_context(nc.Block())

        def gate(eng):
            eng.sem_inc(s_gate, 1)

        def parity_first(phase, b):
            return phase * (ROUNDS // 2 + 1 - b)

        def seg_index(phase):
            return SEG_PHASES.index(phase)

        def stores_before(phase, s):
            return phase * (GROUPS // SLOTS + (1 if s < GROUPS % SLOTS else 0))

        MATMUL = [REL, SAGE0, SAGE1, GCN]
        MID_NORM = [SAGE0, SAGE1]
        ROW_STATS = [REL, ATT, SAGE1]

        def first(phases, phase):
            return phases.index(phase) * GROUPS

        node_in = {REL: x, ATT: rows1, SAGE0: rows2, SAGE1: rowsg, GCN: rows3}
        node_sum = {REL: sums, ATT: attsums, SAGE0: sums, SAGE1: sums, GCN: sums}
        node_out = {REL: rows1, ATT: rows2, SAGE0: rowsg, SAGE1: rows3, GCN: out}
        node_w = {REL: w_loop_sb[:, :], SAGE0: w_t[:, 0, :], SAGE1: w_t[:, 2, :], GCN: w_gcn_sb[:, :]}
        edge_w = {SAGE0: w_t[:, 1, :], SAGE1: w_t[:, 3, :], GCN: w_gcn_sb[:, :]}
        edge_in = {REL: x, ATT: rows1, SAGE0: rows2, SAGE1: rowsg, GCN: rows3}

        ZROWS = zeros.shape[1] // W
        ZPARTS = N // P // ZROWS
        assert ZPARTS * ZROWS * P <= N
        ZERO_DMAS = ZPARTS + 1
        ZLEFT = PAD + 1 - ZPARTS * ZROWS * P
        ZLEFT_A = ZLEFT // P * P
        ZERO_COUNT = ZPARTS + (1 if ZLEFT_A else 0) + (1 if ZLEFT - ZLEFT_A else 0)

        @block.sync
        def _(sp):
            for sig in credited:
                sp.sem_inc(sig.sem, sig.credit)
            sp.wait_ge(s_pads, 1)
            for n, (keys, shift) in enumerate([(src, 0), (dst, 0), (dst, 1), (edge_type, 0)]):
                sp.dma_start(key_rows[:, n, 0, :], keys[shift:shift + P * P].rearrange("(t p) -> t p", p=P))\
                    .then_inc(s_keys, 16)
                full = (E - shift) // P
                sp.dma_start(key_rows[0:full - P, n, 1, :],
                             keys[shift + P * P:shift + full * P].rearrange("(t p) -> t p", p=P)).then_inc(s_keys, 16)
                left = E - shift - full * P
                sp.dma_start(key_rows[full - P:full - P + 1, n, 1, 0:left],
                             keys[shift + full * P:E].rearrange("(t p) -> t p", t=1)).then_inc(s_keys, 16)
            sp.wait_ge(s_const, 1)
            for table, s_zero in ((sums, s_zero_sums), (attsums, s_zero_att)):
                at = 0
                for _z in range(ZPARTS):
                    sp.dma_start(table[at:at + ZROWS * P, :].rearrange("(p r) c -> p (r c)", p=P), zeros[:, :])\
                        .then_inc(s_zero, 16)
                    at += ZROWS * P
                if ZLEFT_A:
                    sp.dma_start(table[at:at + ZLEFT_A, :].rearrange("(p r) c -> p (r c)", p=P),
                                 zeros[:, 0:ZLEFT_A // P * W]).then_inc(s_zero, 16)
                    at += ZLEFT_A
                if ZLEFT - ZLEFT_A:
                    sp.dma_start(table[at:PAD + 1, :], zeros[0:ZLEFT - ZLEFT_A, 0:W]).then_inc(s_zero, 16)

            for phase in range(5):
                if phase == ATT:
                    sp.wait_ge(a_acc.sem, ROUNDS * 64)
                else:
                    for b in range(2):
                        sp.wait_ge(scattered[b].sem, parity_first(seg_index(phase) + 1, b) * 16 * TPR)
                if phase > 0:
                    for s in range(SLOTS):
                        sp.wait_ge(stored[s].sem, 16 * stores_before(phase, s))

                def span(g):
                    if g.i is None and g.offset == GROUPS - 1:
                        return slice(N - GROUP, N)
                    return bass.ds(g.scaled(GROUP), GROUP)

                def load(g):
                    s = g.mod(SLOTS)
                    v = g.div(SLOTS)
                    wait_landed(sp, stored[s], stored[s].before(v, 1, stores_before(phase, s)))
                    table = node_in[phase]
                    width = table.shape[1]
                    sp.dma_start(xr[:, s, :, 0:width], table[span(g), :].rearrange("(p k) c -> p k c", k=K))\
                        .then_inc(loaded[s].sem, 16)
                    sp.dma_start(sr[:, s, :, :], node_sum[phase][span(g), :].rearrange("(p k) c -> p k c", k=K))\
                        .then_inc(loaded[s].sem, 16)
                    if phase == SAGE1:
                        sp.dma_start(x2r[:, s, :, :], rows2[span(g), :].rearrange("(p k) c -> p k c", k=K))\
                            .then_inc(loaded2[s].sem, 16)

                def store(g):
                    s = g.mod(SLOTS)
                    sp.wait_ge(row_ready.sem, row_ready.after(g, phase * GROUPS))
                    if g.i is None and g.offset == GROUPS - 1:
                        o = (GROUPS - 2) % SLOTS
                        sp.wait_ge(stored[o].sem, 16 * (stores_before(phase, o) + (GROUPS - 2) // SLOTS + 1))
                    table = node_out[phase]
                    ring = x2r if phase == SAGE1 else xr
                    sp.dma_start(table[span(g), :].rearrange("(p k) c -> p k c", k=K),
                                 ring[:, s, :, 0:table.shape[1]]).then_inc(stored[s].sem, 16)

                run_steps(sp, [(load, 0), (store, 4)], GROUPS, SLOTS, behind=SLOTS)
            for s in range(SLOTS):
                sp.wait_ge(stored[s].sem, 16 * stores_before(5, s))

        @block.gpsimd
        def _(pool):
            nc.gpsimd.memset(key_rows[:, :, :, :], PAD).then_inc(s_pads, 1)
            nc.gpsimd.memset(zeros[:, :], 0.0).then_inc(s_const, 1)
            nc.gpsimd.memset(ident[:, :], 0.0).then_inc(s_const, 1)
            nc.gpsimd.memset(ones_bf[:, :], 1.0).then_inc(s_const, 1)
            nc.gpsimd.memset(part_mask[:, :], 0.0).then_inc(s_const, 1)
            nc.gpsimd.memset(ones_col[:, :], 1.0).then_inc(s_const, 1)
            nc.gpsimd.memset(eps_col[:, :], EPS).then_inc(s_const, 1)
            nc.gpsimd.memset(msg[:, :, :, :], 0.0).then_inc(s_const, 1)
            nc.gpsimd.memset(psum_out[:, :, :, :], 0.0).then_inc(s_const, 1)
            nc.gpsimd.memset(earlier[:, :, :], 1.0).then_inc(s_const, 1)
            nc.gpsimd.memset(seg_keys[:, :, :], -1.0).then_inc(s_const, 1)
            nc.gpsimd.memset(res[:, :, :, :], 0.0).then_inc(s_const, 1)
            nc.gpsimd.memset(got[:, :, :, :], 0.0).then_inc(s_const, 1)
            nc.gpsimd.memset(got_d[:, :, :, :], 0.0).then_inc(s_const, 1)
            nc.gpsimd.memset(xr[:, :, :, :], 0.0).then_inc(s_const, 1)
            nc.gpsimd.memset(x2r[:, :, :, :], 0.0).then_inc(s_const, 1)
            nc.gpsimd.iota(spare_f[:, :].rearrange("p (q a) -> p q a", a=2), pattern=[[0, 2], [P, 2]], base=N,
                           channel_multiplier=1, allow_small_or_imprecise_dtypes=True).then_inc(s_const, 1)
            pool.wait_ge(s_const, 16)
            nc.gpsimd.affine_select(out=ident[:, :], in_=ident[:, :], compare_op=ALU.not_equal, fill=1.0,
                                    base=0, pattern=[[-1, P]], channel_multiplier=1).then_inc(s_const, 1)
            nc.gpsimd.affine_select(out=part_mask[:, :], in_=part_mask[:, :], compare_op=ALU.not_equal, fill=1.0,
                                    base=0, pattern=[[-1, BP]], channel_multiplier=1).then_inc(s_const, 1)
            nc.gpsimd.affine_select(out=earlier[:, :, :], in_=earlier[:, :, :], compare_op=ALU.is_gt, fill=0.0,
                                    base=0, pattern=[[P, 2], [-1, 2 * P]], channel_multiplier=1).then_inc(s_const, 1)
            nc.gpsimd.memset(msg[:, :, :, COL_CNT:COL_CNT + 1], 1.0).then_inc(s_const, 1)
            pool.wait_ge(s_keysc, 1)
            nc.gpsimd.affine_select(out=seg_keys[:, 1:TILES, 1], in_=dst_f[:, 0:TILES - 1], compare_op=ALU.is_ge,
                                    fill=-1.0, base=-(P - 1), pattern=[[0, TILES - 1]], channel_multiplier=1)\
                .then_inc(s_setup, 1)
            bound = pool.to_reg(N - 1)
            top = pool.to_reg(PAD)

            for phase in range(5):
                if phase > 0:
                    for s in range(SLOTS):
                        pool.wait_ge(stored[s].sem, 16 * stores_before(phase, s))
                table = edge_in[phase]
                width = table.shape[1]

                def gather(r, tiles=range(TPR)):
                    b = r.mod(2)
                    if tiles[0] == 0:
                        pool.wait_ge(gidx_ready.sem, gidx_ready.after(r, phase * ROUNDS))
                        if phase == ATT:
                            pool.wait_ge(a_h.sem, a_h.before(r, 2))
                        else:
                            pool.wait_ge(h_ready.sem, h_ready.before(r, 2, seg_index(phase) * ROUNDS))
                        gate(pool)
                    for j in tiles:
                        pool.indirect_dma_start(
                            out=got[:, b, j, 0:width], out_offset=None, in_=table[:, :],
                            in_offset=bass.IndirectOffsetOnAxis(ap=gidx[:, b, j:j + 1], axis=0),
                            bounds_check=bound, oob_is_err=False).then_inc(gathered[b].sem, 16)
                        if phase == ATT:
                            pool.indirect_dma_start(
                                out=got_d[:, b, j, :], out_offset=None, in_=table[:, :],
                                in_offset=bass.IndirectOffsetOnAxis(ap=didx[:, b, j:j + 1], axis=0),
                                bounds_check=bound, oob_is_err=False).then_inc(gathered_d[b].sem, 16)

                    if phase == REL and r.i is None and r.offset == 1:
                        pool.wait_ge(s_zero_sums, 16 * ZERO_COUNT)

                def scatter(r):
                    b = r.mod(2)
                    seg = seg_index(phase)
                    pool.wait_ge(sidx_ready.sem, sidx_ready.after(r, phase * ROUNDS))
                    for j in range(TPR):
                        pool.wait_ge(seg_out.sem, seg_out.after(r, seg * ROUNDS, j + 1))
                        gate(pool)
                        pool.indirect_dma_start(
                            out=sums[:, :], out_offset=bass.IndirectOffsetOnAxis(ap=sidx[:, b, j:j + 1], axis=0),
                            in_=psum_out[:, b, j, :], in_offset=None,
                            bounds_check=bound, oob_is_err=False).then_inc(scattered[b].sem, 16)

                def add_pair(r, q):
                    b = r.mod(2)
                    if q == 0:
                        pool.wait_ge(sidx_ready.sem, sidx_ready.after(r, phase * ROUNDS))
                    pool.wait_ge(a_out.sem, a_out.after(r, 0, 2 * q + 2))
                    wait_landed(pool, a_acc, a_acc.after(r, 0, 32 * q))
                    gate(pool)
                    for j in (2 * q, 2 * q + 1):
                        pool.indirect_dma_start(
                            out=attsums[:, :], out_offset=bass.IndirectOffsetOnAxis(ap=sidx[:, b, j:j + 1], axis=0),
                            in_=psum_out[:, b, j, :], in_offset=None, bounds_check=top, oob_is_err=True,
                            compute_op=ALU.add).then_inc(a_acc.sem, 16)

                if phase == ATT:
                    pool.wait_ge(s_zero_att, 16 * ZERO_COUNT)
                    run_steps(pool, [(lambda r: gather(r, range(0, 2)), 0), (lambda r: add_pair(r, 0), 2),
                                     (lambda r: gather(r, range(2, 4)), 0), (lambda r: add_pair(r, 1), 2)],
                              ROUNDS, 2, behind=2)
                else:
                    run_steps(pool, [(gather, 0), (scatter, 3)], ROUNDS, 2)

                if phase not in MID_NORM:
                    continue
                gains = ln_g_bc[:, :].unsqueeze(1).to_broadcast([P, K, D])
                shifts = ln_b_bc[:, :].unsqueeze(1).to_broadcast([P, K, D])
                pool.wait_ge(s_weights, 16 * 15)

                def scale_and_shift(g):
                    s, b = g.mod(SLOTS), g.mod(2)
                    pool.wait_ge(mid_ready.sem, mid_ready.after(g, first(MID_NORM, phase)))
                    gate(pool)
                    nc.gpsimd.tensor_tensor(n_u[:, b, :, :], n_u[:, b, :, :], gains, ALU.mult)\
                        .then_inc(scaled_ready.sem, 1)
                    if phase == SAGE0:
                        nc.gpsimd.memset(xr[:, s, :, COL_A], 1.0)
                        nc.gpsimd.memset(xr[:, s, :, COL_C], 0.0)
                    pool.wait_ge(scaled_ready.sem, scaled_ready.after(g, first(MID_NORM, phase)))
                    if phase == SAGE0:
                        nc.gpsimd.tensor_tensor(xr[:, s, :, 0:D], n_u[:, b, :, :], shifts, ALU.add)\
                            .then_inc(row_ready.sem, 1)
                    else:
                        nc.gpsimd.tensor_tensor(n_u[:, b, :, :], n_u[:, b, :, :], shifts, ALU.add)\
                            .then_inc(affine_ready.sem, 1)

                run_steps(pool, [(scale_and_shift, 0)], GROUPS, SLOTS)

        @block.scalar
        def _(act):
            act.dma_start(w_rel_sb[:, :, :], w_rel.rearrange("r d o -> d r o")).then_inc(s_weights, 16)
            act.dma_start(w_loop_sb[:, :], w_loop).then_inc(s_weights, 16)
            for n, w in enumerate((w_self0, w_neigh0, w_self1, w_neigh1)):
                act.dma_start(w_in[:, n, :], w).then_inc(s_weights, 16)
            act.dma_start(w_q_sb[:, :], w_q).then_inc(s_weights, 16)
            act.dma_start(w_kv_sb[:, 0, :], w_k).then_inc(s_weights, 16)
            act.dma_start(w_kv_sb[:, 1, :], w_v).then_inc(s_weights, 16)
            act.dma_start(w_gcn_sb[:, :], w_gcn).then_inc(s_weights, 16)
            for n, v in enumerate((b_loop, b0, b1)):
                act.dma_start(bias_f[:, n, :], v.rearrange("(a n) -> a n", a=1).to_broadcast([BP, D]))\
                    .then_inc(s_weights, 16)
            act.dma_start(ln_g_bc[:, :], ln_g.rearrange("(a n) -> a n", a=1).to_broadcast([P, D])).then_inc(s_weights, 16)
            act.dma_start(ln_b_bc[:, :], ln_b.rearrange("(a n) -> a n", a=1).to_broadcast([P, D])).then_inc(s_weights, 16)
            act.wait_ge(s_const, 20)

            def seg_phase(phase):
                first_r = seg_index(phase) * ROUNDS

                def root(r):
                    if phase != REL:
                        return
                    act.wait_ge(e_var_ready.sem, e_var_ready.after(r))
                    nc.scalar.activation(e_sd[:, :], e_mv[:, :, 1], ACT.Sqrt, bias=eps_col[:, 0:1])\
                        .then_inc(e_sd_ready.sem, 1)

                def normalise(r, j):
                    b = r.mod(2)
                    if j == 0:
                        if phase == REL:
                            act.wait_ge(e_scale_ready.sem, e_scale_ready.after(r))
                        act.wait_ge(gathered[b].sem, gathered[b].after(r.div(2), parity_first(phase, b)))
                        act.wait_ge(turned.sem, turned.before(r, 2, first_r))
                    last = nc.scalar.activation(e_h[:, b, j, :], got[:, b, j, 0:D], ACT.Relu,
                                                bias=got[:, b, j, COL_C:COL_C + 1],
                                                scale=got[:, b, j, COL_A:COL_A + 1])
                    if j == TPR - 1:
                        last.then_inc(h_ready.sem, 1)

                def take_turned(r):
                    b = r.mod(2)
                    act.wait_ge(turned.sem, turned.after(r, first_r))
                    act.wait_ge(y_ready.sem, y_ready.before(r, 2, first_r))
                    nc.scalar.activation(e_ht[:, b, :], bank[0][:, :], ACT.Copy).then_inc(ht_ready.sem, 1)

                def take_messages(r):
                    b = r.mod(2)
                    act.wait_ge(y_ready.sem, y_ready.after(r, first_r))
                    act.wait_ge(seg_done.sem, seg_done.before(r, 2, first_r))
                    nc.scalar.activation(msg[:, b, :, 0:D], bank[1][:, :].rearrange("p (j d) -> p j d", j=TPR),
                                         ACT.Copy).then_inc(msg_ready.sem, 1)

                def take_sums(r, j):
                    b = r.mod(2)
                    if j == 0:
                        wait_landed(act, scattered[b], scattered[b].before(r.div(2), 1, parity_first(seg_index(phase), b)))
                    act.wait_ge(seg_done.sem, seg_done.after(r, first_r, j + 1))
                    nc.scalar.activation(psum_out[:, b, j, :], bank[4 + j % 2][:, 0:W], ACT.Copy)\
                        .then_inc(seg_out.sem, 1)

                stages = [(take_turned, 2), (root, 1)]
                for j in range(TPR):
                    stages += [(lambda r, j=j: take_sums(r, j), 3), (lambda r, j=j: normalise(r, j), 1)]
                run_steps(act, stages + [(take_messages, 2)], ROUNDS, 2, behind=2)

            def att_phase():
                def normalise(r, q):
                    b = r.mod(2)
                    if q == 0:
                        act.wait_ge(gathered[b].sem, gathered[b].after(r.div(2), parity_first(ATT, b)))
                        act.wait_ge(gathered_d[b].sem, gathered_d[b].after(r.div(2)))
                    act.wait_ge(a_turned.sem, a_turned.after(r, 0, 2 * 0 + q + 1 - 2))
                    for a in range(2):
                        for n, rows in enumerate((got, got_d)):
                            last = nc.scalar.activation(e_h[:, q, 2 * n + a, :], rows[:, b, 2 * q + a, 0:D], ACT.Relu,
                                                        bias=rows[:, b, 2 * q + a, COL_C:COL_C + 1],
                                                        scale=rows[:, b, 2 * q + a, COL_A:COL_A + 1])
                    last.then_inc(a_h.sem, 1)

                def take_turned(r, q):
                    act.wait_ge(a_turned.sem, a_turned.after(r, 0, q + 1))
                    act.wait_ge(a_qkv.sem, a_qkv.after(r, 0, q + 1 - 2))
                    nc.scalar.activation(e_ht[:, q, :], bank[0][:, :], ACT.Copy).then_inc(a_ht.sem, 1)

                def take_q(r, q):
                    act.wait_ge(a_qkv.sem, a_qkv.after(r, 0, q + 1))
                    act.wait_ge(a_logit.sem, a_logit.after(r, 0, q + 1 - 2))
                    nc.scalar.activation(q_sb[:, q, :, :], bank[1 + q][:, 0:2 * P], ACT.Copy)\
                        .then_inc(a_q.sem, 1)

                def exponentials(r, q):
                    act.wait_ge(a_logit.sem, a_logit.after(r, 0, q + 1))
                    b = r.mod(2)
                    act.wait_ge(a_sum.sem, a_sum.before(r, 2))
                    nc.scalar.activation(res[:, b, 2 * q:2 * q + 2, D:W],
                                         att_raw[:, q, :].rearrange("p (a h) -> p a h", a=2), ACT.Exp)\
                        .then_inc(a_exp.sem, 1)

                def take_sums(r, q):
                    b = r.mod(2)
                    wait_landed(act, a_acc, a_acc.before(r, 2))
                    for a in range(2):
                        j = 2 * q + a
                        act.wait_ge(a_sum.sem, a_sum.after(r, 0, j + 1))
                        nc.scalar.activation(psum_out[:, b, j, :], bank[4 + a][:, 0:W], ACT.Copy)\
                            .then_inc(a_out.sem, 1)

                def last_sums(r):
                    take_sums(r, 0)
                    take_sums(r, 1)

                def pairs(r):
                    normalise(r, 0)
                    take_turned(r, 0)
                    normalise(r, 1)
                    take_q(r, 0)
                    take_turned(r, 1)
                    exponentials(r, 0)
                    take_q(r, 1)
                    exponentials(r, 1)

                run_steps(act, [(last_sums, 1), (pairs, 0)], ROUNDS, 2, behind=2)

            def node_phase(phase):
                def in_root(g):
                    act.wait_ge(in_var.sem, in_var.after(g))
                    nc.scalar.activation(in_sd[:, g.mod(2), :], in_mv[:, g.mod(2), :, 1], ACT.Sqrt, bias=eps_col[:, 0:1])\
                        .then_inc(in_sd_ready.sem, 1)

                def normalise(g):
                    s, b = g.mod(SLOTS), g.mod(2)
                    mm = first(MATMUL, phase)
                    act.wait_ge(loaded[s].sem, loaded[s].after(g.div(SLOTS), stores_before(phase, s)))
                    if phase == REL:
                        act.wait_ge(in_scale.sem, in_scale.after(g))
                    act.wait_ge(n_turned.sem, n_turned.before(g, 2, mm))
                    for k in range(K):
                        last = nc.scalar.activation(n_h[:, b, k, :], xr[:, s, k, 0:D], ACT.Relu,
                                                    bias=xr[:, s, k, COL_C:COL_C + 1],
                                                    scale=xr[:, s, k, COL_A:COL_A + 1])
                    last.then_inc(n_h_ready.sem, 1)

                def take_turned(g):
                    b = g.mod(2)
                    mm = first(MATMUL, phase)
                    act.wait_ge(n_turned.sem, n_turned.after(g, mm))
                    act.wait_ge(n_y_ready.sem, n_y_ready.before(g, 2, mm))
                    nc.scalar.activation(n_ht[:, b, :], bank[b][:, :], ACT.Copy).then_inc(n_ht_ready.sem, 1)

                def mid_root(g):
                    act.wait_ge(mid_var.sem, mid_var.after(g, first(MID_NORM, phase)))
                    if phase == SAGE1:
                        nc.scalar.activation(root_deg[:, g.mod(2), :], sr[:, g.mod(SLOTS), :, COL_CNT], ACT.Sqrt,
                                             bias=ones_col[:, 0:1])
                    nc.scalar.activation(mid_sd[:, g.mod(2), :], mid_mv[:, g.mod(2), :, 1], ACT.Sqrt, bias=eps_col[:, 0:1])\
                        .then_inc(mid_sd_ready.sem, 1)

                def mid_normalise(g):
                    b = g.mod(2)
                    act.wait_ge(mid_scale.sem, mid_scale.after(g, first(MID_NORM, phase)))
                    if phase == SAGE0:
                        act.wait_ge(row_ready.sem, row_ready.before(g, 2, phase * GROUPS))
                    else:
                        act.wait_ge(n_u_used.sem, n_u_used.before(g, 2))
                    for k in range(K):
                        last = nc.scalar.activation(n_u[:, b, k, :], n_t[:, b, k, :], ACT.Identity,
                                                    bias=mid_ac[:, b, 1, k:k + 1], scale=mid_ac[:, b, 0, k:k + 1])
                    last.then_inc(mid_ready.sem, 1)

                def out_root(g):
                    act.wait_ge(out_var.sem, out_var.after(g, first(ROW_STATS, phase)))
                    nc.scalar.activation(out_sd[:, g.mod(2), :], out_mv[:, g.mod(2), :, 1], ACT.Sqrt, bias=eps_col[:, 0:1])\
                        .then_inc(out_sd_ready.sem, 1)

                stages = {
                    REL: [(take_turned, 1), (in_root, 0), (out_root, 2), (normalise, 0)],
                    ATT: [(out_root, 0)],
                    SAGE0: [(take_turned, 1), (mid_root, 2), (normalise, 0), (mid_normalise, 2)],
                    SAGE1: [(take_turned, 1), (mid_root, 2), (normalise, 0), (out_root, 3), (mid_normalise, 2)],
                    GCN: [(take_turned, 1), (normalise, 0)],
                }[phase]
                run_steps(act, stages, GROUPS, SLOTS)

            for phase in range(5):
                if phase == ATT:
                    att_phase()
                else:
                    seg_phase(phase)
                node_phase(phase)

        @block.tensor
        def _(pe):
            pe.wait_ge(s_const, 20)
            pe.wait_ge(s_keysf, 1)
            for n in range(4):
                for half in range(2):
                    at = (2 * n + half) * P
                    last = nc.tensor.transpose(bank[at // 512][:, at % 512:at % 512 + P],
                                               key_rows_f[:, n, half, :], ident[:, :])
            last.then_inc(s_keyst, 1)
            pe.wait_ge(s_weights, 16 * 15)
            for n in range(4):
                last = nc.tensor.transpose(bank[2][:, n * P:(n + 1) * P], w_in[:, n, :], ident[:, :])
            last.then_inc(s_wt, 1)
            pe.wait_ge(s_prep, 1)

            def spread(n, r, j, out_ps):
                for m in n:
                    last = nc.tensor.matmul(out_ps, lhsT=slot_keys[:, r.mod(2), m, j:j + 1].to_broadcast([P, P]),
                                            rhs=ident_bf[:, :], start=(m == n[0]), stop=(m == n[-1]))
                return last

            def seg_phase(phase):
                f = seg_index(phase) * ROUNDS

                def spread_keys(r):
                    pe.wait_ge(slots_ready.sem, slots_ready.after(r, phase * ROUNDS))
                    pe.wait_ge(eq_ready.sem, eq_ready.before(r, 1, f))
                    if phase == REL:
                        pe.wait_ge(htm_ready.sem, htm_ready.before(r, 1))
                    for j in range(TPR):
                        last = spread((0, 1), r, j, bank[2][:, j * P:(j + 1) * P])
                    if phase == REL:
                        for j in range(TPR):
                            last = spread((2,), r, j, bank[3][:, j * P:(j + 1) * P])
                    last.then_inc(keys_spread.sem, 1)

                def turn_rows(r):
                    pe.wait_ge(h_ready.sem, h_ready.after(r, f))
                    pe.wait_ge(ht_ready.sem, ht_ready.before(r, 1, f))
                    for j in range(TPR):
                        last = nc.tensor.transpose(bank[0][:, j * P:(j + 1) * P], e_h[:, r.mod(2), j, :], ident[:, :])
                    last.then_inc(turned.sem, 1)

                def products(r, j):
                    b = r.mod(2)
                    if j == 0:
                        pe.wait_ge(ht_ready.sem, ht_ready.after(r, f))
                        pe.wait_ge(msg_ready.sem, msg_ready.before(r, 1, f))
                    o = bank[1][:, j * P:(j + 1) * P]
                    if phase == REL:
                        pe.wait_ge(htm_ready.sem, htm_ready.after(r, 0, j + 1))
                        for rel in range(NREL):
                            last = nc.tensor.matmul(o, lhsT=e_htm[:, j % 2, rel, :], rhs=w_rel_sb[:, rel, :],
                                                    start=(rel == 0), stop=(rel == NREL - 1))
                    else:
                        last = nc.tensor.matmul(o, lhsT=e_ht[:, b, j * P:(j + 1) * P], rhs=edge_w[phase],
                                                start=True, stop=True)
                    last.then_inc(y_ready.sem, 1)

                def segment_sums(r, j):
                    b = r.mod(2)
                    if j == 0:
                        pe.wait_ge(eq_ready.sem, eq_ready.after(r, f))
                        pe.wait_ge(msg_ready.sem, msg_ready.after(r, f))
                    o = bank[4 + j % 2][:, 0:W]
                    pe.wait_ge(seg_out.sem, seg_out.after(r, f, j + 1 - 2))
                    nc.tensor.matmul(o, lhsT=eq[:, b, j, 0, :], rhs=msg[:, b, j, :], start=True, stop=False)
                    pe.wait_ge(seg_out.sem, seg_out.after(r, f, j))
                    carried = psum_out[:, b, j - 1, :] if j else psum_out[:, 1 - b, TPR - 1, :]
                    nc.tensor.matmul(o, lhsT=eq[:, b, j, 1, :], rhs=carried, start=False, stop=True)\
                        .then_inc(seg_done.sem, 1)

                stages = []
                for j in range(TPR):
                    stages += [(lambda r, j=j: segment_sums(r, j), 3), (lambda r, j=j: products(r, j), 2)]
                run_steps(pe, stages + [(turn_rows, 1), (spread_keys, 1)], ROUNDS, 2)

            def att_phase():
                def pair_sums(r, q):
                    b = r.mod(2)
                    if q == 0:
                        pe.wait_ge(a_eq.sem, a_eq.after(r))
                    pe.wait_ge(a_res.sem, a_res.after(r, 0, q + 1))
                    for a in range(2):
                        pe.wait_ge(a_out.sem, a_out.after(r, 0, 2 * q + a + 1 - 2))
                        for a2 in range(2):
                            last = nc.tensor.matmul(bank[4 + a][:, 0:W], lhsT=eq[:, b, 2 * q + a2, a, :],
                                                    rhs=res[:, b, 2 * q + a2, :], start=(a2 == 0), stop=(a2 == 1))
                        last.then_inc(a_sum.sem, 1)

                def last_sums(r):
                    pair_sums(r, 0)
                    pair_sums(r, 1)

                def spread_keys(r):
                    pe.wait_ge(slots_ready.sem, slots_ready.after(r, ATT * ROUNDS))
                    pe.wait_ge(a_eq.sem, a_eq.before(r, 1))
                    for j in range(TPR):
                        last = spread((0, 1), r, j, bank[7][:, j * P:(j + 1) * P])
                    last.then_inc(a_spread.sem, 1)

                def pairs(r):
                    for q in range(2):
                        pe.wait_ge(a_h.sem, a_h.after(r, 0, q + 1))
                        pe.wait_ge(a_ht.sem, a_ht.after(r, 0, q))
                        for n in range(4):
                            last = nc.tensor.transpose(bank[0][:, n * P:(n + 1) * P], e_h[:, q, n, :], ident[:, :])
                        last.then_inc(a_turned.sem, 1)
                        pe.wait_ge(a_ht.sem, a_ht.after(r, 0, q + 1))
                        pe.wait_ge(a_q.sem, a_q.after(r, 0, q + 1 - 2))
                        pe.wait_ge(a_res.sem, a_res.after(r, 0, q + 1 - 2))
                        for a in range(2):
                            nc.tensor.matmul(bank[1 + q][:, a * P:(a + 1) * P],
                                             lhsT=e_ht[:, q, a * P:(a + 1) * P], rhs=w_q_sb[:, :],
                                             start=True, stop=True)
                            last = nc.tensor.matmul(kv_bank[q][:, 256 * a:256 * a + 256],
                                                    lhsT=e_ht[:, q, (2 + a) * P:(3 + a) * P],
                                                    rhs=w_kv_sb[:, :, :].rearrange("p n d -> p (n d)"),
                                                    start=True, stop=True)
                        last.then_inc(a_qkv.sem, 1)

                run_steps(pe, [(last_sums, 1), (spread_keys, 0), (pairs, 0)], ROUNDS, 2)

            def node_phase(phase):
                mm = first(MATMUL, phase)

                def turn_rows(g):
                    b = g.mod(2)
                    pe.wait_ge(n_h_ready.sem, n_h_ready.after(g, mm))
                    pe.wait_ge(n_ht_ready.sem, n_ht_ready.before(g, 2, mm))
                    for k in range(K):
                        last = nc.tensor.transpose(bank[b][:, k * P:(k + 1) * P], n_h[:, b, k, :], ident[:, :])
                    last.then_inc(n_turned.sem, 1)

                def products(g):
                    b = g.mod(2)
                    pe.wait_ge(n_ht_ready.sem, n_ht_ready.after(g, mm))
                    pe.wait_ge(n_y_used.sem, n_y_used.before(g, 2, mm))
                    bias = {REL: 0, SAGE0: 1, SAGE1: 2}.get(phase)
                    if bias is not None:
                        nc.tensor.matmul(bank[2 + b][:, :], lhsT=ones_bf[:, :],
                                         rhs=bias_bf[:, bias, :, :].rearrange("p k d -> p (k d)"),
                                         start=True, stop=False)
                    for k in range(K):
                        o = bank[2 + b][:, k * P:(k + 1) * P]
                        last = nc.tensor.matmul(o, lhsT=n_ht[:, b, k * P:(k + 1) * P], rhs=node_w[phase],
                                                start=(bias is None), stop=(bias is None or k == K - 1))
                    last.then_inc(n_y_ready.sem, 1)

                run_steps(pe, [(products, 1), (turn_rows, 0)], GROUPS, SLOTS)

            for phase in range(5):
                if phase == ATT:
                    att_phase()
                else:
                    seg_phase(phase)
                    node_phase(phase)

        @block.vector
        def _(dve):
            own = Chain(dve, dve_setup)
            own.begin(Step(None, 1, 0))
            dve.wait_ge(s_const, 20)
            dve.wait_ge(s_keys, 16 * 12)
            nc.vector.tensor_copy(key_rows_f[:, :, :, :], key_rows[:, :, :, :]).then_inc(s_keysf, 1)
            dve.wait_ge(s_keyst, 1)
            for n, cols in enumerate((src_f, dst_f, next_f, type_f)):
                at = 2 * n * P
                last = nc.vector.tensor_copy(cols[:, :], bank[at // 512][:, at % 512:at % 512 + TILES])
            last.then_inc(s_keysc, 1)
            dve.wait_ge(s_keysc, 1)
            own.mark(nc.vector.tensor_copy(src_i[:, :], src_f[:, :]))
            own.mark(nc.vector.tensor_copy(dst_i[:, :], dst_f[:, :]))
            own.mark(nc.vector.tensor_copy(seg_keys[:, :, 0], dst_f[:, :]))
            own.mark(nc.vector.tensor_copy(ident_bf[:, :], ident[:, :]))
            own.mark(nc.vector.tensor_copy(dst_parts[:, 2, :], type_f[:, :]))
            own.wait()
            for n, keys_i in enumerate((src_i, dst_i)):
                own.mark(nc.vector.tensor_scalar(low_i[:, n, :], keys_i[:, :], 255, None, ALU.bitwise_and))
            own.wait()
            for n, (keys, parts) in enumerate(((src_f, src_parts), (dst_f, dst_parts))):
                own.mark(nc.vector.tensor_tensor(parts[:, 0, :], keys[:, :], low_i[:, n, :], ALU.subtract))
                own.mark(nc.vector.tensor_copy(parts[:, 1, :], low_i[:, n, :]))
            own.mark(nc.vector.tensor_tensor(next_f[:, :], dst_f[:, :], next_f[:, :], ALU.is_equal))
            own.wait()
            own.mark(nc.vector.scalar_tensor_tensor(out=last_i[:, :], in0=next_f[:, :], scalar=float(PAD),
                                                    in1=dst_f[:, :], op0=ALU.mult, op1=ALU.max))
            dve.wait_ge(s_wt, 1)
            own.mark(nc.vector.tensor_copy(w_t[:, :, :].rearrange("p n d -> p (n d)"), bank[2][:, :]))
            own.mark(nc.vector.tensor_copy(bias_part[:, 0, :, :], bias_f[:, :, :]))
            own.wait()
            own.mark(nc.vector.tensor_tensor(bias_left[:, 0, :, :], bias_f[:, :, :], bias_part[:, 0, :, :], ALU.subtract))
            own.wait()
            own.mark(nc.vector.tensor_copy(bias_part[:, 1, :, :], bias_left[:, 0, :, :]))
            own.wait()
            own.mark(nc.vector.tensor_tensor(bias_left[:, 1, :, :], bias_left[:, 0, :, :], bias_part[:, 1, :, :],
                                             ALU.subtract))
            own.wait()
            own.mark(nc.vector.tensor_copy(bias_part[:, 2, :, :], bias_left[:, 1, :, :]))
            own.wait()
            own.mark(nc.vector.tensor_scalar(bias_sum[:, :, :], bias_part[:, 0, :, :], part_mask[:, 0:1], None, ALU.mult))
            for n in range(1, BP):
                own.wait()
                own.mark(nc.vector.scalar_tensor_tensor(out=bias_sum[:, :, :], in0=bias_part[:, n, :, :],
                                                        scalar=part_mask[:, n:n + 1], in1=bias_sum[:, :, :],
                                                        op0=ALU.mult, op1=ALU.add))
            own.wait()
            for k in range(K):
                own.mark(nc.vector.tensor_copy(bias_bf[:, :, k, :], bias_sum[:, :, :]))
            own.wait()
            dve.wait_ge(s_setup, 1)
            dve.sem_inc(s_prep, 1)

            edge_chain = Chain(dve, dve_edge)
            scales_chain = Chain(dve, dve_scales)
            in_chain = Chain(dve, dve_in)
            in_scales_chain = Chain(dve, dve_in_scales)
            combine_chain = Chain(dve, dve_combine)
            mid_scales_chain = Chain(dve, dve_mid_scales)
            finish_chain = Chain(dve, dve_finish)
            out_scales_chain = Chain(dve, dve_out_scales)

            def first_indices(phase):
                for b in range(2):
                    fill_slots(phase, b, slice(b * TPR, (b + 1) * TPR))
                    if phase == ATT:
                        nc.vector.tensor_copy(didx[:, b, :], dst_i[:, b * TPR:(b + 1) * TPR])
                    nc.vector.tensor_copy(gidx[:, b, :], src_i[:, b * TPR:(b + 1) * TPR])\
                        .then_inc(gidx_ready.sem, 1)

            def fill_slots(phase, b, columns):
                n = {REL: 3}.get(phase, 2)
                nc.vector.tensor_copy(slot_keys[:, b, 0:n, :], (src_parts if phase == ATT else dst_parts)[:, 0:n, columns])\
                    .then_inc(slots_ready.sem, 1)

            def next_slots(phase, r):
                if r.i is None and r.offset + 2 >= ROUNDS:
                    return
                fill_slots(phase, r.mod(2), bass.ds(r.scaled(TPR, 2 * TPR), TPR))

            def next_indices(phase, r):
                b = r.mod(2)
                dve.wait_ge(gathered[b].sem, gathered[b].after(r.div(2), parity_first(phase, b)))
                if phase == ATT:
                    dve.wait_ge(gathered_d[b].sem, gathered_d[b].after(r.div(2)))
                if r.i is None and r.offset + 2 >= ROUNDS:
                    return
                at = r.scaled(TPR, 2 * TPR)
                if phase == ATT:
                    nc.vector.tensor_copy(didx[:, b, :], dst_i[:, bass.ds(at, TPR)])
                nc.vector.tensor_copy(gidx[:, b, :], src_i[:, bass.ds(at, TPR)]).then_inc(gidx_ready.sem, 1)

            def seg_phase(phase):
                f = seg_index(phase) * ROUNDS
                chain = [edge_chain, scales_chain]
                for own in chain:
                    own.open(1 if phase == REL else 0)

                def arrive(r):
                    next_indices(phase, r)
                    if phase != REL:
                        return
                    own = edge_chain
                    own.begin(r)
                    b = r.mod(2)
                    for j in range(TPR):
                        last = nc.vector.bn_stats(e_stats[:, j, :], got[:, b, j, 0:D])
                    own.mark(last)
                    own.wait()
                    gate(dve)
                    for j in range(TPR):
                        last = nc.vector.bn_aggr(e_mv[:, j, :], e_stats[:, j, :])
                    last.then_inc(e_var_ready.sem, 1)
                    own.end()

                def scales(r):
                    if phase != REL:
                        return
                    own = scales_chain
                    own.begin(r)
                    b = r.mod(2)
                    dve.wait_ge(e_sd_ready.sem, e_sd_ready.after(r))
                    own.mark(nc.vector.reciprocal(got[:, b, :, COL_A], e_sd[:, :]))
                    own.wait()
                    nc.vector.scalar_tensor_tensor(out=got[:, b, :, COL_C], in0=e_mv[:, :, 0], scalar=-1.0,
                                                   in1=got[:, b, :, COL_A], op0=ALU.mult, op1=ALU.mult)\
                        .then_inc(e_scale_ready.sem, 1)
                    own.end()

                def same_keys(r):
                    b = r.mod(2)
                    dve.wait_ge(keys_spread.sem, keys_spread.after(r, f))
                    dve.wait_ge(seg_done.sem, seg_done.before(r, 2, f))
                    nc.vector.tensor_tensor(
                        eq[:, b, :, :, :],
                        bank[2][:, :].rearrange("p (j e) -> p j e", j=TPR).unsqueeze(2).to_broadcast([P, TPR, 2, P]),
                        seg_keys[:, bass.ds(r.scaled(TPR), TPR), :].unsqueeze(3).to_broadcast([P, TPR, 2, P]),
                        ALU.is_equal).then_inc(eq_ready.sem, 1)
                    next_slots(phase, r)

                def scatter_indices(r):
                    b = r.mod(2)
                    wait_landed(dve, scattered[b], scattered[b].before(r.div(2), 1, parity_first(seg_index(phase), b)))
                    nc.vector.tensor_copy(sidx[:, b, :], last_i[:, bass.ds(r.scaled(TPR), TPR)])\
                        .then_inc(sidx_ready.sem, 1)

                def by_relation(r):
                    if phase != REL:
                        return
                    b = r.mod(2)
                    dve.wait_ge(ht_ready.sem, ht_ready.after(r, f))
                    for j in range(TPR):
                        dve.wait_ge(y_ready.sem, y_ready.after(r, f, j + 1 - 2))
                        for rel in range(NREL):
                            last = nc.vector.scalar_tensor_tensor(
                                out=e_htm[:, j % 2, rel, :], in0=bank[3][:, j * P:(j + 1) * P], scalar=float(rel),
                                in1=e_ht[:, b, j * P:(j + 1) * P], op0=ALU.is_equal, op1=ALU.mult)
                        last.then_inc(htm_ready.sem, 1)

                first_indices(phase)
                run_steps(dve, [(arrive, 1), (same_keys, 2), (scatter_indices, 3), (scales, 1), (by_relation, 2)],
                          ROUNDS, 2, ahead=2, behind=2)
                for own in chain:
                    own.close(ROUNDS)

            def att_phase():
                own = edge_chain
                own.open(7)

                def same_keys(r):
                    b = r.mod(2)
                    dve.wait_ge(a_spread.sem, a_spread.after(r))
                    dve.wait_ge(a_sum.sem, a_sum.before(r, 2))
                    for j in range(TPR):
                        q = j // 2
                        last = nc.vector.tensor_scalar(eq[:, b, j, :, :].rearrange("p a e -> p (a e)"),
                                                       bank[7][:, 256 * q:256 * q + 256],
                                                       src_f[:, bass.ds(r.scaled(TPR, j), 1)], None, ALU.is_equal)
                    last.then_inc(a_eq.sem, 1)

                def sum_rows(r):
                    b = r.mod(2)
                    dve.wait_ge(a_eq.sem, a_eq.after(r))
                    own.mark(nc.vector.tensor_tensor(sp_a[:, :], spare_f[:, :], src_f[:, bass.ds(r.scaled(TPR), TPR)],
                                                     ALU.subtract))
                    for j in range(TPR):
                        last = nc.vector.tensor_tensor_reduce(
                            out=dup_out[:, j, :], in0=eq[:, b, j, :, :].rearrange("p a e -> p (a e)"),
                            in1=earlier[:, j % 2, :], scale=1.0, scalar=0.0, op0=ALU.mult, op1=ALU.add,
                            accum_out=dup[:, j:j + 1])
                    own.mark(last)
                    own.wait()
                    own.mark(nc.vector.scalar_tensor_tensor(out=sp_b[:, :], in0=dup[:, :], scalar=0.5, in1=sp_a[:, :],
                                                            op0=ALU.is_gt, op1=ALU.mult))
                    own.wait()
                    wait_landed(dve, a_acc, a_acc.before(r, 2))
                    nc.vector.tensor_tensor(sidx[:, b, :], sp_b[:, :], src_f[:, bass.ds(r.scaled(TPR), TPR)], ALU.add)\
                        .then_inc(sidx_ready.sem, 1)

                def logits(r, q):
                    kv = kv_bank[q][:, :].rearrange("p (a n d) -> p a n d", a=2, n=2)
                    dve.wait_ge(a_q.sem, a_q.after(r, 0, q + 1))
                    own.mark(nc.vector.tensor_tensor(qk[:, :, :], q_sb[:, q, :, :], kv[:, :, 0, :], ALU.mult))
                    own.wait()
                    own.mark(nc.vector.tensor_reduce(att_sum[:, :], qk[:, :, :].rearrange("p a (h d) -> p (a h) d", d=DH),
                                                     AX.X, ALU.add))
                    own.wait()
                    dve.wait_ge(a_exp.sem, a_exp.after(r, 0, q + 1 - 2))
                    nc.vector.tensor_scalar(att_raw[:, q, :], att_sum[:, :], 10.0, -10.0, ALU.min, ALU.max)\
                        .then_inc(a_logit.sem, 1)

                def weighted(r, q):
                    b = r.mod(2)
                    kv = kv_bank[q][:, :].rearrange("p (a n d) -> p a n d", a=2, n=2)
                    dve.wait_ge(a_exp.sem, a_exp.after(r, 0, q + 1))
                    for a in range(2):
                        e = res[:, b, 2 * q + a, D:W].unsqueeze(2).to_broadcast([P, HEADS, DH])
                        last = nc.vector.tensor_tensor(
                            res[:, b, 2 * q + a, 0:D].rearrange("p (h d) -> p h d", d=DH),
                            kv[:, a, 1, :].rearrange("p (h d) -> p h d", d=DH), e, ALU.mult)
                    last.then_inc(a_res.sem, 1)

                def round_(r):
                    own.begin(r)
                    next_indices(ATT, r)
                    same_keys(r)
                    next_slots(ATT, r)
                    sum_rows(r)
                    logits(r, 0)
                    logits(r, 1)
                    weighted(r, 0)
                    weighted(r, 1)
                    own.end()

                first_indices(ATT)
                run_steps(dve, [(round_, 0)], ROUNDS, 2, ahead=2, behind=2)
                own.close(ROUNDS)

            def node_phase(phase):
                rows = x2r if phase == SAGE1 else xr

                def arrived(g):
                    s = g.mod(SLOTS)
                    dve.wait_ge(loaded[s].sem, loaded[s].after(g.div(SLOTS), stores_before(phase, s)))
                    if phase == SAGE1:
                        dve.wait_ge(loaded2[s].sem, loaded2[s].after(g.div(SLOTS)))

                def moments(own, source, stats, mv):
                    for k in range(K):
                        last = nc.vector.bn_stats(stats[:, k, :], source(k))
                    own.mark(last)
                    own.wait()
                    gate(dve)
                    for k in range(K):
                        last = nc.vector.bn_aggr(mv[:, k, :], stats[:, k, :])
                    return last

                def scales(own, sd, mv, a, c):
                    own.mark(nc.vector.reciprocal(a, sd))
                    own.wait()
                    return nc.vector.scalar_tensor_tensor(out=c, in0=mv[:, :, 0], scalar=-1.0, in1=a,
                                                          op0=ALU.mult, op1=ALU.mult)

                def in_moments(g, own):
                    s = g.mod(SLOTS)
                    arrived(g)
                    moments(own, lambda k: xr[:, s, k, 0:D], in_stats[:, g.mod(2), :, :], in_mv[:, g.mod(2), :, :]).then_inc(in_var.sem, 1)

                def in_scales(g, own):
                    s = g.mod(SLOTS)
                    dve.wait_ge(in_sd_ready.sem, in_sd_ready.after(g))
                    scales(own, in_sd[:, g.mod(2), :], in_mv[:, g.mod(2), :, :], xr[:, s, :, COL_A], xr[:, s, :, COL_C]).then_inc(in_scale.sem, 1)

                def product(g):
                    dve.wait_ge(n_y_ready.sem, n_y_ready.after(g, first(MATMUL, phase)))
                    return bank[2 + g.mod(2)][:, :].rearrange("p (k d) -> p k d", k=K)

                def out_moments(g, own):
                    moments(own, lambda k: rows[:, g.mod(SLOTS), k, 0:D], out_stats[:, g.mod(2), :, :], out_mv[:, g.mod(2), :, :]).then_inc(out_var.sem, 1)

                def out_scales(g, own):
                    s = g.mod(SLOTS)
                    dve.wait_ge(out_sd_ready.sem, out_sd_ready.after(g, first(ROW_STATS, phase)))
                    if phase != SAGE1:
                        scales(own, out_sd[:, g.mod(2), :], out_mv[:, g.mod(2), :, :], rows[:, s, :, COL_A], rows[:, s, :, COL_C])\
                            .then_inc(row_ready.sem, 1)
                        return
                    own.mark(nc.vector.reciprocal(rstd[:, :], out_sd[:, g.mod(2), :]))
                    own.wait()
                    own.mark(nc.vector.tensor_tensor(rows[:, s, :, COL_A], rstd[:, :], rows[:, s, :, COL_DIS], ALU.mult))
                    own.wait()
                    nc.vector.scalar_tensor_tensor(out=rows[:, s, :, COL_C], in0=out_mv[:, g.mod(2), :, 0], scalar=-1.0,
                                                   in1=rows[:, s, :, COL_A], op0=ALU.mult, op1=ALU.mult)\
                        .then_inc(row_ready.sem, 1)

                def combine_rel(g, own):
                    s, b = g.mod(SLOTS), g.mod(2)
                    y = product(g)
                    own.mark(nc.vector.tensor_tensor(n_t[:, b, :, :], y, sr[:, s, :, 0:D], ALU.add))
                    own.wait()
                    own.mark(nc.vector.scalar_tensor_tensor(out=xr[:, s, :, 0:D], in0=n_t[:, b, :, :], scalar=0.0,
                                                            in1=xr[:, s, :, 0:D], op0=ALU.max, op1=ALU.add))
                    own.wait()
                    dve.sem_inc(n_y_used.sem, 1)
                    out_moments(g, own)

                def combine_att(g, own):
                    s, b = g.mod(SLOTS), g.mod(2)
                    arrived(g)
                    own.mark(nc.vector.tensor_scalar(den[:, :, :], sr[:, s, :, D:W], 1e-8, None, ALU.add))
                    own.wait()
                    own.mark(nc.vector.reciprocal(den[:, :, :], den[:, :, :]))
                    own.wait()
                    for k in range(K):
                        last = nc.vector.tensor_tensor(
                            n_t[:, b, k, :].rearrange("p (h d) -> p h d", d=DH),
                            sr[:, s, k, 0:D].rearrange("p (h d) -> p h d", d=DH),
                            den[:, k, :].unsqueeze(2).to_broadcast([P, HEADS, DH]), ALU.mult)
                    own.mark(last)
                    own.wait()
                    own.mark(nc.vector.tensor_tensor(xr[:, s, :, 0:D], n_t[:, b, :, :], xr[:, s, :, 0:D], ALU.add))
                    own.wait()
                    out_moments(g, own)

                def combine_mid(g, own):
                    s, b = g.mod(SLOTS), g.mod(2)
                    arrived(g)
                    y = product(g)
                    own.mark(nc.vector.tensor_scalar(per_edge[:, :], sr[:, s, :, COL_CNT], 1.0, None, ALU.max))
                    own.wait()
                    own.mark(nc.vector.reciprocal(per_edge[:, :], per_edge[:, :]))
                    own.wait()
                    for k in range(K):
                        last = nc.vector.scalar_tensor_tensor(out=n_t[:, b, k, :], in0=sr[:, s, k, 0:D],
                                                              scalar=per_edge[:, k:k + 1], in1=y[:, k, :],
                                                              op0=ALU.mult, op1=ALU.add)
                    own.mark(last)
                    own.wait()
                    dve.sem_inc(n_y_used.sem, 1)
                    moments(own, lambda k: n_t[:, b, k, :], mid_stats[:, g.mod(2), :, :], mid_mv[:, g.mod(2), :, :]).then_inc(mid_var.sem, 1)

                def mid_scales(g, own):
                    b = g.mod(2)
                    dve.wait_ge(mid_sd_ready.sem, mid_sd_ready.after(g, first(MID_NORM, phase)))
                    if phase == SAGE1:
                        nc.vector.reciprocal(rows[:, g.mod(SLOTS), :, COL_DIS], root_deg[:, g.mod(2), :])
                    scales(own, mid_sd[:, g.mod(2), :], mid_mv[:, g.mod(2), :, :], mid_ac[:, b, 0, :], mid_ac[:, b, 1, :]).then_inc(mid_scale.sem, 1)

                def finish_mid(g, own):
                    s, b = g.mod(SLOTS), g.mod(2)
                    dve.wait_ge(affine_ready.sem, affine_ready.after(g))
                    own.mark(nc.vector.tensor_tensor(x2r[:, s, :, 0:D], n_u[:, b, :, :], x2r[:, s, :, 0:D], ALU.add))
                    own.wait()
                    dve.sem_inc(n_u_used.sem, 1)
                    out_moments(g, own)

                def combine_gcn(g, own):
                    s, b = g.mod(SLOTS), g.mod(2)
                    y = product(g)
                    own.mark(nc.vector.tensor_tensor(n_t[:, b, :, :], y, sr[:, s, :, 0:D], ALU.add))
                    own.wait()
                    dve.sem_inc(n_y_used.sem, 1)
                    for k in range(K):
                        last = nc.vector.scalar_tensor_tensor(out=xr[:, s, k, 0:D], in0=n_t[:, b, k, :],
                                                              scalar=xr[:, s, k, COL_DIS:COL_DIS + 1],
                                                              in1=xr[:, s, k, 0:D], op0=ALU.mult, op1=ALU.add)
                    last.then_inc(row_ready.sem, 1)

                stages = {
                    REL: [(in_moments, 0, in_chain, 1), (combine_rel, 2, combine_chain, 3),
                          (in_scales, 0, in_scales_chain, 1), (out_scales, 2, out_scales_chain, 1)],
                    ATT: [(combine_att, 0, combine_chain, 5), (out_scales, 1, out_scales_chain, 1)],
                    SAGE0: [(combine_mid, 2, combine_chain, 4), (mid_scales, 2, mid_scales_chain, 1)],
                    SAGE1: [(combine_mid, 2, combine_chain, 4), (finish_mid, 3, finish_chain, 2),
                            (mid_scales, 2, mid_scales_chain, 1), (out_scales, 3, out_scales_chain, 2)],
                    GCN: [(combine_gcn, 2, combine_chain, 1)],
                }[phase]

                def counted(stage, chain, per):
                    chain.open(per)

                    def run(g):
                        chain.begin(g)
                        stage(g, chain)
                        chain.end()
                    return run

                run_steps(dve, [(counted(stage, chain, per), lag) for stage, lag, chain, per in stages], GROUPS, SLOTS)
                for _, _, chain, _ in stages:
                    chain.close(GROUPS)

            for phase in range(5):
                if phase == ATT:
                    att_phase()
                else:
                    seg_phase(phase)
                node_phase(phase)


_INS = ['x', 'src', 'dst', 'edge_type_8', 'L0_gnn_weight', 'L0_gnn_self_loop_weight', 'L0_gnn_bias',
        'L1_gnn_qW', 'L1_gnn_kW', 'L1_gnn_vW', 'L2_gnn_W_self0', 'L2_gnn_W_neigh0', 'L2_gnn_b0',
        'L2_gnn_W_self1', 'L2_gnn_W_neigh1', 'L2_gnn_b1', 'L2_gnn_ln_g', 'L2_gnn_ln_b', 'L3_gnn_W']


def kernel(**inputs):
    import numpy as _np
    import concourse.bacc as _bacc
    from concourse import mybir as _mybir
    from concourse.bass_utils import run_bass_kernel_spmd as _run

    nc = _bacc.Bacc("TRN2", target_bir_lowering=False, num_devices=1)
    arrays, args = {}, []
    for name in _INS:
        a = _np.ascontiguousarray(inputs[name])
        arrays[f"in_{name}_dram"] = a
        args.append(nc.dram_tensor(f"in_{name}_dram", a.shape, _mybir.dt.from_np(a.dtype), kind="ExternalInput").ap())
    args.append(nc.dram_tensor("out_0_dram", inputs['x'].shape, _mybir.dt.float32, kind="ExternalOutput").ap())
    gnn_stack_kernel(nc, *args)
    r = _run(nc, [arrays], core_ids=[0])
    return r.results[0]["out_0_dram"]
```

```python
import concourse.bass as bass
from concourse import mybir
from contextlib import ExitStack


class Step:

    def __init__(self, i, times, offset):
        self.i, self.times, self.offset = i, times, offset

    def scaled(self, m, plus=0):
        if self.i is None:
            return self.offset * m + plus
        return self.i * (self.times * m) + (self.offset * m + plus)

    def mod(self, m):
        return self.offset % m

    def div(self, m):
        if self.i is None:
            return Step(None, 1, self.offset // m)
        return Step(self.i, self.times // m, self.offset // m)


class Signal:

    def __init__(self, sem, per, credit=0):
        self.sem, self.per, self.credit = sem, per, credit

    def after(self, step, first=0, n=None):
        n = self.per if n is None else n
        return step.scaled(self.per, self.credit + first * self.per + n)

    def before(self, step, back, first=0):
        return step.scaled(self.per, self.credit + (first - back + 1) * self.per)


def wait_landed(eng, signal, value):
    if not isinstance(value, int) or value > 0:
        eng.wait_ge(signal.sem, value)


class Chain:

    def __init__(self, eng, sem):
        self.eng, self.sem, self.base, self.per = eng, sem, 0, 0

    def open(self, per):
        self.per = per

    def close(self, steps):
        self.base += self.per * steps

    def begin(self, step):
        self.step, self.k = step, 0

    def mark(self, ins):
        self.k += 1
        ins.then_inc(self.sem, 1)

    def wait(self):
        self.eng.wait_ge(self.sem, self.step.scaled(self.per, self.base + self.k))

    def end(self):
        assert self.k == self.per, (self.k, self.per)


def run_steps(eng, stages, total, unroll, ahead=0, behind=0):
    deepest = max(lag for _, lag in stages)
    low = -(-(deepest + behind) // unroll) * unroll
    high = (total - 1 - ahead) // unroll * unroll

    def turn(it, i=None):
        for stage, lag in stages:
            if i is not None:
                stage(Step(i, unroll, it - lag))
            elif 0 <= it - lag < total:
                stage(Step(None, 1, it - lag))

    for it in range(low):
        turn(it)
    with eng.Fori(low // unroll, high // unroll) as i:
        for u in range(unroll):
            turn(u, i)
    for it in range(high, total + deepest):
        turn(it)


def gnn_stack_kernel(nc, x, src, dst, edge_type, w_rel, w_loop, b_loop, w_q, w_k, w_v,
                     w_self0, w_neigh0, b0, w_self1, w_neigh1, b1, ln_g, ln_b, w_gcn, out):
    fp32 = mybir.dt.float32
    i32 = mybir.dt.int32
    bf16 = mybir.dt.bfloat16
    ALU = mybir.AluOpType
    ACT = mybir.ActivationFunctionType
    AX = mybir.AxisListType

    P = 128
    N, D = x.shape
    E = src.shape[0]
    NREL = w_rel.shape[0]
    HEADS = 4
    DH = D // HEADS
    EPS = 1e-5

    COL_A, COL_C, COL_DIS = D, D + 1, D + 2
    COL_CNT = D
    W = D + HEADS

    TPR = 4
    TILES = -(-E // P)
    ROUNDS = TILES // TPR
    assert TILES == ROUNDS * TPR and ROUNDS % 2 == 1
    SPARE = 2 * P
    PAD = N + SPARE

    K = 4
    GROUP = K * P
    GROUPS = -(-N // GROUP)
    SLOTS = 8
    DEEP = 4

    REL, ATT, SAGE0, SAGE1, GCN = range(5)
    SEG_PHASES = [REL, SAGE0, SAGE1, GCN]

    rows1 = nc.dram_tensor("rows1", (N, W), fp32, kind="Internal").ap()
    rows2 = nc.dram_tensor("rows2", (N, W), fp32, kind="Internal").ap()
    rowsg = nc.dram_tensor("rowsg", (N, W), fp32, kind="Internal").ap()
    rows3 = nc.dram_tensor("rows3", (N, W), fp32, kind="Internal").ap()
    sums = nc.dram_tensor("sums", (PAD + 1, W), fp32, kind="Internal").ap()
    attsums = nc.dram_tensor("attsums", (PAD + 1, W), fp32, kind="Internal").ap()

    ctx = ExitStack()
    with ctx:
        def sb(name, shape, dt=fp32):
            return ctx.enter_context(nc.sbuf_tensor(name, shape, dt))

        def sem(name):
            return ctx.enter_context(nc.semaphore(name))

        ident = sb("ident", [P, P])
        ident_bf = sb("ident_bf", [P, P], bf16)
        zeros = sb("zeros", [P, 5148])
        eps_col = sb("eps_col", [P, 1])
        ones_col = sb("ones_col", [P, 1])
        w_rel_sb = sb("w_rel_sb", [P, NREL, D])
        w_in = sb("w_in", [P, 4, D])
        w_t = sb("w_t", [P, 4, D])
        w_loop_sb = sb("w_loop_sb", [P, D])
        w_q_sb = sb("w_q_sb", [P, D])
        w_kv_sb = sb("w_kv_sb", [P, 2, D])
        w_gcn_sb = sb("w_gcn_sb", [P, D])
        BP = 3
        bias_f = sb("bias_f", [BP, 3, D])
        bias_part = sb("bias_part", [BP, 3, 3, D], bf16)
        bias_left = sb("bias_left", [BP, 2, 3, D])
        bias_sum = sb("bias_sum", [BP, 3, D])
        part_mask = sb("part_mask", [BP, BP])
        bias_bf = sb("bias_bf", [BP, 3, K, D], bf16)
        ones_bf = sb("ones_bf", [BP, P], bf16)
        ln_g_bc = sb("ln_g_bc", [P, D])
        ln_b_bc = sb("ln_b_bc", [P, D])
        key_rows = sb("key_rows", [P, 4, 2, P], i32)
        key_rows_f = sb("key_rows_f", [P, 4, 2, P])
        src_f = sb("src_f", [P, TILES])
        dst_f = sb("dst_f", [P, TILES])
        next_f = sb("next_f", [P, TILES])
        type_f = sb("type_f", [P, TILES])
        low_i = sb("low_i", [P, 2, TILES], i32)
        src_parts = sb("src_parts", [P, 2, TILES], bf16)
        dst_parts = sb("dst_parts", [P, 3, TILES], bf16)
        seg_keys = sb("seg_keys", [P, TILES, 2])
        src_i = sb("src_i", [P, TILES], i32)
        dst_i = sb("dst_i", [P, TILES], i32)
        last_i = sb("last_i", [P, TILES], i32)
        spare_f = sb("spare_f", [P, TPR])
        earlier = sb("earlier", [P, 2, 2 * P])
        gidx = sb("gidx", [P, 2, TPR], i32)
        didx = sb("didx", [P, 2, TPR], i32)
        sidx = sb("sidx", [P, 2, TPR], i32)
        slot_keys = sb("slot_keys", [P, 2, 3, TPR], bf16)
        got = sb("got", [P, 2, TPR, W])
        got_d = sb("got_d", [P, 2, TPR, W])
        e_stats = sb("e_stats", [P, TPR, 6])
        e_mv = sb("e_mv", [P, TPR, 2])
        e_sd = sb("e_sd", [P, TPR])
        e_h = sb("e_h", [P, 2, TPR, D])
        e_ht = sb("e_ht", [P, 2, TPR * P])
        e_htm = sb("e_htm", [P, 2, NREL, 2 * P])
        eq = sb("eq", [P, 2, TPR, 2, P])
        msg = sb("msg", [P, 2, TPR, W])
        res = sb("res", [P, 2, TPR, W])
        psum_out = sb("psum_out", [P, 2, TPR, W])
        q_sb = sb("q_sb", [P, 2, 2, D])
        qk = sb("qk", [P, 2, D])
        att_raw = sb("att_raw", [P, 2, 2 * HEADS])
        dup_out = sb("dup_out", [P, TPR, 2 * P])
        att_sum = sb("att_sum", [P, 2 * HEADS])
        dup = sb("dup", [P, TPR])
        sp_a = sb("sp_a", [P, TPR])
        sp_b = sb("sp_b", [P, TPR])
        xr = sb("xr", [P, SLOTS, K, W])
        sr = sb("sr", [P, SLOTS, K, W])
        x2r = sb("x2r", [P, SLOTS, K, W])
        in_stats = sb("in_stats", [P, 2, K, 6])
        in_mv = sb("in_mv", [P, DEEP, K, 2])
        in_sd = sb("in_sd", [P, 2, K])
        mid_stats = sb("mid_stats", [P, 2, K, 6])
        mid_mv = sb("mid_mv", [P, DEEP, K, 2])
        mid_sd = sb("mid_sd", [P, 2, K])
        mid_ac = sb("mid_ac", [P, 2, 2, K])
        root_deg = sb("root_deg", [P, 2, K])
        out_stats = sb("out_stats", [P, 2, K, 6])
        out_mv = sb("out_mv", [P, DEEP, K, 2])
        out_sd = sb("out_sd", [P, 2, K])
        rstd = sb("rstd", [P, 2, K])
        den = sb("den", [P, 2, K, HEADS])
        n_h = sb("n_h", [P, 2, K, D])
        n_ht = sb("n_ht", [P, 2, K * P])
        n_t = sb("n_t", [P, DEEP, K, D])
        n_u = sb("n_u", [P, 2, K, D])

        bank = [ctx.enter_context(nc.psum_tensor(f"bank{i}", [P, 512], fp32)) for i in range(8)]
        kv_bank = [bank[3], bank[6]]
        type_bank = [bank[3], bank[6]]

        s_const = sem("s_const")
        s_zeros = sem("s_zeros")
        s_pads = sem("s_pads")
        s_weights = sem("s_weights")
        s_keys = sem("s_keys")
        s_keysf = sem("s_keysf")
        s_keyst = sem("s_keyst")
        s_keysc = sem("s_keysc")
        s_prep = sem("s_prep")
        s_setup = sem("s_setup")
        s_wt = sem("s_wt")
        s_zero_sums = sem("s_zero_sums")
        s_zero_att = sem("s_zero_att")
        s_gate = sem("s_gate")

        gidx_ready = Signal(sem("gidx_ready"), 1)
        slots_ready = Signal(sem("slots_ready"), 1)
        sidx_ready = Signal(sem("sidx_ready"), 1)
        gathered = [Signal(sem(f"gathered{b}"), 16 * TPR) for b in range(2)]
        gathered_d = [Signal(sem(f"gathered_d{b}"), 16 * TPR) for b in range(2)]
        e_var_ready = Signal(sem("e_var_ready"), 1)
        e_sd_ready = Signal(sem("e_sd_ready"), 1)
        e_scale_ready = Signal(sem("e_scale_ready"), 1)
        h_ready = Signal(sem("h_ready"), 1, 2)
        turned = Signal(sem("turned"), 1, 2)
        ht_ready = Signal(sem("ht_ready"), 1, 2)
        htm_ready = Signal(sem("htm_ready"), 2, 4)
        y_ready = Signal(sem("y_ready"), TPR, 2 * TPR)
        keys_spread = Signal(sem("keys_spread"), 1)
        eq_ready = Signal(sem("eq_ready"), 1, 2)
        msg_ready = Signal(sem("msg_ready"), 1, 2)
        seg_done = Signal(sem("seg_done"), TPR, 2 * TPR)
        seg_out = Signal(sem("seg_out"), TPR, 2 * TPR)
        scattered = [Signal(sem(f"scattered{b}"), 16 * TPR) for b in range(2)]
        a_h = Signal(sem("a_h"), 2, 4)
        a_turned = Signal(sem("a_turned"), 2, 4)
        a_ht = Signal(sem("a_ht"), 2, 4)
        a_qkv = Signal(sem("a_qkv"), 2, 4)
        a_q = Signal(sem("a_q"), 2, 4)
        a_logit = Signal(sem("a_logit"), 2, 4)
        a_exp = Signal(sem("a_exp"), 2, 4)
        a_res = Signal(sem("a_res"), 2, 4)
        a_sum = Signal(sem("a_sum"), 4, 8)
        a_out = Signal(sem("a_out"), 4, 8)
        a_eq = Signal(sem("a_eq"), 1, 2)
        a_spread = Signal(sem("a_spread"), 1)
        a_acc = Signal(sem("a_acc"), 64)
        credited = [h_ready, turned, ht_ready, htm_ready, y_ready, eq_ready, msg_ready, seg_done, seg_out,
                    a_h, a_turned, a_ht, a_qkv, a_q, a_logit, a_exp, a_res, a_sum, a_out, a_eq]
        loaded = [Signal(sem(f"loaded{s}"), 32) for s in range(SLOTS)]
        loaded2 = [Signal(sem(f"loaded2_{s}"), 16) for s in range(SLOTS)]
        stored = [Signal(sem(f"stored{s}"), 16) for s in range(SLOTS)]
        in_var = Signal(sem("in_var"), 1)
        in_sd_ready = Signal(sem("in_sd_ready"), 1)
        in_scale = Signal(sem("in_scale"), 1)
        out_var = Signal(sem("out_var"), 1)
        out_sd_ready = Signal(sem("out_sd_ready"), 1)
        n_h_ready = Signal(sem("n_h_ready"), 1, 2)
        n_turned = Signal(sem("n_turned"), 1, 2)
        n_ht_ready = Signal(sem("n_ht_ready"), 1, 2)
        n_y_ready = Signal(sem("n_y_ready"), 1, 2)
        n_y_used = Signal(sem("n_y_used"), 1, 2)
        mid_var = Signal(sem("mid_var"), 1)
        mid_sd_ready = Signal(sem("mid_sd_ready"), 1)
        mid_scale = Signal(sem("mid_scale"), 1, 2)
        mid_ready = Signal(sem("mid_ready"), 1, DEEP)
        scaled_ready = Signal(sem("scaled_ready"), 1)
        shifted_ready = Signal(sem("shifted_ready"), 1)
        weighted_ready = Signal(sem("weighted_ready"), 1)
        x_added = Signal(sem("x_added"), 1, SLOTS)
        row_ready = Signal(sem("row_ready"), 1, 2)
        credited += [n_h_ready, n_turned, n_ht_ready, n_y_ready, n_y_used, mid_scale, mid_ready, x_added, row_ready]
        dve_edge = sem("dve_edge")
        dve_scales = sem("dve_scales")
        dve_setup = sem("dve_setup")
        in_stats_done = Signal(sem("in_stats_done"), 1)
        mid_stats_done = Signal(sem("mid_stats_done"), 1)
        out_stats_done = Signal(sem("out_stats_done"), 1)
        in_rstd_done = Signal(sem("in_rstd_done"), 1)
        mid_rstd_done = Signal(sem("mid_rstd_done"), 1)
        out_rstd_done = Signal(sem("out_rstd_done"), 1)
        out_a_done = Signal(sem("out_a_done"), 1)
        den_done = Signal(sem("den_done"), 1)
        den_inverted = Signal(sem("den_inverted"), 1)

        block = ctx.enter_context(nc.Block())

        def gate(eng):
            eng.sem_inc(s_gate, 1)

        def parity_first(phase, b):
            return phase * (ROUNDS // 2 + 1 - b)

        def seg_index(phase):
            return SEG_PHASES.index(phase)

        def extra(phase):
            return 1 if phase == REL else 0

        def stores_before(phase, s):
            return phase * (GROUPS // SLOTS + (1 if s < GROUPS % SLOTS else 0))

        MATMUL = [REL, SAGE0, SAGE1, GCN]
        MID_NORM = [SAGE0, SAGE1]
        ROW_STATS = [REL, ATT, SAGE1]
        OUT_RING = [REL, SAGE0, SAGE1]
        DIVIDED = [ATT, SAGE0, SAGE1]

        def first(phases, phase):
            return phases.index(phase) * GROUPS

        node_in = {REL: x, ATT: rows1, SAGE0: rows2, SAGE1: rowsg, GCN: rows3}
        node_sum = {REL: sums, ATT: attsums, SAGE0: sums, SAGE1: sums, GCN: sums}
        node_out = {REL: rows1, ATT: rows2, SAGE0: rowsg, SAGE1: rows3, GCN: out}
        node_w = {REL: w_loop_sb[:, :], SAGE0: w_t[:, 0, :], SAGE1: w_t[:, 2, :], GCN: w_gcn_sb[:, :]}
        edge_w = {SAGE0: w_t[:, 1, :], SAGE1: w_t[:, 3, :], GCN: w_gcn_sb[:, :]}
        edge_in = {REL: x, ATT: rows1, SAGE0: rows2, SAGE1: rowsg, GCN: rows3}

        ZROWS = zeros.shape[1] // W
        ZPARTS = N // P // ZROWS
        ZLEFT = PAD + 1 - ZPARTS * ZROWS * P
        ZLEFT_A = ZLEFT // P * P
        ZERO_COUNT = ZPARTS + (1 if ZLEFT_A else 0) + (1 if ZLEFT - ZLEFT_A else 0)
        ZROUND = (PAD + 1) // (ROUNDS * P)
        assert 0 < PAD + 1 - ROUNDS * ZROUND * P <= P

        @block.sync
        def _(sp):
            for sig in credited:
                sp.sem_inc(sig.sem, sig.credit)
            sp.wait_ge(s_zeros, 1)
            sp.wait_ge(s_keys, 16 * 12)
            sp.wait_ge(s_weights, 16 * 15)
            at = 0
            for z in range(ZPARTS):
                if z >= 1:
                    sp.wait_ge(s_zero_sums, 16 * z)
                sp.dma_start(sums[at:at + ZROWS * P, :].rearrange("(p r) c -> p (r c)", p=P), zeros[:, :])\
                    .then_inc(s_zero_sums, 16)
                at += ZROWS * P
            if ZLEFT_A:
                sp.dma_start(sums[at:at + ZLEFT_A, :].rearrange("(p r) c -> p (r c)", p=P),
                             zeros[:, 0:ZLEFT_A // P * W]).then_inc(s_zero_sums, 16)
                at += ZLEFT_A
            if ZLEFT - ZLEFT_A:
                sp.dma_start(sums[at:PAD + 1, :], zeros[0:ZLEFT - ZLEFT_A, 0:W]).then_inc(s_zero_sums, 16)

            def zero_att(r):
                sp.wait_ge(turned.sem, turned.after(r))
                sp.dma_start(attsums[bass.ds(r.scaled(ZROUND * P), ZROUND * P), :].rearrange("(p r) c -> p (r c)", p=P),
                             zeros[:, 0:ZROUND * W]).then_inc(s_zero_att, 16)

            run_steps(sp, [(zero_att, 0)], ROUNDS, 1)
            sp.dma_start(attsums[ROUNDS * ZROUND * P:PAD + 1, :], zeros[0:PAD + 1 - ROUNDS * ZROUND * P, 0:W])\
                .then_inc(s_zero_att, 16)

            for phase in range(5):
                if phase == ATT:
                    sp.wait_ge(a_acc.sem, ROUNDS * 64)
                else:
                    for b in range(2):
                        sp.wait_ge(scattered[b].sem, parity_first(seg_index(phase) + 1, b) * 16 * TPR)
                if phase > 0:
                    for s in range(SLOTS):
                        sp.wait_ge(stored[s].sem, 16 * stores_before(phase, s))

                def span(g):
                    if g.i is None and g.offset == GROUPS - 1:
                        return slice(N - GROUP, N)
                    return bass.ds(g.scaled(GROUP), GROUP)

                def load(g):
                    s = g.mod(SLOTS)
                    v = g.div(SLOTS)
                    if phase == REL:
                        sp.wait_ge(x_added.sem, x_added.before(g, SLOTS))
                    elif phase == SAGE0:
                        sp.wait_ge(n_y_used.sem, n_y_used.before(g, SLOTS, first(MATMUL, phase)))
                    elif phase == SAGE1:
                        sp.wait_ge(mid_sd_ready.sem, mid_sd_ready.before(g, SLOTS, first(MID_NORM, phase)))
                    else:
                        wait_landed(sp, stored[s], stored[s].before(v, 1, stores_before(phase, s)))
                    table = node_in[phase]
                    width = table.shape[1]
                    sp.dma_start(xr[:, s, :, 0:width], table[span(g), :].rearrange("(p k) c -> p k c", k=K))\
                        .then_inc(loaded[s].sem, 16)
                    sp.dma_start(sr[:, s, :, :], node_sum[phase][span(g), :].rearrange("(p k) c -> p k c", k=K))\
                        .then_inc(loaded[s].sem, 16)

                def load_x2(g):
                    if phase != SAGE1:
                        return
                    s = g.mod(SLOTS)
                    wait_landed(sp, stored[s], stored[s].before(g.div(SLOTS), 1, stores_before(phase, s)))
                    sp.dma_start(x2r[:, s, :, :], rows2[span(g), :].rearrange("(p k) c -> p k c", k=K))\
                        .then_inc(loaded2[s].sem, 16)

                def store(g):
                    s = g.mod(SLOTS)
                    sp.wait_ge(row_ready.sem, row_ready.after(g, phase * GROUPS))
                    if g.i is None and g.offset == GROUPS - 1:
                        o = (GROUPS - 2) % SLOTS
                        sp.wait_ge(stored[o].sem, 16 * (stores_before(phase, o) + (GROUPS - 2) // SLOTS + 1))
                    table = node_out[phase]
                    ring = x2r if phase in OUT_RING else xr
                    sp.dma_start(table[span(g), :].rearrange("(p k) c -> p k c", k=K),
                                 ring[:, s, :, 0:table.shape[1]]).then_inc(stored[s].sem, 16)

                store_lag = {REL: 9, ATT: 6, SAGE0: 9, SAGE1: 13, GCN: 6}[phase]
                run_steps(sp, [(load, 0), (load_x2, 7), (store, store_lag)], GROUPS, SLOTS, behind=SLOTS)
            for s in range(SLOTS):
                sp.wait_ge(stored[s].sem, 16 * stores_before(5, s))

        @block.gpsimd
        def _(pool):
            nc.gpsimd.memset(key_rows[:, :, :, :], PAD).then_inc(s_pads, 1)
            nc.gpsimd.memset(ident[:, :], 0.0).then_inc(s_const, 1)
            nc.gpsimd.memset(ones_bf[:, :], 1.0).then_inc(s_const, 1)
            nc.gpsimd.memset(part_mask[:, :], 0.0).then_inc(s_const, 1)
            nc.gpsimd.memset(ones_col[:, :], 1.0).then_inc(s_const, 1)
            nc.gpsimd.memset(eps_col[:, :], EPS).then_inc(s_const, 1)
            nc.gpsimd.memset(msg[:, :, :, :], 0.0).then_inc(s_const, 1)
            nc.gpsimd.memset(psum_out[:, :, :, :], 0.0).then_inc(s_const, 1)
            nc.gpsimd.memset(earlier[:, :, :], 1.0).then_inc(s_const, 1)
            nc.gpsimd.memset(seg_keys[:, :, :], -1.0).then_inc(s_const, 1)
            nc.gpsimd.memset(res[:, :, :, :], 0.0).then_inc(s_const, 1)
            nc.gpsimd.memset(got[:, :, :, :], 0.0).then_inc(s_const, 1)
            nc.gpsimd.memset(got_d[:, :, :, :], 0.0).then_inc(s_const, 1)
            nc.gpsimd.memset(x2r[:, :, :, D:W], 0.0).then_inc(s_const, 1)
            nc.gpsimd.iota(spare_f[:, :].rearrange("p (q a) -> p q a", a=2), pattern=[[0, 2], [P, 2]], base=N,
                           channel_multiplier=1, allow_small_or_imprecise_dtypes=True).then_inc(s_const, 1)
            pool.wait_ge(s_const, 14)
            nc.gpsimd.affine_select(out=ident[:, :], in_=ident[:, :], compare_op=ALU.not_equal, fill=1.0,
                                    base=0, pattern=[[-1, P]], channel_multiplier=1).then_inc(s_const, 1)
            nc.gpsimd.affine_select(out=part_mask[:, :], in_=part_mask[:, :], compare_op=ALU.not_equal, fill=1.0,
                                    base=0, pattern=[[-1, BP]], channel_multiplier=1).then_inc(s_const, 1)
            nc.gpsimd.affine_select(out=earlier[:, :, :], in_=earlier[:, :, :], compare_op=ALU.is_gt, fill=0.0,
                                    base=0, pattern=[[P, 2], [-1, 2 * P]], channel_multiplier=1).then_inc(s_const, 1)
            nc.gpsimd.memset(msg[:, :, :, COL_CNT:COL_CNT + 1], 1.0).then_inc(s_const, 1)
            pool.wait_ge(s_keysc, 1)
            nc.gpsimd.affine_select(out=seg_keys[:, 1:TILES, 1], in_=dst_f[:, 0:TILES - 1], compare_op=ALU.is_ge,
                                    fill=-1.0, base=-(P - 1), pattern=[[0, TILES - 1]], channel_multiplier=1)\
                .then_inc(s_setup, 1)
            bound = pool.to_reg(N - 1)
            top = pool.to_reg(PAD)

            for phase in range(5):
                if phase > 0:
                    for s in range(SLOTS):
                        pool.wait_ge(stored[s].sem, 16 * stores_before(phase, s))
                table = edge_in[phase]
                width = table.shape[1]

                def gather(r, tiles=range(TPR)):
                    b = r.mod(2)
                    if tiles[0] == 0:
                        pool.wait_ge(gidx_ready.sem, gidx_ready.after(r, phase * ROUNDS))
                        if phase == ATT:
                            pool.wait_ge(a_h.sem, a_h.before(r, 2))
                        else:
                            pool.wait_ge(h_ready.sem, h_ready.before(r, 2, seg_index(phase) * ROUNDS))
                        gate(pool)
                    for j in tiles:
                        pool.indirect_dma_start(
                            out=got[:, b, j, 0:width], out_offset=None, in_=table[:, :],
                            in_offset=bass.IndirectOffsetOnAxis(ap=gidx[:, b, j:j + 1], axis=0),
                            bounds_check=bound, oob_is_err=False).then_inc(gathered[b].sem, 16)
                        if phase == ATT:
                            pool.indirect_dma_start(
                                out=got_d[:, b, j, :], out_offset=None, in_=table[:, :],
                                in_offset=bass.IndirectOffsetOnAxis(ap=didx[:, b, j:j + 1], axis=0),
                                bounds_check=bound, oob_is_err=False).then_inc(gathered_d[b].sem, 16)


                def scatter(r):
                    b = r.mod(2)
                    seg = seg_index(phase)
                    if phase == REL and r.i is None and r.offset == 0:
                        pool.wait_ge(s_zero_sums, 16 * ZERO_COUNT)
                    pool.wait_ge(sidx_ready.sem, sidx_ready.after(r, phase * ROUNDS))
                    for j in range(TPR):
                        pool.wait_ge(seg_out.sem, seg_out.after(r, seg * ROUNDS, j + 1))
                        gate(pool)
                        pool.indirect_dma_start(
                            out=sums[:, :], out_offset=bass.IndirectOffsetOnAxis(ap=sidx[:, b, j:j + 1], axis=0),
                            in_=psum_out[:, b, j, :], in_offset=None,
                            bounds_check=bound, oob_is_err=False).then_inc(scattered[b].sem, 16)

                def add_pair(r, q):
                    b = r.mod(2)
                    if q == 0:
                        pool.wait_ge(sidx_ready.sem, sidx_ready.after(r, phase * ROUNDS))
                    pool.wait_ge(a_out.sem, a_out.after(r, 0, 2 * q + 2))
                    wait_landed(pool, a_acc, a_acc.after(r, 0, 32 * q))
                    gate(pool)
                    for j in (2 * q, 2 * q + 1):
                        pool.indirect_dma_start(
                            out=attsums[:, :], out_offset=bass.IndirectOffsetOnAxis(ap=sidx[:, b, j:j + 1], axis=0),
                            in_=psum_out[:, b, j, :], in_offset=None, bounds_check=top, oob_is_err=True,
                            compute_op=ALU.add).then_inc(a_acc.sem, 16)

                if phase == ATT:
                    pool.wait_ge(s_zero_att, 16 * (ROUNDS + 1))
                    run_steps(pool, [(lambda r: gather(r, range(0, 2)), 0), (lambda r: add_pair(r, 0), 2),
                                     (lambda r: gather(r, range(2, 4)), 0), (lambda r: add_pair(r, 1), 2)],
                              ROUNDS, 2, behind=2)
                else:
                    run_steps(pool, [(gather, 0), (scatter, 3 + extra(phase))], ROUNDS, 2, behind=1)

                gains = ln_g_bc[:, :].unsqueeze(1).to_broadcast([P, K, D])
                shifts = ln_b_bc[:, :].unsqueeze(1).to_broadcast([P, K, D])
                pool.wait_ge(s_weights, 16 * 15)

                def add_x(g):
                    s = g.mod(SLOTS)
                    if phase == REL:
                        pool.wait_ge(n_y_used.sem, n_y_used.after(g))
                        wait_landed(pool, stored[s], stored[s].before(g.div(SLOTS), 1, stores_before(phase, s)))
                    else:
                        pool.wait_ge(weighted_ready.sem, weighted_ready.after(g))
                    gate(pool)
                    ring = x2r if phase in OUT_RING else xr
                    nc.gpsimd.tensor_tensor(ring[:, s, :, 0:D], n_t[:, g.mod(DEEP), :, :], xr[:, s, :, 0:D], ALU.add)\
                        .then_inc(x_added.sem, 1)

                def scale(g):
                    b = g.mod(2)
                    pool.wait_ge(mid_ready.sem, mid_ready.after(g, first(MID_NORM, phase)))
                    gate(pool)
                    nc.gpsimd.tensor_tensor(n_u[:, b, :, :], n_u[:, b, :, :], gains, ALU.mult)\
                        .then_inc(scaled_ready.sem, 1)

                def shift(g):
                    s, b = g.mod(SLOTS), g.mod(2)
                    wait_landed(pool, stored[s], stored[s].before(g.div(SLOTS), 1, stores_before(phase, s)))
                    gate(pool)
                    nc.gpsimd.memset(x2r[:, s, :, COL_A], 1.0)
                    nc.gpsimd.memset(x2r[:, s, :, COL_C], 0.0)
                    pool.wait_ge(scaled_ready.sem, scaled_ready.after(g))
                    gate(pool)
                    nc.gpsimd.tensor_tensor(x2r[:, s, :, 0:D], n_u[:, b, :, :], shifts, ALU.add)\
                        .then_inc(row_ready.sem, 1)

                def shift_x2(g):
                    s = g.mod(SLOTS)
                    pool.wait_ge(loaded2[s].sem, loaded2[s].after(g.div(SLOTS)))
                    gate(pool)
                    nc.gpsimd.tensor_tensor(x2r[:, s, :, 0:D], x2r[:, s, :, 0:D], shifts, ALU.add)\
                        .then_inc(shifted_ready.sem, 1)

                def add_x2(g):
                    s, b = g.mod(SLOTS), g.mod(2)
                    pool.wait_ge(shifted_ready.sem, shifted_ready.after(g))
                    pool.wait_ge(scaled_ready.sem, scaled_ready.after(g, first(MID_NORM, phase)))
                    gate(pool)
                    nc.gpsimd.tensor_tensor(x2r[:, s, :, 0:D], n_u[:, b, :, :], x2r[:, s, :, 0:D], ALU.add)\
                        .then_inc(x_added.sem, 1)

                stages = {
                    REL: [(add_x, 0)],
                    ATT: [(add_x, 0)],
                    SAGE0: [(scale, 0), (shift, 0)],
                    SAGE1: [(scale, 1), (shift_x2, 0), (add_x2, 1)],
                    GCN: [],
                }[phase]
                if stages:
                    run_steps(pool, stages, GROUPS, SLOTS, behind=SLOTS)

        @block.scalar
        def _(act):
            act.wait_ge(s_pads, 1)
            for n, (keys, shift) in enumerate([(src, 0), (dst, 0), (dst, 1), (edge_type, 0)]):
                act.dma_start(key_rows[:, n, 0, :], keys[shift:shift + P * P].rearrange("(t p) -> t p", p=P))\
                    .then_inc(s_keys, 16)
                full = (E - shift) // P
                act.dma_start(key_rows[0:full - P, n, 1, :],
                             keys[shift + P * P:shift + full * P].rearrange("(t p) -> t p", p=P)).then_inc(s_keys, 16)
                left = E - shift - full * P
                act.dma_start(key_rows[full - P:full - P + 1, n, 1, 0:left],
                             keys[shift + full * P:E].rearrange("(t p) -> t p", t=1)).then_inc(s_keys, 16)
            act.dma_start(w_rel_sb[:, :, :], w_rel.rearrange("r d o -> d r o")).then_inc(s_weights, 16)
            act.dma_start(w_loop_sb[:, :], w_loop).then_inc(s_weights, 16)
            for n, w in enumerate((w_self0, w_neigh0, w_self1, w_neigh1)):
                act.dma_start(w_in[:, n, :], w).then_inc(s_weights, 16)
            act.dma_start(w_q_sb[:, :], w_q).then_inc(s_weights, 16)
            act.dma_start(w_kv_sb[:, 0, :], w_k).then_inc(s_weights, 16)
            act.dma_start(w_kv_sb[:, 1, :], w_v).then_inc(s_weights, 16)
            act.dma_start(w_gcn_sb[:, :], w_gcn).then_inc(s_weights, 16)
            for n, v in enumerate((b_loop, b0, b1)):
                act.dma_start(bias_f[:, n, :], v.rearrange("(a n) -> a n", a=1).to_broadcast([BP, D]))\
                    .then_inc(s_weights, 16)
            act.dma_start(ln_g_bc[:, :], ln_g.rearrange("(a n) -> a n", a=1).to_broadcast([P, D])).then_inc(s_weights, 16)
            act.dma_start(ln_b_bc[:, :], ln_b.rearrange("(a n) -> a n", a=1).to_broadcast([P, D])).then_inc(s_weights, 16)
            act.wait_ge(s_const, 18)

            def seg_phase(phase):
                first_r = seg_index(phase) * ROUNDS

                def root(r):
                    act.wait_ge(e_var_ready.sem, e_var_ready.after(r))
                    nc.scalar.activation(e_sd[:, :], e_mv[:, :, 1], ACT.Sqrt, bias=eps_col[:, 0:1])\
                        .then_inc(e_sd_ready.sem, 1)

                def normalise(r, j):
                    b = r.mod(2)
                    if j == 0:
                        if phase == REL:
                            act.wait_ge(e_scale_ready.sem, e_scale_ready.after(r))
                        act.wait_ge(gathered[b].sem, gathered[b].after(r.div(2), parity_first(phase, b)))
                        act.wait_ge(turned.sem, turned.before(r, 2, first_r))
                    last = nc.scalar.activation(e_h[:, b, j, :], got[:, b, j, 0:D], ACT.Relu,
                                                bias=got[:, b, j, COL_C:COL_C + 1],
                                                scale=got[:, b, j, COL_A:COL_A + 1])
                    if j == TPR - 1:
                        last.then_inc(h_ready.sem, 1)

                def take_turned(r):
                    b = r.mod(2)
                    act.wait_ge(turned.sem, turned.after(r, first_r))
                    act.wait_ge(y_ready.sem, y_ready.before(r, 2, first_r))
                    nc.scalar.activation(e_ht[:, b, :], bank[0][:, :], ACT.Copy).then_inc(ht_ready.sem, 1)

                def take_messages(r):
                    b = r.mod(2)
                    act.wait_ge(y_ready.sem, y_ready.after(r, first_r))
                    act.wait_ge(seg_done.sem, seg_done.before(r, 2, first_r))
                    nc.scalar.activation(msg[:, b, :, 0:D], bank[1][:, :].rearrange("p (j d) -> p j d", j=TPR),
                                         ACT.Copy).then_inc(msg_ready.sem, 1)

                def take_sums(r, j):
                    b = r.mod(2)
                    if j == 0:
                        wait_landed(act, scattered[b], scattered[b].before(r.div(2), 1, parity_first(seg_index(phase), b)))
                    act.wait_ge(seg_done.sem, seg_done.after(r, first_r, j + 1))
                    nc.scalar.activation(psum_out[:, b, j, :], bank[4 + j % 2][:, 0:W], ACT.Copy)\
                        .then_inc(seg_out.sem, 1)

                x = extra(phase)
                stages = [(take_turned, 2)]
                for j in range(TPR):
                    stages += [(lambda r, j=j: take_sums(r, j), 3 + x), (lambda r, j=j: normalise(r, j), 1)]
                if phase == REL:
                    stages.append((root, 0))
                run_steps(act, stages + [(take_messages, 2 + x)], ROUNDS, 2, behind=2)

            def att_phase():
                def normalise(r, q):
                    b = r.mod(2)
                    if q == 0:
                        act.wait_ge(gathered[b].sem, gathered[b].after(r.div(2), parity_first(ATT, b)))
                        act.wait_ge(gathered_d[b].sem, gathered_d[b].after(r.div(2)))
                    act.wait_ge(a_turned.sem, a_turned.after(r, 0, q + 1 - 2))
                    for a in range(2):
                        for n, rows in enumerate((got, got_d)):
                            last = nc.scalar.activation(e_h[:, q, 2 * n + a, :], rows[:, b, 2 * q + a, 0:D], ACT.Relu,
                                                        bias=rows[:, b, 2 * q + a, COL_C:COL_C + 1],
                                                        scale=rows[:, b, 2 * q + a, COL_A:COL_A + 1])
                    last.then_inc(a_h.sem, 1)

                def take_turned(r, q):
                    act.wait_ge(a_turned.sem, a_turned.after(r, 0, q + 1))
                    act.wait_ge(a_qkv.sem, a_qkv.after(r, 0, q + 1 - 2))
                    nc.scalar.activation(e_ht[:, q, :], bank[0][:, :], ACT.Copy).then_inc(a_ht.sem, 1)

                def take_q(r, q):
                    act.wait_ge(a_qkv.sem, a_qkv.after(r, 0, q + 1))
                    act.wait_ge(a_logit.sem, a_logit.after(r, 0, q + 1 - 2))
                    nc.scalar.activation(q_sb[:, q, :, :], bank[1 + q][:, 0:2 * P], ACT.Copy)\
                        .then_inc(a_q.sem, 1)

                def exponentials(r, q):
                    act.wait_ge(a_logit.sem, a_logit.after(r, 0, q + 1))
                    b = r.mod(2)
                    act.wait_ge(a_sum.sem, a_sum.before(r, 2))
                    nc.scalar.activation(res[:, b, 2 * q:2 * q + 2, D:W],
                                         att_raw[:, q, :].rearrange("p (a h) -> p a h", a=2), ACT.Exp)\
                        .then_inc(a_exp.sem, 1)

                def take_sums(r, q):
                    b = r.mod(2)
                    wait_landed(act, a_acc, a_acc.before(r, 2))
                    for a in range(2):
                        j = 2 * q + a
                        act.wait_ge(a_sum.sem, a_sum.after(r, 0, j + 1))
                        nc.scalar.activation(psum_out[:, b, j, :], bank[4 + a][:, 0:W], ACT.Copy)\
                            .then_inc(a_out.sem, 1)

                def pairs(r):
                    normalise(r, 0)
                    take_turned(r, 0)
                    normalise(r, 1)
                    take_q(r, 0)
                    take_turned(r, 1)
                    exponentials(r, 0)
                    take_q(r, 1)
                    take_sums(r, 0)
                    exponentials(r, 1)

                run_steps(act, [(lambda r: take_sums(r, 1), 1), (pairs, 0)], ROUNDS, 2, behind=2)

            def node_phase(phase):
                def in_root(g):
                    act.wait_ge(in_var.sem, in_var.after(g))
                    nc.scalar.activation(in_sd[:, g.mod(2), :], in_mv[:, g.mod(DEEP), :, 1], ACT.Sqrt, bias=eps_col[:, 0:1])\
                        .then_inc(in_sd_ready.sem, 1)

                def normalise(g):
                    s, b = g.mod(SLOTS), g.mod(2)
                    mm = first(MATMUL, phase)
                    act.wait_ge(loaded[s].sem, loaded[s].after(g.div(SLOTS), stores_before(phase, s)))
                    if phase == REL:
                        act.wait_ge(in_scale.sem, in_scale.after(g))
                    act.wait_ge(n_turned.sem, n_turned.before(g, 2, mm))
                    for k in range(K):
                        last = nc.scalar.activation(n_h[:, b, k, :], xr[:, s, k, 0:D], ACT.Relu,
                                                    bias=xr[:, s, k, COL_C:COL_C + 1],
                                                    scale=xr[:, s, k, COL_A:COL_A + 1])
                    last.then_inc(n_h_ready.sem, 1)

                def take_turned(g):
                    b = g.mod(2)
                    mm = first(MATMUL, phase)
                    act.wait_ge(n_turned.sem, n_turned.after(g, mm))
                    act.wait_ge(n_y_ready.sem, n_y_ready.before(g, 2, mm))
                    nc.scalar.activation(n_ht[:, b, :], bank[b][:, :], ACT.Copy).then_inc(n_ht_ready.sem, 1)

                def take_sum(g):
                    act.wait_ge(n_y_ready.sem, n_y_ready.after(g, first(MATMUL, phase)))
                    act.wait_ge(x_added.sem, x_added.before(g, DEEP))
                    nc.scalar.activation(n_t[:, g.mod(DEEP), :, :],
                                         bank[2 + g.mod(2)][:, :].rearrange("p (k d) -> p k d", k=K), ACT.Relu)\
                        .then_inc(n_y_used.sem, 1)

                def mid_root(g):
                    act.wait_ge(mid_var.sem, mid_var.after(g, first(MID_NORM, phase)))
                    if phase == SAGE1:
                        nc.scalar.activation(root_deg[:, g.mod(2), :], sr[:, g.mod(SLOTS), :, COL_CNT], ACT.Sqrt,
                                             bias=ones_col[:, 0:1])
                    nc.scalar.activation(mid_sd[:, g.mod(2), :], mid_mv[:, g.mod(DEEP), :, 1], ACT.Sqrt, bias=eps_col[:, 0:1])\
                        .then_inc(mid_sd_ready.sem, 1)

                def mid_normalise(g):
                    b = g.mod(2)
                    act.wait_ge(mid_scale.sem, mid_scale.after(g, first(MID_NORM, phase)))
                    if phase == SAGE0:
                        act.wait_ge(row_ready.sem, row_ready.before(g, 2, phase * GROUPS))
                    else:
                        act.wait_ge(x_added.sem, x_added.before(g, 2, first(ROW_STATS, phase)))
                    for k in range(K):
                        last = nc.scalar.activation(n_u[:, b, k, :], n_t[:, g.mod(DEEP), k, :], ACT.Identity,
                                                    bias=mid_ac[:, b, 1, k:k + 1], scale=mid_ac[:, b, 0, k:k + 1])
                    last.then_inc(mid_ready.sem, 1)

                def out_root(g):
                    act.wait_ge(out_var.sem, out_var.after(g, first(ROW_STATS, phase)))
                    nc.scalar.activation(out_sd[:, g.mod(2), :], out_mv[:, g.mod(DEEP), :, 1], ACT.Sqrt, bias=eps_col[:, 0:1])\
                        .then_inc(out_sd_ready.sem, 1)

                stages = {
                    REL: [(in_root, 1), (out_root, 6), (take_sum, 4), (take_turned, 2), (normalise, 1)],
                    ATT: [(out_root, 3)],
                    SAGE0: [(mid_root, 5), (normalise, 0), (mid_normalise, 5)],
                    SAGE1: [(take_turned, 1), (mid_root, 5), (out_root, 9), (normalise, 0), (mid_normalise, 6)],
                    GCN: [(take_turned, 1), (normalise, 0)],
                }[phase]
                run_steps(act, stages, GROUPS, SLOTS)

            for phase in range(5):
                if phase == ATT:
                    att_phase()
                else:
                    seg_phase(phase)
                node_phase(phase)

        @block.tensor
        def _(pe):
            pe.wait_ge(s_const, 18)
            pe.wait_ge(s_keysf, 1)
            for n in range(4):
                for half in range(2):
                    at = (2 * n + half) * P
                    last = nc.tensor.transpose(bank[at // 512][:, at % 512:at % 512 + P],
                                               key_rows_f[:, n, half, :], ident[:, :])
            last.then_inc(s_keyst, 1)
            pe.wait_ge(s_weights, 16 * 15)
            for n in range(4):
                last = nc.tensor.transpose(bank[2][:, n * P:(n + 1) * P], w_in[:, n, :], ident[:, :])
            last.then_inc(s_wt, 1)
            pe.wait_ge(s_prep, 1)

            def spread(n, r, j, out_ps):
                for m in n:
                    last = nc.tensor.matmul(out_ps, lhsT=slot_keys[:, r.mod(2), m, j:j + 1].to_broadcast([P, P]),
                                            rhs=ident_bf[:, :], start=(m == n[0]), stop=(m == n[-1]))
                return last

            def seg_phase(phase):
                f = seg_index(phase) * ROUNDS

                def spread_keys(r):
                    pe.wait_ge(slots_ready.sem, slots_ready.after(r, phase * ROUNDS))
                    pe.wait_ge(eq_ready.sem, eq_ready.before(r, 1, f))
                    if phase == REL:
                        pe.wait_ge(htm_ready.sem, htm_ready.before(r, 2))
                    for j in range(TPR):
                        last = spread((0, 1), r, j, bank[2][:, j * P:(j + 1) * P])
                    if phase == REL:
                        for j in range(TPR):
                            last = spread((2,), r, j, type_bank[r.mod(2)][:, j * P:(j + 1) * P])
                    last.then_inc(keys_spread.sem, 1)

                def turn_rows(r):
                    pe.wait_ge(h_ready.sem, h_ready.after(r, f))
                    pe.wait_ge(ht_ready.sem, ht_ready.before(r, 1, f))
                    for j in range(TPR):
                        last = nc.tensor.transpose(bank[0][:, j * P:(j + 1) * P], e_h[:, r.mod(2), j, :], ident[:, :])
                    last.then_inc(turned.sem, 1)

                def products(r, j):
                    b = r.mod(2)
                    if j == 0:
                        pe.wait_ge(ht_ready.sem, ht_ready.after(r, f))
                        pe.wait_ge(msg_ready.sem, msg_ready.before(r, 1, f))
                    o = bank[1][:, j * P:(j + 1) * P]
                    if phase == REL:
                        h, at = j // 2, j % 2 * P
                        pe.wait_ge(htm_ready.sem, htm_ready.after(r, 0, h + 1))
                        for rel in range(NREL):
                            last = nc.tensor.matmul(o, lhsT=e_htm[:, h, rel, at:at + P], rhs=w_rel_sb[:, rel, :],
                                                    start=(rel == 0), stop=(rel == NREL - 1))
                    else:
                        last = nc.tensor.matmul(o, lhsT=e_ht[:, b, j * P:(j + 1) * P], rhs=edge_w[phase],
                                                start=True, stop=True)
                    last.then_inc(y_ready.sem, 1)

                def segment_sums(r, j):
                    b = r.mod(2)
                    if j == 0:
                        pe.wait_ge(eq_ready.sem, eq_ready.after(r, f))
                        pe.wait_ge(msg_ready.sem, msg_ready.after(r, f))
                    o = bank[4 + j % 2][:, 0:W]
                    pe.wait_ge(seg_out.sem, seg_out.after(r, f, j + 1 - 2))
                    nc.tensor.matmul(o, lhsT=eq[:, b, j, 0, :], rhs=msg[:, b, j, :], start=True, stop=False)
                    pe.wait_ge(seg_out.sem, seg_out.after(r, f, j))
                    carried = psum_out[:, b, j - 1, :] if j else psum_out[:, 1 - b, TPR - 1, :]
                    nc.tensor.matmul(o, lhsT=eq[:, b, j, 1, :], rhs=carried, start=False, stop=True)\
                        .then_inc(seg_done.sem, 1)

                x = extra(phase)
                parts = []
                for j in range(TPR):
                    parts += [(lambda r, j=j: segment_sums(r, j), 3 + x), (lambda r, j=j: products(r, j), 2 + x)]
                if phase == REL:
                    stages = [(turn_rows, 2)] + parts[:4] + [(spread_keys, 2)] + parts[4:]
                else:
                    stages = parts + [(turn_rows, 1), (spread_keys, 1)]
                run_steps(pe, stages, ROUNDS, 2)

            def att_phase():
                def pair_sums(r, q):
                    b = r.mod(2)
                    if q == 0:
                        pe.wait_ge(a_eq.sem, a_eq.after(r))
                    pe.wait_ge(a_res.sem, a_res.after(r, 0, q + 1))
                    for a in range(2):
                        pe.wait_ge(a_out.sem, a_out.after(r, 0, 2 * q + a + 1 - 2))
                        for a2 in range(2):
                            last = nc.tensor.matmul(bank[4 + a][:, 0:W], lhsT=eq[:, b, 2 * q + a2, a, :],
                                                    rhs=res[:, b, 2 * q + a2, :], start=(a2 == 0), stop=(a2 == 1))
                        last.then_inc(a_sum.sem, 1)

                def spread_keys(r):
                    pe.wait_ge(slots_ready.sem, slots_ready.after(r, ATT * ROUNDS))
                    pe.wait_ge(a_eq.sem, a_eq.before(r, 1))
                    for j in range(TPR):
                        last = spread((0, 1), r, j, bank[7][:, j * P:(j + 1) * P])
                    last.then_inc(a_spread.sem, 1)

                def pairs(r):
                    for q in range(2):
                        pe.wait_ge(a_h.sem, a_h.after(r, 0, q + 1))
                        pe.wait_ge(a_ht.sem, a_ht.after(r, 0, q))
                        for n in range(4):
                            last = nc.tensor.transpose(bank[0][:, n * P:(n + 1) * P], e_h[:, q, n, :], ident[:, :])
                        last.then_inc(a_turned.sem, 1)
                        pe.wait_ge(a_ht.sem, a_ht.after(r, 0, q + 1))
                        pe.wait_ge(a_q.sem, a_q.after(r, 0, q + 1 - 2))
                        pe.wait_ge(a_res.sem, a_res.after(r, 0, q + 1 - 2))
                        for a in range(2):
                            nc.tensor.matmul(bank[1 + q][:, a * P:(a + 1) * P],
                                             lhsT=e_ht[:, q, a * P:(a + 1) * P], rhs=w_q_sb[:, :],
                                             start=True, stop=True)
                            last = nc.tensor.matmul(kv_bank[q][:, 256 * a:256 * a + 256],
                                                    lhsT=e_ht[:, q, (2 + a) * P:(3 + a) * P],
                                                    rhs=w_kv_sb[:, :, :].rearrange("p n d -> p (n d)"),
                                                    start=True, stop=True)
                        last.then_inc(a_qkv.sem, 1)

                run_steps(pe, [(lambda r: pair_sums(r, 1), 1), (spread_keys, 0), (pairs, 0),
                               (lambda r: pair_sums(r, 0), 0)], ROUNDS, 2)

            def node_phase(phase):
                mm = first(MATMUL, phase)

                def turn_rows(g):
                    b = g.mod(2)
                    pe.wait_ge(n_h_ready.sem, n_h_ready.after(g, mm))
                    pe.wait_ge(n_ht_ready.sem, n_ht_ready.before(g, 2, mm))
                    for k in range(K):
                        last = nc.tensor.transpose(bank[b][:, k * P:(k + 1) * P], n_h[:, b, k, :], ident[:, :])
                    last.then_inc(n_turned.sem, 1)

                def products(g):
                    b = g.mod(2)
                    pe.wait_ge(n_ht_ready.sem, n_ht_ready.after(g, mm))
                    pe.wait_ge(n_y_used.sem, n_y_used.before(g, 2, mm))
                    bias = {REL: 0, SAGE0: 1, SAGE1: 2}.get(phase)
                    if bias is not None:
                        nc.tensor.matmul(bank[2 + b][:, :], lhsT=ones_bf[:, :],
                                         rhs=bias_bf[:, bias, :, :].rearrange("p k d -> p (k d)"),
                                         start=True, stop=False)
                    for k in range(K):
                        o = bank[2 + b][:, k * P:(k + 1) * P]
                        last = nc.tensor.matmul(o, lhsT=n_ht[:, b, k * P:(k + 1) * P], rhs=node_w[phase],
                                                start=(bias is None),
                                                stop=(bias is None or (phase != REL and k == K - 1)))
                    if phase == REL:
                        s = g.mod(SLOTS)
                        pe.wait_ge(loaded[s].sem, loaded[s].after(g.div(SLOTS), stores_before(phase, s)))
                        for k in range(K):
                            last = nc.tensor.matmul(bank[2 + b][:, k * P:(k + 1) * P], lhsT=ident[:, :],
                                                    rhs=sr[:, s, k, 0:D], start=False, stop=(k == K - 1))
                    last.then_inc(n_y_ready.sem, 1)

                first_lag = 1 if phase == REL else 0
                run_steps(pe, [(products, first_lag + 2), (turn_rows, first_lag)], GROUPS, SLOTS)

            for phase in range(5):
                if phase == ATT:
                    att_phase()
                else:
                    seg_phase(phase)
                    node_phase(phase)

        @block.vector
        def _(dve):
            nc.vector.memset(zeros[:, :], 0.0).then_inc(s_zeros, 1)
            own = Chain(dve, dve_setup)
            own.begin(Step(None, 1, 0))
            dve.wait_ge(s_const, 18)
            dve.wait_ge(s_keys, 16 * 12)
            nc.vector.tensor_copy(key_rows_f[:, :, :, :], key_rows[:, :, :, :]).then_inc(s_keysf, 1)
            dve.wait_ge(s_keyst, 1)
            for n, cols in enumerate((src_f, dst_f, next_f, type_f)):
                at = 2 * n * P
                last = nc.vector.tensor_copy(cols[:, :], bank[at // 512][:, at % 512:at % 512 + TILES])
            last.then_inc(s_keysc, 1)
            dve.wait_ge(s_keysc, 1)
            own.mark(nc.vector.tensor_copy(src_i[:, :], src_f[:, :]))
            own.mark(nc.vector.tensor_copy(dst_i[:, :], dst_f[:, :]))
            own.mark(nc.vector.tensor_copy(seg_keys[:, :, 0], dst_f[:, :]))
            own.mark(nc.vector.tensor_copy(ident_bf[:, :], ident[:, :]))
            own.mark(nc.vector.tensor_copy(dst_parts[:, 2, :], type_f[:, :]))
            own.wait()
            for n, keys_i in enumerate((src_i, dst_i)):
                own.mark(nc.vector.tensor_scalar(low_i[:, n, :], keys_i[:, :], 255, None, ALU.bitwise_and))
            own.wait()
            for n, (keys, parts) in enumerate(((src_f, src_parts), (dst_f, dst_parts))):
                own.mark(nc.vector.tensor_tensor(parts[:, 0, :], keys[:, :], low_i[:, n, :], ALU.subtract))
                own.mark(nc.vector.tensor_copy(parts[:, 1, :], low_i[:, n, :]))
            own.mark(nc.vector.tensor_tensor(next_f[:, :], dst_f[:, :], next_f[:, :], ALU.is_equal))
            own.wait()
            own.mark(nc.vector.scalar_tensor_tensor(out=last_i[:, :], in0=next_f[:, :], scalar=float(PAD),
                                                    in1=dst_f[:, :], op0=ALU.mult, op1=ALU.max))
            dve.wait_ge(s_wt, 1)
            own.mark(nc.vector.tensor_copy(w_t[:, :, :].rearrange("p n d -> p (n d)"), bank[2][:, :]))
            own.mark(nc.vector.tensor_copy(bias_part[:, 0, :, :], bias_f[:, :, :]))
            own.wait()
            own.mark(nc.vector.tensor_tensor(bias_left[:, 0, :, :], bias_f[:, :, :], bias_part[:, 0, :, :], ALU.subtract))
            own.wait()
            own.mark(nc.vector.tensor_copy(bias_part[:, 1, :, :], bias_left[:, 0, :, :]))
            own.wait()
            own.mark(nc.vector.tensor_tensor(bias_left[:, 1, :, :], bias_left[:, 0, :, :], bias_part[:, 1, :, :],
                                             ALU.subtract))
            own.wait()
            own.mark(nc.vector.tensor_copy(bias_part[:, 2, :, :], bias_left[:, 1, :, :]))
            own.wait()
            own.mark(nc.vector.tensor_scalar(bias_sum[:, :, :], bias_part[:, 0, :, :], part_mask[:, 0:1], None, ALU.mult))
            for n in range(1, BP):
                own.wait()
                own.mark(nc.vector.scalar_tensor_tensor(out=bias_sum[:, :, :], in0=bias_part[:, n, :, :],
                                                        scalar=part_mask[:, n:n + 1], in1=bias_sum[:, :, :],
                                                        op0=ALU.mult, op1=ALU.add))
            own.wait()
            for k in range(K):
                own.mark(nc.vector.tensor_copy(bias_bf[:, :, k, :], bias_sum[:, :, :]))
            own.wait()
            dve.wait_ge(s_setup, 1)
            dve.sem_inc(s_prep, 1)

            edge_chain = Chain(dve, dve_edge)
            scales_chain = Chain(dve, dve_scales)

            def first_indices(phase):
                for b in range(2):
                    fill_slots(phase, b, slice(b * TPR, (b + 1) * TPR))
                    if phase == ATT:
                        nc.vector.tensor_copy(didx[:, b, :], dst_i[:, b * TPR:(b + 1) * TPR])
                    nc.vector.tensor_copy(gidx[:, b, :], src_i[:, b * TPR:(b + 1) * TPR])\
                        .then_inc(gidx_ready.sem, 1)

            def fill_slots(phase, b, columns):
                n = {REL: 3}.get(phase, 2)
                nc.vector.tensor_copy(slot_keys[:, b, 0:n, :], (src_parts if phase == ATT else dst_parts)[:, 0:n, columns])\
                    .then_inc(slots_ready.sem, 1)

            def next_slots(phase, r):
                if r.i is None and r.offset + 2 >= ROUNDS:
                    return
                fill_slots(phase, r.mod(2), bass.ds(r.scaled(TPR, 2 * TPR), TPR))

            def next_indices(phase, r):
                b = r.mod(2)
                dve.wait_ge(gathered[b].sem, gathered[b].after(r.div(2), parity_first(phase, b)))
                if phase == ATT:
                    dve.wait_ge(gathered_d[b].sem, gathered_d[b].after(r.div(2)))
                if r.i is None and r.offset + 2 >= ROUNDS:
                    return
                at = r.scaled(TPR, 2 * TPR)
                if phase == ATT:
                    nc.vector.tensor_copy(didx[:, b, :], dst_i[:, bass.ds(at, TPR)])
                nc.vector.tensor_copy(gidx[:, b, :], src_i[:, bass.ds(at, TPR)]).then_inc(gidx_ready.sem, 1)

            def seg_phase(phase):
                f = seg_index(phase) * ROUNDS
                chain = [edge_chain, scales_chain]
                for own in chain:
                    own.open(1 if phase == REL else 0)

                def arrive(r):
                    next_indices(phase, r)
                    if phase != REL:
                        return
                    own = edge_chain
                    own.begin(r)
                    b = r.mod(2)
                    for j in range(TPR):
                        last = nc.vector.bn_stats(e_stats[:, j, :], got[:, b, j, 0:D])
                    own.mark(last)
                    own.wait()
                    gate(dve)
                    for j in range(TPR):
                        last = nc.vector.bn_aggr(e_mv[:, j, :], e_stats[:, j, :])
                    last.then_inc(e_var_ready.sem, 1)
                    own.end()

                def scales(r):
                    own = scales_chain
                    own.begin(r)
                    b = r.mod(2)
                    dve.wait_ge(e_sd_ready.sem, e_sd_ready.after(r))
                    own.mark(nc.vector.reciprocal(got[:, b, :, COL_A], e_sd[:, :]))
                    own.wait()
                    nc.vector.scalar_tensor_tensor(out=got[:, b, :, COL_C], in0=e_mv[:, :, 0], scalar=-1.0,
                                                   in1=got[:, b, :, COL_A], op0=ALU.mult, op1=ALU.mult)\
                        .then_inc(e_scale_ready.sem, 1)
                    own.end()

                def same_keys(r):
                    b = r.mod(2)
                    dve.wait_ge(keys_spread.sem, keys_spread.after(r, f))
                    dve.wait_ge(seg_done.sem, seg_done.before(r, 2, f))
                    nc.vector.tensor_tensor(
                        eq[:, b, :, :, :],
                        bank[2][:, :].rearrange("p (j e) -> p j e", j=TPR).unsqueeze(2).to_broadcast([P, TPR, 2, P]),
                        seg_keys[:, bass.ds(r.scaled(TPR), TPR), :].unsqueeze(3).to_broadcast([P, TPR, 2, P]),
                        ALU.is_equal).then_inc(eq_ready.sem, 1)
                    next_slots(phase, r)

                def scatter_indices(r):
                    b = r.mod(2)
                    wait_landed(dve, scattered[b], scattered[b].before(r.div(2), 1, parity_first(seg_index(phase), b)))
                    nc.vector.tensor_copy(sidx[:, b, :], last_i[:, bass.ds(r.scaled(TPR), TPR)])\
                        .then_inc(sidx_ready.sem, 1)

                def by_relation(r, h):
                    b = r.mod(2)
                    at = 2 * h * P
                    dve.wait_ge(ht_ready.sem, ht_ready.after(r, f))
                    dve.wait_ge(keys_spread.sem, keys_spread.after(r, f))
                    dve.wait_ge(y_ready.sem, y_ready.after(r, f, 2 * h + 2 - TPR))
                    for rel in range(NREL):
                        last = nc.vector.scalar_tensor_tensor(
                            out=e_htm[:, h, rel, :], in0=type_bank[b][:, at:at + 2 * P], scalar=float(rel),
                            in1=e_ht[:, b, at:at + 2 * P], op0=ALU.is_equal, op1=ALU.mult)
                    last.then_inc(htm_ready.sem, 1)

                first_indices(phase)
                if phase == REL:
                    stages = [(arrive, 1), (lambda r: by_relation(r, 0), 3), (scales, 1), (same_keys, 3),
                              (lambda r: by_relation(r, 1), 3), (scatter_indices, 4)]
                else:
                    stages = [(arrive, 1), (same_keys, 2), (scatter_indices, 3)]
                run_steps(dve, stages, ROUNDS, 2, ahead=2, behind=2)
                for own in chain:
                    own.close(ROUNDS)

            def att_phase():
                own = edge_chain
                own.open(7)

                def same_keys(r):
                    b = r.mod(2)
                    dve.wait_ge(a_spread.sem, a_spread.after(r))
                    dve.wait_ge(a_sum.sem, a_sum.before(r, 2))
                    for j in range(TPR):
                        q = j // 2
                        last = nc.vector.tensor_scalar(eq[:, b, j, :, :].rearrange("p a e -> p (a e)"),
                                                       bank[7][:, 256 * q:256 * q + 256],
                                                       src_f[:, bass.ds(r.scaled(TPR, j), 1)], None, ALU.is_equal)
                    last.then_inc(a_eq.sem, 1)

                def sum_rows(r):
                    b = r.mod(2)
                    dve.wait_ge(a_eq.sem, a_eq.after(r))
                    own.mark(nc.vector.tensor_tensor(sp_a[:, :], spare_f[:, :], src_f[:, bass.ds(r.scaled(TPR), TPR)],
                                                     ALU.subtract))
                    for j in range(TPR):
                        last = nc.vector.tensor_tensor_reduce(
                            out=dup_out[:, j, :], in0=eq[:, b, j, :, :].rearrange("p a e -> p (a e)"),
                            in1=earlier[:, j % 2, :], scale=1.0, scalar=0.0, op0=ALU.mult, op1=ALU.add,
                            accum_out=dup[:, j:j + 1])
                    own.mark(last)
                    own.wait()
                    own.mark(nc.vector.scalar_tensor_tensor(out=sp_b[:, :], in0=dup[:, :], scalar=0.5, in1=sp_a[:, :],
                                                            op0=ALU.is_gt, op1=ALU.mult))
                    own.wait()
                    wait_landed(dve, a_acc, a_acc.before(r, 2))
                    nc.vector.tensor_tensor(sidx[:, b, :], sp_b[:, :], src_f[:, bass.ds(r.scaled(TPR), TPR)], ALU.add)\
                        .then_inc(sidx_ready.sem, 1)

                def logits(r, q):
                    kv = kv_bank[q][:, :].rearrange("p (a n d) -> p a n d", a=2, n=2)
                    dve.wait_ge(a_q.sem, a_q.after(r, 0, q + 1))
                    own.mark(nc.vector.tensor_tensor(qk[:, :, :], q_sb[:, q, :, :], kv[:, :, 0, :], ALU.mult))
                    own.wait()
                    own.mark(nc.vector.tensor_reduce(att_sum[:, :], qk[:, :, :].rearrange("p a (h d) -> p (a h) d", d=DH),
                                                     AX.X, ALU.add))
                    own.wait()
                    dve.wait_ge(a_exp.sem, a_exp.after(r, 0, q + 1 - 2))
                    nc.vector.tensor_scalar(att_raw[:, q, :], att_sum[:, :], 10.0, -10.0, ALU.min, ALU.max)\
                        .then_inc(a_logit.sem, 1)

                def weighted(r, q):
                    b = r.mod(2)
                    kv = kv_bank[q][:, :].rearrange("p (a n d) -> p a n d", a=2, n=2)
                    dve.wait_ge(a_exp.sem, a_exp.after(r, 0, q + 1))
                    for a in range(2):
                        e = res[:, b, 2 * q + a, D:W].unsqueeze(2).to_broadcast([P, HEADS, DH])
                        last = nc.vector.tensor_tensor(
                            res[:, b, 2 * q + a, 0:D].rearrange("p (h d) -> p h d", d=DH),
                            kv[:, a, 1, :].rearrange("p (h d) -> p h d", d=DH), e, ALU.mult)
                    last.then_inc(a_res.sem, 1)

                def round_(r):
                    own.begin(r)
                    next_indices(ATT, r)
                    same_keys(r)
                    next_slots(ATT, r)
                    sum_rows(r)
                    logits(r, 0)
                    weighted(r, 0)
                    logits(r, 1)
                    weighted(r, 1)
                    own.end()

                first_indices(ATT)
                run_steps(dve, [(round_, 0)], ROUNDS, 2, ahead=2, behind=2)
                own.close(ROUNDS)

            def node_phase(phase):
                rows = x2r if phase in OUT_RING else xr

                def arrived(g):
                    s = g.mod(SLOTS)
                    dve.wait_ge(loaded[s].sem, loaded[s].after(g.div(SLOTS), stores_before(phase, s)))

                def product(g):
                    return bank[2 + g.mod(2)][:, :].rearrange("p (k d) -> p k d", k=K)

                class Moments:

                    def __init__(self, phases, source, ready, stats, mv, sd, columns, stats_done, var, sd_ready,
                                 rstd_done, scale):
                        self.f = first(phases, phase) if phase in phases else 0
                        self.source, self.ready, self.columns = source, ready, columns
                        self.stats_, self.mv, self.sd = stats, mv, sd
                        self.stats_done, self.var, self.sd_ready = stats_done, var, sd_ready
                        self.rstd_done, self.scale = rstd_done, scale

                    def stats(self, g):
                        self.ready(g)
                        for k in range(K):
                            last = nc.vector.bn_stats(self.stats_[:, g.mod(2), k, :], self.source(g, k))
                        last.then_inc(self.stats_done.sem, 1)

                    def moments(self, g):
                        dve.wait_ge(self.stats_done.sem, self.stats_done.after(g, self.f))
                        gate(dve)
                        for k in range(K):
                            last = nc.vector.bn_aggr(self.mv[:, g.mod(DEEP), k, :], self.stats_[:, g.mod(2), k, :])
                        last.then_inc(self.var.sem, 1)

                    def rstd(self, g):
                        dve.wait_ge(self.sd_ready.sem, self.sd_ready.after(g, self.f))
                        nc.vector.reciprocal(self.columns(g)[0], self.sd[:, g.mod(2), :]).then_inc(self.rstd_done.sem, 1)

                    def shifts(self, g):
                        a, c = self.columns(g)
                        dve.wait_ge(self.rstd_done.sem, self.rstd_done.after(g, self.f))
                        nc.vector.scalar_tensor_tensor(out=c, in0=self.mv[:, g.mod(DEEP), :, 0], scalar=-1.0, in1=a,
                                                       op0=ALU.mult, op1=ALU.mult).then_inc(self.scale.sem, 1)

                def row_columns(ring):
                    return lambda g: (ring[:, g.mod(SLOTS), :, COL_A], ring[:, g.mod(SLOTS), :, COL_C])

                def product_taken(g):
                    dve.wait_ge(n_y_used.sem, n_y_used.after(g, first(MATMUL, phase)))

                def row_added(g):
                    dve.wait_ge(x_added.sem, x_added.after(g, first(ROW_STATS, phase)))

                of_in = Moments([REL], lambda g, k: xr[:, g.mod(SLOTS), k, 0:D], arrived, in_stats, in_mv, in_sd,
                                row_columns(xr), in_stats_done, in_var, in_sd_ready, in_rstd_done, in_scale)
                of_mid = Moments(MID_NORM, lambda g, k: n_t[:, g.mod(DEEP), k, :], product_taken, mid_stats, mid_mv,
                                 mid_sd, lambda g: (mid_ac[:, g.mod(2), 0, :], mid_ac[:, g.mod(2), 1, :]),
                                 mid_stats_done, mid_var, mid_sd_ready, mid_rstd_done, mid_scale)
                of_out = Moments(ROW_STATS, lambda g, k: rows[:, g.mod(SLOTS), k, 0:D], row_added, out_stats, out_mv,
                                 out_sd, row_columns(rows), out_stats_done, out_var, out_sd_ready, out_rstd_done,
                                 row_ready)

                def last_rstd(g):
                    dve.wait_ge(out_sd_ready.sem, out_sd_ready.after(g, first(ROW_STATS, phase)))
                    nc.vector.reciprocal(rstd[:, g.mod(2), :], out_sd[:, g.mod(2), :]).then_inc(out_rstd_done.sem, 1)

                def last_a(g):
                    s = g.mod(SLOTS)
                    dve.wait_ge(out_rstd_done.sem, out_rstd_done.after(g, first(ROW_STATS, phase)))
                    nc.vector.tensor_tensor(rows[:, s, :, COL_A], rstd[:, g.mod(2), :], rows[:, s, :, COL_DIS], ALU.mult)\
                        .then_inc(out_a_done.sem, 1)

                def last_c(g):
                    s = g.mod(SLOTS)
                    dve.wait_ge(out_a_done.sem, out_a_done.after(g))
                    nc.vector.scalar_tensor_tensor(out=rows[:, s, :, COL_C], in0=out_mv[:, g.mod(DEEP), :, 0], scalar=-1.0,
                                                   in1=rows[:, s, :, COL_A], op0=ALU.mult, op1=ALU.mult)\
                        .then_inc(row_ready.sem, 1)

                def denominators(g):
                    s, b = g.mod(SLOTS), g.mod(2)
                    arrived(g)
                    if phase == ATT:
                        last = nc.vector.tensor_scalar(den[:, b, :, :], sr[:, s, :, D:W], 1e-8, None, ALU.add)
                    else:
                        last = nc.vector.tensor_scalar(den[:, b, :, 0], sr[:, s, :, COL_CNT], 1.0, None, ALU.max)
                    last.then_inc(den_done.sem, 1)

                def inverses(g):
                    d = den[:, g.mod(2), :, :] if phase == ATT else den[:, g.mod(2), :, 0]
                    dve.wait_ge(den_done.sem, den_done.after(g, first(DIVIDED, phase)))
                    nc.vector.reciprocal(d, d).then_inc(den_inverted.sem, 1)

                def weigh_heads(g):
                    s = g.mod(SLOTS)
                    dve.wait_ge(den_inverted.sem, den_inverted.after(g, first(DIVIDED, phase)))
                    dve.wait_ge(x_added.sem, x_added.before(g, DEEP, first(ROW_STATS, phase)))
                    for k in range(K):
                        last = nc.vector.tensor_tensor(
                            n_t[:, g.mod(DEEP), k, :].rearrange("p (h d) -> p h d", d=DH),
                            sr[:, s, k, 0:D].rearrange("p (h d) -> p h d", d=DH),
                            den[:, g.mod(2), k, :].unsqueeze(2).to_broadcast([P, HEADS, DH]), ALU.mult)
                    last.then_inc(weighted_ready.sem, 1)

                def take_turned(g):
                    b = g.mod(2)
                    mm = first(MATMUL, phase)
                    dve.wait_ge(n_turned.sem, n_turned.after(g, mm))
                    dve.wait_ge(n_y_ready.sem, n_y_ready.before(g, 2, mm))
                    nc.vector.tensor_copy(n_ht[:, b, :], bank[b][:, :]).then_inc(n_ht_ready.sem, 1)

                def add_mean(g):
                    s = g.mod(SLOTS)
                    dve.wait_ge(n_y_ready.sem, n_y_ready.after(g, first(MATMUL, phase)))
                    dve.wait_ge(den_inverted.sem, den_inverted.after(g, first(DIVIDED, phase)))
                    dve.wait_ge(mid_ready.sem, mid_ready.before(g, DEEP, first(MID_NORM, phase)))
                    for k in range(K):
                        last = nc.vector.scalar_tensor_tensor(out=n_t[:, g.mod(DEEP), k, :], in0=sr[:, s, k, 0:D],
                                                              scalar=den[:, g.mod(2), k, 0:1],
                                                              in1=product(g)[:, k, :], op0=ALU.mult, op1=ALU.add)
                    last.then_inc(n_y_used.sem, 1)

                def mid_rstd(g):
                    of_mid.rstd(g)
                    if phase == SAGE1:
                        s = g.mod(SLOTS)
                        dve.wait_ge(loaded2[s].sem, loaded2[s].after(g.div(SLOTS)))
                        nc.vector.reciprocal(rows[:, s, :, COL_DIS], root_deg[:, g.mod(2), :])

                def add_sums(g):
                    dve.wait_ge(n_y_ready.sem, n_y_ready.after(g, first(MATMUL, phase)))
                    nc.vector.tensor_tensor(n_t[:, g.mod(DEEP), :, :], product(g), sr[:, g.mod(SLOTS), :, 0:D],
                                            ALU.add).then_inc(n_y_used.sem, 1)

                def finish_gcn(g):
                    s = g.mod(SLOTS)
                    product_taken(g)
                    for k in range(K):
                        last = nc.vector.scalar_tensor_tensor(out=xr[:, s, k, 0:D], in0=n_t[:, g.mod(DEEP), k, :],
                                                              scalar=xr[:, s, k, COL_DIS:COL_DIS + 1],
                                                              in1=xr[:, s, k, 0:D], op0=ALU.mult, op1=ALU.add)
                    last.then_inc(row_ready.sem, 1)

                stages = {
                    REL: [(of_in.stats, 0), (of_in.rstd, 1), (of_out.rstd, 6), (of_in.shifts, 1), (of_out.shifts, 6),
                          (of_out.stats, 5), (of_in.moments, 0), (of_out.moments, 5)],
                    ATT: [(denominators, 0), (of_out.rstd, 3), (inverses, 0), (of_out.stats, 2), (of_out.shifts, 3),
                          (weigh_heads, 0), (of_out.moments, 2)],
                    SAGE0: [(denominators, 3), (take_turned, 1), (mid_rstd, 5), (inverses, 3), (of_mid.stats, 4),
                            (of_mid.shifts, 5), (add_mean, 3), (of_mid.moments, 4)],
                    SAGE1: [(denominators, 3), (mid_rstd, 6), (inverses, 3), (of_mid.shifts, 6), (add_mean, 3),
                            (last_rstd, 10), (of_out.stats, 8), (last_a, 10), (of_mid.stats, 4), (last_c, 10),
                            (of_out.moments, 8), (of_mid.moments, 4)],
                    GCN: [(add_sums, 2), (finish_gcn, 3)],
                }[phase]
                run_steps(dve, stages, GROUPS, SLOTS)

            for phase in range(5):
                if phase == ATT:
                    att_phase()
                else:
                    seg_phase(phase)
                node_phase(phase)


_INS = ['x', 'src', 'dst', 'edge_type_8', 'L0_gnn_weight', 'L0_gnn_self_loop_weight', 'L0_gnn_bias',
        'L1_gnn_qW', 'L1_gnn_kW', 'L1_gnn_vW', 'L2_gnn_W_self0', 'L2_gnn_W_neigh0', 'L2_gnn_b0',
        'L2_gnn_W_self1', 'L2_gnn_W_neigh1', 'L2_gnn_b1', 'L2_gnn_ln_g', 'L2_gnn_ln_b', 'L3_gnn_W']


def kernel(**inputs):
    import numpy as _np
    import concourse.bacc as _bacc
    from concourse import mybir as _mybir
    from concourse.bass_utils import run_bass_kernel_spmd as _run

    nc = _bacc.Bacc("TRN2", target_bir_lowering=False, num_devices=1)
    arrays, args = {}, []
    for name in _INS:
        a = _np.ascontiguousarray(inputs[name])
        arrays[f"in_{name}_dram"] = a
        args.append(nc.dram_tensor(f"in_{name}_dram", a.shape, _mybir.dt.from_np(a.dtype), kind="ExternalInput").ap())
    args.append(nc.dram_tensor("out_0_dram", inputs['x'].shape, _mybir.dt.float32, kind="ExternalOutput").ap())
    gnn_stack_kernel(nc, *args)
    r = _run(nc, [arrays], core_ids=[0])
    return r.results[0]["out_0_dram"]
```
